# Optimizing a Trainium2 kernel written in Bass

```python
import numpy as np
import jax
import jax.numpy as jnp

def _softmax(x, axis=-1):
    return jax.nn.softmax(x, axis=axis)

def _gelu(x):
    return jax.nn.gelu(x, approximate=True)

def _silu(x):
    return jax.nn.silu(x)

def _sigmoid(x):
    return jax.nn.sigmoid(x)

def _layernorm(x, axis=-1, eps=1e-05):
    m = jnp.mean(x, axis=axis, keepdims=True)
    v = jnp.var(x, axis=axis, keepdims=True)
    return (x - m) / jnp.sqrt(v + eps)

def _scatter_add(tgt, idx, src, axis=0):
    return tgt.at[idx].add(src)

def _segment_sum(src, seg, n):
    return jax.ops.segment_sum(src, seg, n)
kernel_name = 'mk_xattn_ffn_d2_seqx_r8_6004d9'

def setup_inputs(seed: int=0):
    np.random.seed(seed)
    _w = jnp.asarray

    def _rec_inputs():
        import jax
        import jax.numpy as jnp
        _rk = jax.random.key(seed)
        x = -0.0002928 + 1 * jax.random.normal(jax.random.fold_in(_rk, 1), (8, 256, 128), jnp.float32)
        _lenS = 256 - jax.random.randint(jax.random.fold_in(_rk, 7), (8,), 0, max(1, 256 // 4) + 1, jnp.int32)
        _lenS2 = 256 - jax.random.randint(jax.random.fold_in(_rk, 8), (8,), 0, max(1, 256 // 4) + 1, jnp.int32)
        _ctx_1024P = jax.random.normal(jax.random.fold_in(_rk, 11), (8, 16, 128), jnp.float32)
        _ctx_1024c = jax.random.dirichlet(jax.random.fold_in(_rk, 511), 0.3 * jnp.ones((16,), jnp.float32), (8, 256))
        _ctx_1024t = jnp.einsum('bsk,bkd->bsd', _ctx_1024c, _ctx_1024P)
        _ctx_1024t = _ctx_1024t * jax.lax.rsqrt(jnp.mean(jnp.square(_ctx_1024t)) + 1e-12) * 0.953939
        ctx_1024 = -1.39393e-06 + 0.999914 * (_ctx_1024t + 0.3 * jax.random.normal(jax.random.fold_in(_rk, 611), (8, 256, 128), jnp.float32))
        _validS = jnp.arange(256)[None, :] < _lenS[:, None]
        _validS2 = jnp.arange(256)[None, :] < _lenS2[:, None]
        _causal = jnp.tril(jnp.ones((256, 256), dtype=bool))
        mask_BxSxS2_ik1 = jnp.where(jnp.broadcast_to(_validS2[:, None, :], (8, 256, 256)), 1, 0).astype(jnp.int32)
        mask_BxS2_bf1 = jnp.ones((8, 256), dtype=bool)
        return (x, ctx_1024, mask_BxSxS2_ik1, mask_BxS2_bf1)
    x, ctx_1024, mask_BxSxS2_ik1, mask_BxS2_bf1 = _rec_inputs()

    def _L0_xattn_setup():
        import jax, jax.numpy as jnp
        import numpy as np
        B, S, D, H = (2, 256, 128, 16)
        DK = D // H
        key = jax.random.key(seed)
        ks = jax.random.split(key, 8)
        return {'query': jax.random.normal(ks[0], (B, S, D), dtype=jnp.float32), 'key': jax.random.normal(ks[1], (B, S, D), dtype=jnp.float32), 'value': jax.random.normal(ks[2], (B, S, D), dtype=jnp.float32), 'mask': jax.random.randint(ks[3], (B, S, S), 0, 2, dtype=jnp.int32), 'w_q': jax.random.normal(ks[4], (D, D), dtype=jnp.float32) * D ** (-0.5), 'w_k': jax.random.normal(ks[5], (D, D), dtype=jnp.float32) * D ** (-0.5), 'w_v': jax.random.normal(ks[6], (D, D), dtype=jnp.float32) * D ** (-0.5), 'w_o': jax.random.normal(ks[7], (D, D), dtype=jnp.float32) * D ** (-0.5)}
    _L0_xattn_all = _L0_xattn_setup()
    _L0_xattn_in = {k: v for k, v in _L0_xattn_all.items() if k in ('w_q', 'w_k', 'w_v', 'w_o')}
    del _L0_xattn_all

    def _L0_ffn_setup():
        import jax, jax.numpy as jnp
        import numpy as np
        H = 128
        I = 64
        E = 32
        TOP_K = 6
        N_GROUP = 8
        TOPK_GROUP = 4
        SCALE = 2.5
        N_SHARED = 2
        SI = I * N_SHARED
        B, S = (2, 128)
        key = jax.random.key(seed)
        ks = jax.random.split(key, 8)
        x = jax.random.normal(ks[0], (B, S, H), jnp.float32)
        gate_weight = jax.random.normal(ks[1], (E, H), jnp.float32) * 0.02
        e_score_correction_bias = jax.random.normal(ks[2], (E,), jnp.float32) * 0.01
        experts_gate_up = jax.random.normal(ks[3], (E, 2 * I, H), jnp.float32) * 0.02
        experts_down = jax.random.normal(ks[4], (E, H, I), jnp.float32) * 0.02
        shared_gate_w = jax.random.normal(ks[5], (SI, H), jnp.float32) * 0.02
        shared_up_w = jax.random.normal(ks[6], (SI, H), jnp.float32) * 0.02
        shared_down_w = jax.random.normal(ks[7], (H, SI), jnp.float32) * 0.02
        return {'x': x, 'gate_weight': gate_weight, 'e_score_correction_bias': e_score_correction_bias, 'experts_gate_up': experts_gate_up, 'experts_down': experts_down, 'shared_gate_w': shared_gate_w, 'shared_up_w': shared_up_w, 'shared_down_w': shared_down_w}
    _L0_ffn_all = _L0_ffn_setup()
    _L0_ffn_in = {k: v for k, v in _L0_ffn_all.items() if k in ('gate_weight', 'e_score_correction_bias', 'experts_gate_up', 'experts_down', 'shared_gate_w', 'shared_up_w', 'shared_down_w')}
    del _L0_ffn_all

    def _L1_xattn_setup():
        import jax, jax.numpy as jnp
        import numpy as np
        DIM = 128
        DIM_LATENT = 128
        DIM_HEAD = 64
        HEADS = 16
        INNER = HEADS * DIM_HEAD

        def layernorm(x, g, b, eps=1e-05):
            m = jnp.mean(x, axis=-1, keepdims=True)
            v = jnp.mean((x - m) ** 2, axis=-1, keepdims=True)
            return (x - m) / jnp.sqrt(v + eps) * g + b

        def rmsnorm(x, gamma, eps=1e-08):
            n = jnp.linalg.norm(x, axis=-1, keepdims=True) * x.shape[-1] ** (-0.5)
            return x / jnp.maximum(n, eps) * gamma
        key = jax.random.key(seed)
        ks = jax.random.split(key, 8)
        b, n, m = (4, 512, 64)
        x = jax.random.normal(ks[0], (b, n, DIM), dtype=jnp.float32)
        latents = jax.random.normal(ks[1], (b, m, DIM_LATENT), dtype=jnp.float32)
        mask = jnp.ones((b, n), dtype=bool)
        s = 0.02
        return {'x': x, 'latents': latents, 'mask': mask, 'ln_x_g': jnp.ones((DIM,), jnp.float32), 'ln_x_b': jnp.zeros((DIM,), jnp.float32), 'ln_l_g': jnp.ones((DIM_LATENT,), jnp.float32), 'ln_l_b': jnp.zeros((DIM_LATENT,), jnp.float32), 'qn_g': jnp.ones((DIM_HEAD,), jnp.float32), 'kn_g': jnp.ones((DIM_HEAD,), jnp.float32), 'Wq': jax.random.normal(ks[2], (DIM_LATENT, INNER), jnp.float32) * s, 'Wkv': jax.random.normal(ks[3], (DIM, 2 * INNER), jnp.float32) * s, 'Wout': jax.random.normal(ks[4], (INNER, DIM_LATENT), jnp.float32) * s, 'bout': jnp.zeros((DIM_LATENT,), jnp.float32)}
    _L1_xattn_all = _L1_xattn_setup()
    _L1_xattn_in = {k: v for k, v in _L1_xattn_all.items() if k in ('ln_x_g', 'ln_x_b', 'ln_l_g', 'ln_l_b', 'qn_g', 'kn_g', 'Wq', 'Wkv', 'Wout', 'bout')}
    del _L1_xattn_all

    def _L1_ffn_setup():
        import math
        import jax, jax.numpy as jnp
        import numpy as np
        D_MODEL = 128
        D_FF = 512
        N_EXPERTS = 8
        CAPACITY_FACTOR = 1.25
        L, B = (64, 8)

        def _route(tokens, router_w):
            T = tokens.shape[0]
            E = router_w.shape[0]
            capacity = int(math.ceil(T / E * CAPACITY_FACTOR))
            logits = tokens @ router_w.T
            probs = jax.nn.softmax(logits, axis=-1)
            top1_idx = jnp.argmax(probs, axis=-1)
            top1_prob = jnp.max(probs, axis=-1)
            order = jnp.lexsort((-top1_prob, top1_idx))
            sorted_e = top1_idx[order]
            counts = jnp.bincount(top1_idx, length=E)
            start = jnp.cumsum(counts) - counts
            pos_in_group = jnp.arange(T) - start[sorted_e]
            keep_sorted = pos_in_group < capacity
            keep = jnp.zeros((T,), bool).at[order].set(keep_sorted)
            return jnp.where(keep, top1_idx, 0).astype(jnp.int32)
        key = jax.random.key(seed)
        ks = jax.random.split(key, 6)
        s_in = 1.0 / math.sqrt(D_MODEL)
        s_ff = 1.0 / math.sqrt(D_FF)
        return {'x': jax.random.normal(ks[0], (L, B, D_MODEL), dtype=jnp.float32), 'router_w': jax.random.uniform(ks[1], (N_EXPERTS, D_MODEL), minval=-s_in, maxval=s_in), 'W1': jax.random.uniform(ks[2], (N_EXPERTS, D_MODEL, D_FF), minval=-s_in, maxval=s_in), 'b1': jax.random.uniform(ks[3], (N_EXPERTS, D_FF), minval=-s_in, maxval=s_in), 'W2': jax.random.uniform(ks[4], (N_EXPERTS, D_FF, D_MODEL), minval=-s_ff, maxval=s_ff), 'b2': jax.random.uniform(ks[5], (N_EXPERTS, D_MODEL), minval=-s_ff, maxval=s_ff)}
    _L1_ffn_all = _L1_ffn_setup()
    _L1_ffn_in = {k: v for k, v in _L1_ffn_all.items() if k in ('router_w', 'W1', 'b1', 'W2', 'b2')}
    del _L1_ffn_all
    return {'x': x, 'ctx_1024': ctx_1024, 'mask_BxSxS2_ik1': mask_BxSxS2_ik1, 'mask_BxS2_bf1': mask_BxS2_bf1, 'L0_xattn_w_q': _L0_xattn_in['w_q'], 'L0_xattn_w_k': _L0_xattn_in['w_k'], 'L0_xattn_w_v': _L0_xattn_in['w_v'], 'L0_xattn_w_o': _L0_xattn_in['w_o'], 'L0_ffn_gate_weight': _L0_ffn_in['gate_weight'], 'L0_ffn_e_score_correction_bias': _L0_ffn_in['e_score_correction_bias'], 'L0_ffn_experts_gate_up': _L0_ffn_in['experts_gate_up'], 'L0_ffn_experts_down': _L0_ffn_in['experts_down'], 'L0_ffn_shared_gate_w': _L0_ffn_in['shared_gate_w'], 'L0_ffn_shared_up_w': _L0_ffn_in['shared_up_w'], 'L0_ffn_shared_down_w': _L0_ffn_in['shared_down_w'], 'L1_xattn_ln_x_g': _L1_xattn_in['ln_x_g'], 'L1_xattn_ln_x_b': _L1_xattn_in['ln_x_b'], 'L1_xattn_ln_l_g': _L1_xattn_in['ln_l_g'], 'L1_xattn_ln_l_b': _L1_xattn_in['ln_l_b'], 'L1_xattn_qn_g': _L1_xattn_in['qn_g'], 'L1_xattn_kn_g': _L1_xattn_in['kn_g'], 'L1_xattn_Wq': _L1_xattn_in['Wq'], 'L1_xattn_Wkv': _L1_xattn_in['Wkv'], 'L1_xattn_Wout': _L1_xattn_in['Wout'], 'L1_xattn_bout': _L1_xattn_in['bout'], 'L1_ffn_router_w': _L1_ffn_in['router_w'], 'L1_ffn_W1': _L1_ffn_in['W1'], 'L1_ffn_b1': _L1_ffn_in['b1'], 'L1_ffn_W2': _L1_ffn_in['W2'], 'L1_ffn_b2': _L1_ffn_in['b2']}

def reference(x, ctx_1024, mask_BxSxS2_ik1, mask_BxS2_bf1, L0_xattn_w_q, L0_xattn_w_k, L0_xattn_w_v, L0_xattn_w_o, L0_ffn_gate_weight, L0_ffn_e_score_correction_bias, L0_ffn_experts_gate_up, L0_ffn_experts_down, L0_ffn_shared_gate_w, L0_ffn_shared_up_w, L0_ffn_shared_down_w, L1_xattn_ln_x_g, L1_xattn_ln_x_b, L1_xattn_ln_l_g, L1_xattn_ln_l_b, L1_xattn_qn_g, L1_xattn_kn_g, L1_xattn_Wq, L1_xattn_Wkv, L1_xattn_Wout, L1_xattn_bout, L1_ffn_router_w, L1_ffn_W1, L1_ffn_b1, L1_ffn_W2, L1_ffn_b2):
    import jax
    import jax.numpy as jnp

    def _L0_xattn_ref(query, key, value, mask, w_q, w_k, w_v, w_o):
        import jax, jax.numpy as jnp
        import numpy as np
        B, S, D, H = (2, 256, 128, 16)
        DK = D // H
        b, s, d = query.shape
        Q = jnp.einsum('bsd,ed->bse', query, w_q).reshape(b, s, H, DK).transpose(0, 2, 1, 3)
        K = jnp.einsum('bsd,ed->bse', key, w_k).reshape(b, s, H, DK).transpose(0, 2, 1, 3)
        V = jnp.einsum('bsd,ed->bse', value, w_v).reshape(b, s, H, DK).transpose(0, 2, 1, 3)
        scale = jnp.float32(DK ** 0.5)
        scores = jnp.einsum('bhqd,bhkd->bhqk', Q, K) / scale
        scores = jnp.where(mask[:, None, :, :] == 0, jnp.float32(-1000000000.0), scores)
        attn = jax.nn.softmax(scores, axis=-1)
        out = jnp.einsum('bhqk,bhkd->bhqd', attn, V)
        out = out.transpose(0, 2, 1, 3).reshape(b, s, d)
        return jnp.einsum('bsd,ed->bse', out, w_o)

    def _L0_ffn_ref(x, gate_weight, e_score_correction_bias, experts_gate_up, experts_down, shared_gate_w, shared_up_w, shared_down_w):
        import jax, jax.numpy as jnp
        import numpy as np
        H = 128
        I = 64
        E = 32
        TOP_K = 6
        N_GROUP = 8
        TOPK_GROUP = 4
        SCALE = 2.5
        N_SHARED = 2
        SI = I * N_SHARED
        B, S = (2, 128)
        b, s, h = x.shape
        xf = x.reshape(-1, h)
        T = xf.shape[0]
        logits = xf.astype(jnp.float32) @ gate_weight.astype(jnp.float32).T
        scores = jax.nn.sigmoid(logits)
        sfc = scores + e_score_correction_bias[None, :]
        gs = E // N_GROUP
        group_scores = sfc.reshape(T, N_GROUP, gs).max(axis=-1)
        _, gidx = jax.lax.top_k(group_scores, TOPK_GROUP)
        gmask = jnp.zeros((T, N_GROUP), bool).at[jnp.arange(T)[:, None], gidx].set(True)
        smask = jnp.repeat(gmask, gs, axis=1)
        masked = jnp.where(smask, sfc, 0.0)
        _, topk_idx = jax.lax.top_k(masked, TOP_K)
        tw = jnp.take_along_axis(scores, topk_idx, axis=1)
        tw = tw / (tw.sum(-1, keepdims=True) + 1e-20)
        tw = (tw * SCALE).astype(xf.dtype)
        combine = jnp.zeros((T, E), xf.dtype).at[jnp.arange(T)[:, None], topk_idx].add(tw)

        def expert_step(acc, inp):
            gu, dn, c = inp
            g = xf @ gu[:I].T
            u = xf @ gu[I:].T
            o = jax.nn.silu(g) * u @ dn.T
            return (acc + c[:, None] * o, None)
        routed, _ = jax.lax.scan(expert_step, jnp.zeros_like(xf), (experts_gate_up, experts_down, combine.T))
        sh = jax.nn.silu(xf @ shared_gate_w.T) * (xf @ shared_up_w.T)
        shared_out = sh @ shared_down_w.T
        return (routed + shared_out).reshape(b, s, h)

    def _L1_xattn_ref(x, latents, mask, ln_x_g, ln_x_b, ln_l_g, ln_l_b, qn_g, kn_g, Wq, Wkv, Wout, bout):
        import jax, jax.numpy as jnp
        import numpy as np
        DIM = 128
        DIM_LATENT = 128
        DIM_HEAD = 64
        HEADS = 16
        INNER = HEADS * DIM_HEAD

        def layernorm(x, g, b, eps=1e-05):
            m = jnp.mean(x, axis=-1, keepdims=True)
            v = jnp.mean((x - m) ** 2, axis=-1, keepdims=True)
            return (x - m) / jnp.sqrt(v + eps) * g + b

        def rmsnorm(x, gamma, eps=1e-08):
            n = jnp.linalg.norm(x, axis=-1, keepdims=True) * x.shape[-1] ** (-0.5)
            return x / jnp.maximum(n, eps) * gamma
        b, n, _ = x.shape
        m = latents.shape[1]
        h, d = (HEADS, DIM_HEAD)
        scale = d ** (-0.5)
        xn = layernorm(x, ln_x_g, ln_x_b)
        ln = layernorm(latents, ln_l_g, ln_l_b)
        q = (ln @ Wq).reshape(b, m, h, d).transpose(0, 2, 1, 3)
        kv = jnp.concatenate([xn @ Wkv, ln @ Wkv], axis=1)
        kv = kv.reshape(b, n + m, 2, h, d)
        k = kv[:, :, 0].transpose(0, 2, 1, 3)
        v = kv[:, :, 1].transpose(0, 2, 1, 3)
        qn = rmsnorm(q, qn_g) * scale
        kn = rmsnorm(k, kn_g)
        sim = jnp.einsum('bhid,bhjd->bhij', qn, kn)
        max_neg = -jnp.finfo(sim.dtype).max
        padded_mask = jnp.concatenate([mask, jnp.ones((b, m), bool)], axis=1)
        sim = jnp.where(padded_mask[:, None, None, :], sim, max_neg)
        attn = jax.nn.softmax(sim.astype(jnp.float32), axis=-1).astype(sim.dtype)
        out = jnp.einsum('bhij,bhjd->bhid', attn, v)
        out = out.transpose(0, 2, 1, 3).reshape(b, m, h * d)
        return out @ Wout + bout

    def _L1_ffn_ref(x, router_w, W1, b1, W2, b2):
        import math
        import jax, jax.numpy as jnp
        import numpy as np
        D_MODEL = 128
        D_FF = 512
        N_EXPERTS = 8
        CAPACITY_FACTOR = 1.25
        L, B = (64, 8)

        def _route(tokens, router_w):
            T = tokens.shape[0]
            E = router_w.shape[0]
            capacity = int(math.ceil(T / E * CAPACITY_FACTOR))
            logits = tokens @ router_w.T
            probs = jax.nn.softmax(logits, axis=-1)
            top1_idx = jnp.argmax(probs, axis=-1)
            top1_prob = jnp.max(probs, axis=-1)
            order = jnp.lexsort((-top1_prob, top1_idx))
            sorted_e = top1_idx[order]
            counts = jnp.bincount(top1_idx, length=E)
            start = jnp.cumsum(counts) - counts
            pos_in_group = jnp.arange(T) - start[sorted_e]
            keep_sorted = pos_in_group < capacity
            keep = jnp.zeros((T,), bool).at[order].set(keep_sorted)
            return jnp.where(keep, top1_idx, 0).astype(jnp.int32)
        Lx, Bx, D = x.shape
        T = Lx * Bx
        E = router_w.shape[0]
        tokens = x.reshape(T, D)
        final_e = _route(tokens, router_w)
        out = jnp.zeros_like(tokens)
        for e in range(E):
            h = jax.nn.relu(tokens @ W1[e] + b1[e])
            y = h @ W2[e] + b2[e]
            out = out + jnp.where((final_e == e)[:, None], y, 0.0)
        return out.reshape(Lx, Bx, D)
    x = x + _L0_xattn_ref(_layernorm(x, axis=-1), ctx_1024, ctx_1024, mask_BxSxS2_ik1, L0_xattn_w_q, L0_xattn_w_k, L0_xattn_w_v, L0_xattn_w_o)
    x = x + _L0_ffn_ref(_layernorm(x, axis=-1), L0_ffn_gate_weight, L0_ffn_e_score_correction_bias, L0_ffn_experts_gate_up, L0_ffn_experts_down, L0_ffn_shared_gate_w, L0_ffn_shared_up_w, L0_ffn_shared_down_w)
    x = x + _L1_xattn_ref(ctx_1024, _layernorm(x, axis=-1), mask_BxS2_bf1, L1_xattn_ln_x_g, L1_xattn_ln_x_b, L1_xattn_ln_l_g, L1_xattn_ln_l_b, L1_xattn_qn_g, L1_xattn_kn_g, L1_xattn_Wq, L1_xattn_Wkv, L1_xattn_Wout, L1_xattn_bout)
    x = x + _L1_ffn_ref(_layernorm(x, axis=-1), L1_ffn_router_w, L1_ffn_W1, L1_ffn_b1, L1_ffn_W2, L1_ffn_b2)
    return x

_drawn_inputs = setup_inputs


def setup_inputs(seed=0):
    import zlib

    import numpy as np

    out = dict(_drawn_inputs(seed))
    spreads = {'L1_xattn_ln_x_g': (1.0, 0.2),
     'L1_xattn_ln_x_b': (0.0, 0.1),
     'L1_xattn_ln_l_g': (1.0, 0.2),
     'L1_xattn_ln_l_b': (0.0, 0.308),
     'L1_xattn_qn_g': (1.0, 0.6),
     'L1_xattn_kn_g': (1.0, 0.6),
     'L1_xattn_bout': (0.0, 0.1)}
    factors = {'L0_ffn_gate_weight': 4.035,
     'L0_ffn_e_score_correction_bias': 8.0,
     'L0_ffn_experts_gate_up': 3.883,
     'L0_ffn_experts_down': 3.452,
     'L0_ffn_shared_gate_w': 3.71,
     'L0_ffn_shared_up_w': 3.241,
     'L0_ffn_shared_down_w': 3.149,
     'L1_ffn_b1': 3.145}
    for name, (base, spread) in spreads.items():
        noise = np.random.default_rng([zlib.crc32(name.encode()), seed]).standard_normal(out[name].shape)
        drawn = base * np.exp(spread * noise) if base else spread * noise
        out[name] = jnp.asarray(drawn.astype(out[name].dtype))
    for name, factor in factors.items():
        out[name] = (out[name] * factor).astype(out[name].dtype)
    return out
```

```python
from contextlib import ExitStack

import numpy as np

import concourse.bass as bass
from concourse import mybir

F32 = mybir.dt.float32
F16 = mybir.dt.float16
BF16 = mybir.dt.bfloat16
I32 = mybir.dt.int32
U32 = mybir.dt.uint32
U8 = mybir.dt.uint8
ALU = mybir.AluOpType
ACT = mybir.ActivationFunctionType
AX = mybir.AxisListType
ds = bass.ds

P = 128
D = 128
B = 8
S = 256
T = B * S
NT = T // P
QT = S // P
EPS = 1e-5

H0 = 16
K0 = D // H0
NP0 = H0 // 2
MROW = 32
MASKED = -32768.0


class Chain:

    def __init__(self, engine, sem):
        self.engine, self.sem, self.base, self.steps = engine, sem, 0, 0

    def start(self, base):
        self.base, self.steps = base, 0

    def then(self, instruction):
        instruction.then_inc(self.sem, 1)
        self.steps += 1
        self.engine.wait_ge(self.sem, self.base + self.steps)


def bc(ap, shape, axis):
    return ap.unsqueeze(axis).to_broadcast(shape)


def layer_norm_all(dve, chain, sem_centred, sem_squared, sem_var, sem_root, src, out, squares, small, count):
    total, shift, var, inv = (small[:, i * NT:(i + 1) * NT] for i in range(4))
    chain.then(dve.tensor_reduce(total, src[:], AX.X, ALU.add))
    chain.then(dve.tensor_scalar(shift, total, -1.0 / D, None, ALU.mult))
    dve.tensor_tensor(out[:], src[:], bc(shift, (P, NT, D), 2), ALU.add).then_inc(sem_centred, 1)
    dve.wait_ge(sem_squared, count)
    chain.then(dve.tensor_reduce(var, squares[:], AX.X, ALU.add))
    dve.tensor_scalar(var, var, 1.0 / D, EPS, ALU.mult, ALU.add).then_inc(sem_var, 1)
    dve.wait_ge(sem_root, count)
    chain.then(dve.reciprocal(inv, var))
    return inv


def layer_norm_all_act(act, sem_centred, sem_squared, sem_var, sem_root, out, squares, small, count):
    var = small[:, 2 * NT:3 * NT]
    act.wait_ge(sem_centred, count)
    act.activation(squares[:], out[:], ACT.Square).then_inc(sem_squared, 1)
    act.wait_ge(sem_var, count)
    act.activation(var, var, ACT.Sqrt).then_inc(sem_root, 1)


def identity(nc, pool, ident32, ident16, ident_b, sem, done):
    pool.memset(ident32[:], 0.0).then_inc(sem, 1)
    pool.wait_ge(sem, 1)
    pool.affine_select(out=ident32[:], in_=ident32[:], compare_op=ALU.not_equal, fill=1.0, base=0,
                       pattern=[[-1, P]], channel_multiplier=1).then_inc(sem, 1)
    pool.wait_ge(sem, 2)
    pool.tensor_copy(ident_b[:], ident32[:]).then_inc(done, 1)
    pool.tensor_copy(ident16[:], ident32[:]).then_inc(done, 1)


def project_layer0(nc, io, keep):
    with ExitStack() as ctx:
        def sb(name, shape, dt):
            return ctx.enter_context(nc.sbuf_tensor(name, shape, dt))

        def sem(name):
            return ctx.enter_context(nc.semaphore(name))

        xr, nrm, ident32, ident16 = keep["xr"], keep["nrm"], keep["ident32"], keep["ident16"]
        bias_q, bias_k, v_all = keep["bias_q"], keep["bias_k"], keep["v_all"]
        squares = sb("a_squares", [P, NT, D], F32)
        small = sb("a_small", [P, 6 * NT], F32)
        mask_q = sb("a_mask_q", [P, NT, S], I32)
        mask_k = sb("a_mask_k", [P, NT, S], I32)
        ctx_t = sb("a_ctx_t", [P, T], F32)
        w3 = sb("a_w3", [P, 3, D], F32)
        w3_hi = sb("a_w3_hi", [P, 3, D], F16)
        w3_lo = sb("a_w3_lo", [P, 3, D], F16)
        ctx_hi = sb("a_ctx_hi", [P, T], F16)
        ctx_lo = sb("a_ctx_lo", [P, T], F16)
        x_hi = sb("a_x_hi", [P, T], F16)
        x_lo = sb("a_x_lo", [P, T], F16)
        parts = sb("a_parts", [P, 4, T], F16)
        banks = [ctx.enter_context(nc.psum_tensor(f"a_bank{i}", [P, 512], F32)) for i in range(4)]

        x_in, ctx_in, w_in, mask_in, mask_k_in = (sem(f"a_{n}") for n in ("x_in", "ctx_in", "w_in", "mask_in", "mask_k_in"))
        made, ident_done = sem("a_made"), sem("a_ident_done")
        centred, squared, var_done, root_done = (sem(f"a_{n}") for n in ("centred", "squared", "var", "root"))
        steps, operands, norm_done = sem("a_steps"), sem("a_operands"), sem("a_norm_done")
        bank_ready, hi_done, lo_done, stored = (sem(f"a_{n}") for n in ("bank_ready", "hi_done", "lo_done", "stored"))
        masks_done = sem("a_masks_done")

        jobs = [("k", g) for g in range(4)] + [("v", g) for g in range(4)]
        jobs += [(kind, g) for g in range(4) for kind in ("t", "q")]
        order = {job: n for n, job in enumerate(jobs)}
        split = [n for n, job in enumerate(jobs) if job[0] != "v"]

        def lows(n):
            return sum(1 for m in split if m <= n)

        block = ctx.enter_context(nc.Block())

        @block.sync
        def _(sp):
            sp.dma_start(xr[:], io["x_rows"]).then_inc(x_in, 16)
            sp.dma_start(w3[:, 0, :], io["wq0"]).then_inc(w_in, 16)
            sp.dma_start(w3[:, 1, :], io["wk0"]).then_inc(w_in, 16)
            sp.dma_start(w3[:, 2, :], io["wv0"]).then_inc(w_in, 16)
            sp.dma_start(ctx_t[:], io["ctx_t"]).then_inc(ctx_in, 16)
            sp.dma_start(mask_q[:], io["mask_q"]).then_inc(mask_in, 16)
            sp.dma_start(mask_k[:], io["mask_k"]).then_inc(mask_k_in, 16)
            sp.dma_start(keep["wo0"][:], io["wo0"]).then_inc(keep["wo0_in"], 16)
            for i, name in enumerate(("k", "q")):
                sp.wait_ge(hi_done, order[(name, 3)] + 1)
                sp.wait_ge(lo_done, lows(order[(name, 3)]))
                at = 2 if name == "k" else 0
                sp.dma_start(io["parts"].rearrange("a p t -> p a t")[:, at:at + 2, :],
                             parts[:, at:at + 2, :]).then_inc(stored, 16)
            sp.wait_ge(stored, 32)

        @block.gpsimd
        def _(pool):
            nc.gpsimd.memset(keep["nothing"][:], 0.0)
            identity(nc, nc.gpsimd, ident32, ident16, keep["ident_b"], made, ident_done)
            pool.wait_ge(mask_in, 16)
            nc.gpsimd.tensor_scalar(bias_q[:], mask_q[:], 0.0, MASKED, ALU.is_equal, ALU.mult).then_inc(masks_done, 1)
            pool.wait_ge(mask_k_in, 16)
            nc.gpsimd.tensor_scalar(bias_k[:], mask_k[:], 0.0, MASKED, ALU.is_equal, ALU.mult).then_inc(masks_done, 1)
            pool.wait_ge(masks_done, 2)

        @block.scalar
        def _(act):
            layer_norm_all_act(act, centred, squared, var_done, root_done, nrm, squares, small, 1)
            for n, (kind, g) in enumerate(jobs):
                act.wait_ge(bank_ready, n + 1)
                if kind == "v":
                    act.copy(v_all[:, 4 * g:4 * g + 4, :], banks[n % 4][:].rearrange("p (t d) -> p t d", t=4)).then_inc(hi_done, 1)
                    continue
                out = x_hi if kind == "t" else parts[:, 0 if kind == "q" else 2, :]
                act.copy(out[:, 512 * g:512 * g + 512], banks[n % 4][:]).then_inc(hi_done, 1)

        @block.tensor
        def _(pe):
            def three(out, a_hi, a_lo, b_hi, b_lo):
                pe.matmul(out, a_hi, b_hi, start=True, stop=False)
                pe.matmul(out, a_lo, b_hi, start=False, stop=False)
                return pe.matmul(out, a_hi, b_lo, start=False, stop=True)

            for n, (kind, g) in enumerate(jobs):
                bank = banks[n % 4]
                if n >= 4:
                    pe.wait_ge(hi_done, n - 3)
                    pe.wait_ge(lo_done, lows(n - 4))
                cols = slice(512 * g, 512 * g + 512)
                if kind == "k":
                    pe.wait_ge(operands, 4)
                    mm = three(bank[:], w3_hi[:, 1, :], w3_lo[:, 1, :], ctx_hi[:, cols], ctx_lo[:, cols])
                elif kind == "q":
                    pe.wait_ge(hi_done, order[("t", g)] + 1)
                    pe.wait_ge(lo_done, lows(order[("t", g)]))
                    mm = three(bank[:], w3_hi[:, 0, :], w3_lo[:, 0, :], x_hi[:, cols], x_lo[:, cols])
                elif kind == "v":
                    for i in range(4):
                        t = slice(512 * g + P * i, 512 * g + P * i + P)
                        mm = three(bank[:, P * i:P * i + P], ctx_hi[:, t], ctx_lo[:, t], w3_hi[:, 2, :], w3_lo[:, 2, :])
                else:
                    pe.wait_ge(ident_done, 2)
                    pe.wait_ge(norm_done, 1)
                    for i in range(4):
                        mm = pe.transpose(bank[:, P * i:P * i + P], nrm[:, 4 * g + i, :], ident32[:])
                mm.then_inc(bank_ready, 1)

        @block.vector
        def _(dve):
            chain = Chain(dve, steps)
            dve.wait_ge(w_in, 48)
            dve.tensor_copy(w3_hi[:], w3[:]).then_inc(operands, 1)
            dve.wait_ge(ctx_in, 16)
            dve.tensor_copy(ctx_hi[:], ctx_t[:]).then_inc(operands, 1)
            dve.wait_ge(operands, 2)
            dve.tensor_tensor(w3_lo[:], w3[:], w3_hi[:], ALU.subtract).then_inc(operands, 1)
            dve.tensor_tensor(ctx_lo[:], ctx_t[:], ctx_hi[:], ALU.subtract).then_inc(operands, 1)
            dve.wait_ge(x_in, 16)
            inv = layer_norm_all(dve, chain, centred, squared, var_done, root_done, xr, nrm, squares, small, 1)
            any_key, seen = small[:, 4 * NT:5 * NT], small[:, 5 * NT:6 * NT]
            dve.wait_ge(mask_in, 16)
            chain.then(dve.tensor_reduce(any_key, mask_q[:], AX.X, ALU.max, apply_absolute_value=True))
            chain.then(dve.tensor_scalar(seen, any_key, 0.0, None, ALU.is_gt))
            chain.then(dve.tensor_tensor(inv, inv, seen, ALU.mult))
            dve.tensor_tensor(nrm[:], nrm[:], bc(inv, (P, NT, D), 2), ALU.mult).then_inc(norm_done, 1)
            for n, (kind, g) in enumerate(jobs):
                if kind == "v":
                    continue
                dve.wait_ge(hi_done, n + 1)
                hi, lo = (x_hi, x_lo) if kind == "t" else (parts[:, i + (0 if kind == "q" else 2), :] for i in range(2))
                cols = slice(512 * g, 512 * g + 512)
                dve.tensor_tensor(lo[:, cols], banks[n % 4][:], hi[:, cols], ALU.subtract).then_inc(lo_done, 1)


def attend_layer0(nc, io, keep):
    with ExitStack() as ctx:
        def sb(name, shape, dt):
            return ctx.enter_context(nc.sbuf_tensor(name, shape, dt))

        def psum(name, shape):
            return ctx.enter_context(nc.psum_tensor(name, shape, F32))

        def sem(name):
            return ctx.enter_context(nc.semaphore("b_" + name))

        xr, ident32, ident16 = keep["xr"], keep["ident32"], keep["ident16"]
        bias_q, bias_k, v_all, wo0 = keep["bias_q"], keep["bias_k"], keep["v_all"], keep["wo0"]
        nothing = keep["nothing"]
        q_stack = [sb(f"b_q_stack{i}", [P, H0, S], F16) for i in range(2)]
        k_stack = [sb(f"b_k_stack{i}", [P, H0, S], F16) for i in range(2)]
        VW = QT * H0 * P
        v_wide = [sb(f"b_v_wide{i}", [P, VW + P], F32) for i in range(2)]
        probs = [sb(f"b_probs{i}", [P, QT, 2, S], F32) for i in range(2)]
        row_max = sb("b_row_max", [P, QT, H0], F32)
        neg_max = sb("b_neg_max", [P, QT * H0], F32)
        neg_rows = sb("b_neg_rows", [QT * H0, P], F16)
        summed = sb("b_summed", [P, S], F32)
        inverse = sb("b_inverse", [P, S], F32)
        mixed = sb("b_mixed", [P, S], F32)
        attended = sb("b_attended", [P, S], F32)

        row_scores = [psum(f"b_row_scores{i}", [P, 2, S]) for i in range(QT)]
        scores = [psum(f"b_scores{i}", [P, QT, 2, S]) for i in range(2)]
        mix = psum("b_mix", [P, 512])
        misc = psum("b_misc", [P, 512])

        zeroed, ones_done, v_ready = sem("zeroed"), sem("ones_done"), sem("v_ready")
        loaded = [sem(f"loaded{i}") for i in range(2)]
        rows_ready, max_done, neg_done, turned, rows_done, max_in = (sem(n) for n in (
            "rows_ready", "max_done", "neg_done", "turned", "rows_done", "max_in"))
        scored, exp_done, weighed, mix_taken = (sem(n) for n in (
            "scored", "exp_done", "weighed", "mix_taken"))
        inverted, att_done, out_ready, added = sem("inverted"), sem("att_done"), sem("out_ready"), sem("added")

        block = ctx.enter_context(nc.Block())

        def wide(buf, kt, g):
            at = (kt * 2 + g) * 8 * P
            return v_wide[buf][:, at:at + 8 * (P + K0)].rearrange("p (h s) -> p h s", s=P + K0)[:, :, 0:K0]

        @block.sync
        def _(sp):
            def load(b, par):
                if not (isinstance(b, int) and b < 2):
                    sp.wait_ge(scored, (b - 1) * NP0)
                q_hi, q_lo, k_hi, k_lo = (io["parts"][i].rearrange("(h j) t -> j h t", j=K0)[:, :, ds(b * S, S)]
                                          for i in range(4))
                for stack, rows in ((q_stack[par], (q_hi, q_hi, q_lo)), (k_stack[par], (k_hi, k_lo, k_hi))):
                    for i, part in enumerate(rows):
                        sp.dma_start(stack[K0 * i:K0 * i + K0, :, :], part).then_inc(loaded[par], 16)
                sp.dma_start(q_stack[par][MROW:MROW + 1, :, :], io["zeros"]).then_inc(loaded[par], 16)

            def place_max(b, par):
                sp.wait_ge(rows_done, b + 1)
                for qt in range(QT):
                    sp.dma_start(q_stack[par][MROW:MROW + 1, :, P * qt:P * qt + P],
                                 neg_rows[H0 * qt:H0 * qt + H0, :]).then_inc(max_in, 16)

            sp.wait_ge(zeroed, 4)
            load(0, 0)
            load(1, 1)
            place_max(0, 0)
            with sp.Fori(0, (B - 2) // 2) as j:
                for par in range(2):
                    place_max(2 * j + par + 1, 1 - par)
                    load(2 * j + par + 2, par)
            place_max(B - 1, 1)

        @block.gpsimd
        def _(pool):
            for par in range(2):
                nc.gpsimd.memset(q_stack[par][:].bitcast(F32), 0.0).then_inc(zeroed, 1)
                nc.gpsimd.memset(k_stack[par][:].bitcast(F32), 0.0).then_inc(zeroed, 1)

            def place_values(b, par):
                for kt in range(QT):
                    for g in range(2):
                        values = v_all[:, ds(QT * b + kt, 1), 64 * g:64 * g + 64].rearrange("p t (h j) -> p (t h) j", j=K0)
                        ins = nc.gpsimd.tensor_tensor(wide(par, kt, g), values, bc(nothing[:], (P, 8, K0), 2), ALU.add)
                        ins.then_inc(v_ready, 1)

            pool.wait_ge(ones_done, 4)
            place_values(0, 0)
            place_values(1, 1)
            with pool.Fori(0, (B - 2) // 2) as j:
                for par in range(2):
                    pool.wait_ge(weighed, NP0 * (2 * j + par + 1))
                    place_values(2 * j + par + 2, par)

        @block.tensor
        def _(pe):
            def row_scores_of(b, par, p):
                for qt in range(QT):
                    first = isinstance(b, int) and b == 0 and p == 0
                    if not first:
                        pe.wait_ge(max_done, b * 2 * NP0 + 2 * p + qt - 1)
                    for i in range(2):
                        pe.matmul(row_scores[qt][:, i, :], q_stack[par][:, 2 * p + i, P * qt:P * qt + P],
                                  k_stack[par][:, 2 * p + i, :], start=(i == 0), stop=False, skip_group_check=True)
                    mm = pe.matmul(row_scores[qt][:], ident16[:], bias_q[:, ds(QT * b + qt, 1), :].to_broadcast((P, 2, S)),
                                   start=False, stop=True, skip_group_check=True)
                    mm.then_inc(rows_ready, 1)

            def turn_max(b):
                pe.wait_ge(neg_done, b + 1)
                if not (isinstance(b, int) and b < 2):
                    pe.wait_ge(added, b - 1)
                pe.transpose(misc[0:QT * H0, 0:P], neg_max[:], ident32[:]).then_inc(turned, 1)

            def scores_of(b, par, p):
                if not (isinstance(b, int) and b == 0 and p < 2):
                    pe.wait_ge(exp_done, b * NP0 + p - 1)
                for kt in range(QT):
                    for i in range(2):
                        pe.matmul(scores[p % 2][:, kt, i, :], k_stack[par][:, 2 * p + i, P * kt:P * kt + P],
                                  q_stack[par][:, 2 * p + i, :], start=(i == 0), stop=False, skip_group_check=True)
                    mm = pe.matmul(scores[p % 2][:, kt], ident16[:], bias_k[:, ds(QT * b + kt, 1), :].to_broadcast((P, 2, S)),
                                   start=False, stop=True, skip_group_check=True)
                mm.then_inc(scored, 1)

            def weigh(b, par, p):
                pe.wait_ge(exp_done, b * NP0 + p + 1)
                g = p // 4
                if p % 4 == 0 and not (isinstance(b, int) and b == 0 and g == 0):
                    pe.wait_ge(mix_taken, 2 * b + g)
                for i in range(2):
                    for kt in range(QT):
                        at = ((kt * 2 + g) * 8 + (2 * p + i) % 8) * P
                        mm = pe.matmul(mix[:, 0:S], v_wide[par][:, at:at + P], probs[p % 2][:, kt, i, :],
                                       start=(p % 4 == 0 and i == 0 and kt == 0), stop=(p % 4 == 3 and i == 1 and kt == 1))
                mm.then_inc(weighed, 1)

            def project(b):
                pe.wait_ge(att_done, b + 1)
                for qt in range(QT):
                    mm = pe.matmul(misc[:, P * qt:P * qt + P], attended[:, P * qt:P * qt + P], wo0[:], start=True, stop=True)
                mm.then_inc(out_ready, 1)

            def step(j, par, ahead=True, behind=True):
                b = 2 * j + par
                pe.wait_ge(max_in, 16 * QT * (b + 1))
                pe.wait_ge(v_ready, 4 * (b + 1))
                if ahead:
                    pe.wait_ge(loaded[1 - par], 16 * 7 * (j + par + 1))
                for p in range(NP0):
                    if ahead:
                        row_scores_of(b + 1, 1 - par, p)
                    scores_of(b, par, p)
                    if p:
                        weigh(b, par, p - 1)
                    if p == 2 and behind:
                        pe.wait_ge(rows_done, b + 1)
                        project(b - 1)
                weigh(b, par, NP0 - 1)
                if ahead:
                    turn_max(b + 1)

            pe.wait_ge(keep["wo0_in"], 16)
            pe.wait_ge(loaded[0], 16 * 7)
            pe.wait_ge(ones_done, 6)
            for p in range(NP0):
                row_scores_of(0, 0, p)
            turn_max(0)
            step(0, 0, behind=False)
            step(0, 1)
            with pe.Fori(1, B // 2 - 1) as j:
                step(j, 0)
                step(j, 1)
            step(B // 2 - 1, 0)
            step(B // 2 - 1, 1, ahead=False)
            project(B - 1)

        @block.scalar
        def _(act):
            def take_mix(b, g):
                act.wait_ge(weighed, NP0 * b + 4 * g + 4)
                if not (isinstance(b, int) and b == 0):
                    act.wait_ge(att_done, b)
                act.copy(summed[64 * g:64 * g + 64, :], mix[64:128, 0:S])
                act.copy(mixed[64 * g:64 * g + 64, :], mix[0:64, 0:S]).then_inc(mix_taken, 1)

            def take_rows(b):
                act.wait_ge(turned, b + 1)
                if not (isinstance(b, int) and b == 0):
                    act.wait_ge(max_in, 16 * QT * b)
                act.copy(neg_rows[:], misc[0:QT * H0, 0:P]).then_inc(rows_done, 1)

            def step(b, ahead=True):
                for p in range(NP0):
                    act.wait_ge(scored, b * NP0 + p + 1)
                    if not (isinstance(b, int) and b == 0 and p < 2):
                        act.wait_ge(weighed, b * NP0 + p - 1)
                    act.activation(probs[p % 2][:], scores[p % 2][:], ACT.Exp, scale=K0 ** -0.5).then_inc(exp_done, 1)
                    if p == 5:
                        take_mix(b, 0)
                take_mix(b, 1)
                if ahead:
                    take_rows(b + 1)

            take_rows(0)
            step(0)
            step(1)
            with act.Fori(1, B // 2 - 1) as j:
                step(2 * j)
                step(2 * j + 1)
            step(B - 2)
            step(B - 1, ahead=False)

        @block.vector
        def _(dve):
            for par in range(2):
                dve.memset(v_wide[par][:], 0.0).then_inc(ones_done, 1)
            dve.wait_ge(ones_done, 2)
            for par in range(2):
                for kt in range(QT):
                    for g in range(2):
                        at = (kt * 2 + g) * 8 * P + 64
                        ones = v_wide[par][:, at:at + 8 * (P + K0)].rearrange("p (h s) -> p h s", s=P + K0)
                        ins = dve.memset(ones[:, :, 0:K0], 1.0)
                ins.then_inc(ones_done, 1)
            dve.wait_ge(zeroed, 4)
            for par in range(2):
                dve.memset(k_stack[par][MROW:MROW + 1, :, :], 1.0).then_inc(ones_done, 1)

            def maxima(b, par, p):
                for qt in range(QT):
                    dve.wait_ge(rows_ready, b * 2 * NP0 + 2 * p + qt + 1)
                    if p == 0 and qt == 0 and not (isinstance(b, int) and b == 0):
                        dve.wait_ge(neg_done, b)
                    dve.tensor_reduce(row_max[:, qt, 2 * p:2 * p + 2], row_scores[qt][:], AX.X,
                                      ALU.max).then_inc(max_done, 1)

            def negate(b):
                dve.wait_ge(max_done, (b + 1) * 2 * NP0)
                if not (isinstance(b, int) and b == 0):
                    dve.wait_ge(turned, b)
                dve.tensor_scalar(neg_max[:], row_max[:].rearrange("p a h -> p (a h)"), -1.0, None,
                                  ALU.mult).then_inc(neg_done, 1)

            def normalise(b):
                dve.wait_ge(mix_taken, 2 * (b + 1))
                dve.reciprocal(inverse[:], summed[:]).then_inc(inverted, 1)
                dve.wait_ge(inverted, b + 1)
                if not (isinstance(b, int) and b == 0):
                    dve.wait_ge(out_ready, b)
                dve.tensor_tensor(attended[:], mixed[:], inverse[:], ALU.mult).then_inc(att_done, 1)

            def add(b):
                dve.wait_ge(out_ready, b + 1)
                rows = xr[:, ds(QT * b, QT), :]
                dve.tensor_tensor(rows, misc[:, 0:S].rearrange("p (t d) -> p t d", t=QT), rows,
                                  ALU.add).then_inc(added, 1)

            def step(b, par, ahead=True, behind=True):
                for p in range(NP0):
                    if ahead:
                        maxima(b + 1, 1 - par, p)
                    if p == 0 and behind:
                        normalise(b - 1)
                    if p == 3 and behind:
                        add(b - 1)
                if ahead:
                    negate(b + 1)

            for p in range(NP0):
                maxima(0, 0, p)
            negate(0)
            step(0, 0, behind=False)
            step(1, 1)
            with dve.Fori(1, B // 2 - 1) as j:
                step(2 * j, 0)
                step(2 * j + 1, 1)
            step(B - 2, 0)
            step(B - 1, 1, ahead=False)
            normalise(B - 1)
            add(B - 1)


E0 = 32
I0 = 64
G0 = 8
TOPG = 4
TOPK = 6
SCALE0 = 2.5
PAIRS = E0 // 2
CH = 512
NCH = T // CH


def experts_layer0(nc, io, keep):
    with ExitStack() as ctx:
        def sb(name, shape, dt):
            return ctx.enter_context(nc.sbuf_tensor("c_" + name, shape, dt))

        def psum(name, shape, dt=F32):
            return ctx.enter_context(nc.psum_tensor("c_" + name, shape, dt))

        def sem(name):
            return ctx.enter_context(nc.semaphore("c_" + name))

        xr, nrm, ident32, ident_b = keep["xr"], keep["nrm"], keep["ident32"], keep["ident_b"]
        nothing = keep["nothing"]
        squares = sb("squares", [P, NT, D], F32)
        small = sb("small", [P, 6 * NT], F32)
        x_hi, x_lo = sb("x_hi", [P, T], F16), sb("x_lo", [P, T], F16)
        gate = sb("gate", [P, E0], F32)
        gate_hi, gate_lo = sb("gate_hi", [P, E0], F16), sb("gate_lo", [P, E0], F16)
        bias = sb("bias", [P, E0], F32)
        counting = sb("counting", [P, E0], F32)
        score = sb("score", [P, NT, E0], F32)
        choice = sb("choice", [P, NT, E0], F32)
        group = sb("group", [P, NT, G0], F32)
        top = sb("top", [P, NT, 8], F32)
        top_at = sb("top_at", [P, NT, 8], U32)
        top_atf = sb("top_atf", [P, NT, 8], F32)
        hits = sb("hits", [P, NT * E0 * TOPK], F32)
        picked_g = sb("picked_g", [P, NT, G0], F32)
        picked = sb("picked", [P, NT, E0], F32)
        combine = sb("combine", [P, NT, E0], F32)
        rest = sb("rest", [P, NT, E0], F32)
        total, scale = sb("total", [P, NT], F32), sb("scale", [P, NT], F32)
        parts = sb("parts", [P, NT, 3 * E0], BF16)
        combine_t = sb("combine_t", [3 * E0, T], BF16)
        spread = sb("spread", [3 * E0, T], F16)
        w = [sb(f"w{i}", [P, 3, P], F32) for i in range(2)]
        w_hi = [sb(f"w_hi{i}", [P, 2, P], F16) for i in range(2)]
        w_lo = [sb(f"w_lo{i}", [P, 2, P], F16) for i in range(2)]
        gated = [sb(f"gated{i}", [P, CH], F32) for i in range(2)]
        upped = [sb(f"upped{i}", [P, CH], F32) for i in range(2)]
        hidden = [sb(f"hidden{i}", [P, CH], F32) for i in range(2)]
        y_t = sb("y_t", [P, T], F32)

        acc = psum("acc", [P, T])
        gate_ps, up_ps, weight_ps, misc = (psum(n, [P, CH]) for n in ("gate_ps", "up_ps", "weight_ps", "misc"))
        ring = [gate_ps, up_ps, weight_ps, misc]

        w_in = [sem(f"w_in{i}") for i in range(2)]
        gate_in, bias_in, spread_in = sem("gate_in"), sem("bias_in"), sem("spread_in")
        centred, squared, var_done, root_done = (sem(n) for n in ("centred", "squared", "var", "root"))
        steps, norm_done, turned, hi_done, lo_done = (sem(n) for n in ("steps", "norm_done", "turned", "hi_done", "lo_done"))
        gate_split, logits_done, scored, parts_done, parts_turned, parts_taken = (sem(n) for n in (
            "gate_split", "logits_done", "scored", "parts_done", "parts_turned", "parts_taken"))
        w_split, w_lo_done = sem("w_split"), sem("w_lo_done")
        gate_ready, up_ready, weight_ready, gate_taken, up_taken, hidden_done, down_done = (sem(n) for n in (
            "gate_ready", "up_ready", "weight_ready", "gate_taken", "up_taken", "hidden_done", "down_done"))
        y_taken, y_turned, y_added = sem("y_taken"), sem("y_turned"), sem("y_added")

        block = ctx.enter_context(nc.Block())

        @block.sync
        def _(sp):
            sp.dma_start(gate[:], io["gate0"]).then_inc(gate_in, 16)
            sp.dma_start(bias[:], io["bias0"].partition_broadcast(P)).then_inc(bias_in, 16)
            sp.dma_start(counting[:], io["counting"].partition_broadcast(P)).then_inc(bias_in, 16)
            sp.dma_start(spread[:], io["spread0"]).then_inc(spread_in, 16)

            def load(k, par):
                sp.dma_start(w[par][:], io["w0"].rearrange("k p a d -> k p (a d)")[ds(k, 1)].rearrange("k p c -> p (k c)")
                             ).then_inc(w_in[par], 16)

            load(0, 0)
            load(1, 1)
            with sp.Fori(0, PAIRS // 2 - 1) as j:
                sp.wait_ge(down_done, NCH * (2 * j + 1))
                load(2 * j + 2, 0)
                sp.wait_ge(down_done, NCH * (2 * j + 2))
                load(2 * j + 3, 1)
            sp.wait_ge(down_done, NCH * (PAIRS - 1))
            load(PAIRS, 0)

        @block.gpsimd
        def _(pool):
            def split(j, k, par):
                pool.wait_ge(w_in[par], 16 * (j + 1))
                if not (isinstance(k, int) and k < 2):
                    pool.wait_ge(down_done, NCH * (k - 1))
                nc.gpsimd.tensor_tensor(w_hi[par][:], w[par][:, 0:2, :], bc(nothing[:, 0:2], (P, 2, P), 2), ALU.add).then_inc(w_split, 1)
                pool.wait_ge(w_split, k + 1)
                nc.gpsimd.tensor_tensor(w_lo[par][:], w[par][:, 0:2, :], w_hi[par][:], ALU.subtract).then_inc(w_lo_done, 1)

            split(0, 0, 0)
            split(0, 1, 1)
            with pool.Fori(1, PAIRS // 2) as j:
                split(j, 2 * j, 0)
                split(j, 2 * j + 1, 1)
            split(PAIRS // 2, PAIRS, 0)

        @block.tensor
        def _(pe):
            def three(out, a_hi, a_lo, b_hi, b_lo):
                pe.matmul(out, a_hi, b_hi, start=True, stop=False)
                pe.matmul(out, a_lo, b_hi, start=False, stop=False)
                return pe.matmul(out, a_hi, b_lo, start=False, stop=True)

            pe.wait_ge(norm_done, 1)
            for g in range(4):
                for i in range(4):
                    mm = pe.transpose(ring[g][:, P * i:P * i + P], nrm[:, 4 * g + i, :], ident32[:])
                mm.then_inc(turned, 1)
            pe.wait_ge(gate_split, 2)
            pe.wait_ge(lo_done, 4)
            for t in range(NT):
                cols = slice(P * t, P * t + P)
                mm = three(misc[:, E0 * t:E0 * t + E0], x_hi[:, cols], x_lo[:, cols], gate_hi[:], gate_lo[:])
            mm.then_inc(logits_done, 1)

            def down(k, par, c):
                n = NCH * k + c
                pe.wait_ge(hidden_done, n + 1)
                first = isinstance(k, int) and k == 0
                last = isinstance(k, int) and k == PAIRS
                pe.matmul(acc[:, CH * c:CH * c + CH], w[par][:, 2, :], hidden[c % 2][:], start=first, stop=last).then_inc(down_done, 1)

            def chunk(k, par, c, routed=True):
                n = NCH * k + c
                cols = slice(CH * c, CH * c + CH)
                first = isinstance(k, int) and k == 0 and c == 0
                if not first:
                    pe.wait_ge(gate_taken, n)
                three(gate_ps[:], w_hi[par][:, 0, :], w_lo[par][:, 0, :], x_hi[:, cols], x_lo[:, cols]).then_inc(gate_ready, 1)
                if routed:
                    pe.wait_ge(hidden_done, n)
                    pe.matmul(weight_ps[:], spread[:, ds(P * (k - 1), P)], combine_t[:, cols], start=True, stop=True).then_inc(weight_ready, 1)
                if not first:
                    pe.wait_ge(up_taken, n)
                three(up_ps[:], w_hi[par][:, 1, :], w_lo[par][:, 1, :], x_hi[:, cols], x_lo[:, cols]).then_inc(up_ready, 1)

            def pair(j, k, par, routed=True):
                pe.wait_ge(w_lo_done, k + 1)
                for c in range(NCH):
                    chunk(k, par, c, routed)
                    if c:
                        down(k, par, c - 1)
                    elif not (isinstance(k, int) and k == 0):
                        down(k - 1, 1 - par, NCH - 1)

            pair(0, 0, 0, routed=False)
            pe.wait_ge(parts_done, 1)
            pe.wait_ge(scored, 1)
            for g in range(2):
                for i in range(8):
                    mm = pe.transpose(misc[:].bitcast(BF16)[0:3 * E0, P * i:P * i + P], parts[:, 8 * g + i, :], ident_b[:])
                mm.then_inc(parts_turned, 1)
                pe.wait_ge(parts_taken, g + 1)
            pe.wait_ge(spread_in, 16)
            pair(0, 1, 1)
            with pe.Fori(1, PAIRS // 2) as j:
                pair(j, 2 * j, 0)
                pair(j, 2 * j + 1, 1)
            pair(PAIRS // 2, PAIRS, 0)
            down(PAIRS, 0, NCH - 1)
            for g in range(4):
                pe.wait_ge(y_taken, g + 1)
                for i in range(4):
                    t = 4 * g + i
                    mm = pe.transpose(ring[g][:, P * i:P * i + P], y_t[:, P * t:P * t + P], ident32[:])
                mm.then_inc(y_turned, 1)

        @block.scalar
        def _(act):
            layer_norm_all_act(act, centred, squared, var_done, root_done, nrm, squares, small, 1)
            for g in range(4):
                act.wait_ge(turned, g + 1)
                act.copy(x_hi[:, CH * g:CH * g + CH], ring[g][:]).then_inc(hi_done, 1)
            act.wait_ge(logits_done, 1)
            act.activation(score[:].rearrange("p t e -> p (t e)"), misc[:], ACT.Sigmoid).then_inc(scored, 1)

            def silus(k):
                for c in range(NCH):
                    n = NCH * k + c
                    act.wait_ge(gate_ready, n + 1)
                    if not (isinstance(k, int) and k == 0 and c < 2):
                        act.wait_ge(up_taken, n - 1)
                    act.activation(gated[c % 2][:], gate_ps[:], ACT.Silu).then_inc(gate_taken, 1)

            silus(0)
            with act.Fori(1, PAIRS + 1) as k:
                silus(k)
            act.wait_ge(down_done, NCH * (PAIRS + 1))
            for g in range(4):
                act.copy(y_t[:, CH * g:CH * g + CH], acc[:, CH * g:CH * g + CH]).then_inc(y_taken, 1)

        @block.vector
        def _(dve):
            chain = Chain(dve, steps)
            inv = layer_norm_all(dve, chain, centred, squared, var_done, root_done, xr, nrm, squares, small, 1)
            dve.tensor_tensor(nrm[:], nrm[:], bc(inv, (P, NT, D), 2), ALU.mult).then_inc(norm_done, 1)
            dve.wait_ge(gate_in, 16)
            dve.tensor_copy(gate_hi[:], gate[:]).then_inc(gate_split, 1)
            dve.wait_ge(gate_split, 1)
            dve.tensor_tensor(gate_lo[:], gate[:], gate_hi[:], ALU.subtract).then_inc(gate_split, 1)
            for g in range(4):
                cols = slice(CH * g, CH * g + CH)
                dve.wait_ge(hi_done, g + 1)
                dve.tensor_tensor(x_lo[:, cols], ring[g][:], x_hi[:, cols], ALU.subtract).then_inc(lo_done, 1)

            def hiddens(k, routed=True):
                for c in range(NCH):
                    n = NCH * k + c
                    dve.wait_ge(gate_taken, n + 1)
                    dve.wait_ge(up_ready, n + 1)
                    dve.tensor_tensor(upped[c % 2][:], up_ps[:], gated[c % 2][:], ALU.mult).then_inc(up_taken, 1)
                    dve.wait_ge(up_taken, n + 1)
                    if not (isinstance(k, int) and k == 0 and c < 2):
                        dve.wait_ge(down_done, n - 1)
                    if routed:
                        dve.wait_ge(weight_ready, n - NCH + 1)
                        dve.tensor_tensor(hidden[c % 2][:], weight_ps[:], upped[c % 2][:], ALU.mult).then_inc(hidden_done, 1)
                    else:
                        dve.tensor_copy(hidden[c % 2][:], upped[c % 2][:]).then_inc(hidden_done, 1)

            dve.wait_ge(bias_in, 32)
            dve.wait_ge(scored, 1)
            chain.then(dve.tensor_tensor(choice[:], score[:], bc(bias[:], (P, NT, E0), 1), ALU.add))
            hiddens(0, routed=False)
            chain.then(dve.tensor_reduce(group[:].rearrange("p t g -> p (t g)"),
                                         choice[:].rearrange("p t (g e) -> p (t g) e", g=G0), AX.X, ALU.max))

            def pick(values, n, count, out):
                for t in range(NT):
                    ins = dve.max(top[:, t, :], values[:, t, :])
                chain.then(ins)
                for t in range(NT):
                    ins = dve.max_index(top_at[:, t, :], top[:, t, :], values[:, t, :])
                chain.then(ins)
                chain.then(dve.tensor_copy(top_atf[:], top_at[:]))
                hit = hits[:, 0:NT * n * count].rearrange("p (t e k) -> p t e k", t=NT, e=n)
                places = top_atf[:, :, 0:count].unsqueeze(2).to_broadcast((P, NT, n, count))
                numbers = counting[:, 0:n].unsqueeze(1).unsqueeze(3).to_broadcast((P, NT, n, count))
                chain.then(dve.tensor_tensor(hit, numbers, places, ALU.is_equal))
                chain.then(dve.tensor_reduce(out[:].rearrange("p t e -> p (t e)"),
                                             hits[:, 0:NT * n * count].rearrange("p (m k) -> p m k", k=count), AX.X, ALU.add))

            pick(group, G0, TOPG, picked_g)
            per = E0 // G0
            chain.then(dve.tensor_tensor(choice[:].rearrange("p t (g e) -> p t g e", g=G0),
                                         choice[:].rearrange("p t (g e) -> p t g e", g=G0),
                                         picked_g[:].unsqueeze(3).to_broadcast((P, NT, G0, per)), ALU.mult))
            pick(choice, E0, TOPK, picked)
            chain.then(dve.tensor_tensor(combine[:], score[:], picked[:], ALU.mult))
            chain.then(dve.tensor_reduce(total[:], combine[:], AX.X, ALU.add))
            chain.then(dve.tensor_scalar(total[:], total[:], 1e-20, None, ALU.add))
            chain.then(dve.reciprocal(scale[:], total[:]))
            chain.then(dve.tensor_scalar(scale[:], scale[:], SCALE0, None, ALU.mult))
            chain.then(dve.tensor_tensor(combine[:], combine[:], bc(scale[:], (P, NT, E0), 2), ALU.mult))
            chain.then(dve.tensor_copy(parts[:, :, 0:E0], combine[:]))
            chain.then(dve.tensor_tensor(rest[:], combine[:], parts[:, :, 0:E0], ALU.subtract))
            chain.then(dve.tensor_copy(parts[:, :, E0:2 * E0], rest[:]))
            dve.tensor_tensor(parts[:, :, 2 * E0:3 * E0], rest[:], parts[:, :, E0:2 * E0], ALU.subtract).then_inc(parts_done, 1)
            for g in range(2):
                dve.wait_ge(parts_turned, g + 1)
                dve.tensor_copy(combine_t[:, 8 * P * g:8 * P * g + 8 * P], misc[:].bitcast(BF16)[0:3 * E0, :]).then_inc(parts_taken, 1)
            with dve.Fori(1, PAIRS + 1) as k:
                hiddens(k)
            for g in range(4):
                dve.wait_ge(y_turned, g + 1)
                rows = xr[:, 4 * g:4 * g + 4, :]
                dve.tensor_tensor(rows, ring[g][:].rearrange("p (t d) -> p t d", t=4), rows, ALU.add).then_inc(y_added, 1)


H1 = 16
D1 = 64
HU = H1 // 2
PU = HU // 2
NK1 = 2 * S
KT = NK1 // P
MROW1 = D1


def prepare_layer1(nc, io, keep):
    with ExitStack() as ctx:
        def sb(name, shape, dt):
            return ctx.enter_context(nc.sbuf_tensor("d_" + name, shape, dt))

        def sem(name):
            return ctx.enter_context(nc.semaphore("d_" + name))

        xr, nrm, ident32 = keep["xr"], keep["nrm"], keep["ident32"]
        wq_hi, wq_lo, wkv_hi, wkv_lo = (keep[n] for n in ("wq_hi", "wq_lo", "wkv_hi", "wkv_lo"))
        squares = sb("squares", [P, NT, D], F32)
        small = sb("small", [P, 4 * NT], F32)
        ctx_rows = sb("ctx_rows", [P, NT, D], F32)
        ctx_nrm = sb("ctx_nrm", [P, NT, D], F32)
        lat_nrm = sb("lat_nrm", [P, NT, D], F32)
        wq, wkv = sb("wq", [P, H1 * D1], F32), sb("wkv", [P, 2 * H1 * D1], F32)
        norm_w = sb("norm_w", [P, 4], F32)
        q_gain, k_gain = sb("q_gain", [P, D1], F32), sb("k_gain", [P, D1], F32)
        bout = sb("bout", [P, D], F32)
        mask8 = sb("mask8", [B, S], U8)
        mask_bias = sb("mask_bias", [B, S], F16)
        turned = [sb(f"turned{i}", [P, 512], F32) for i in range(2)]
        banks = [ctx.enter_context(nc.psum_tensor(f"d_bank{i}", [P, 512], F32)) for i in range(4)]

        ctx_in, small_in, wq_in, wkv_in, mask_in, mask_out = (sem(n) for n in ("ctx_in", "small_in", "wq_in", "wkv_in", "mask_in", "mask_out"))
        centred, squared, var_done, root_done = (sem(n) for n in ("centred", "squared", "var", "root"))
        steps, ctx_done, lat_done, w_hi_done, mask_done = (sem(n) for n in ("steps", "ctx_done", "lat_done", "w_hi_done", "mask_done"))
        bank_ready, bank_taken, hi_done, lo_done = (sem(n) for n in ("bank_ready", "bank_taken", "hi_done", "lo_done"))

        block = ctx.enter_context(nc.Block())

        @block.sync
        def _(sp):
            sp.dma_start(ctx_rows[:], io["ctx_rows"]).then_inc(ctx_in, 16)
            sp.dma_start(norm_w[:], io["norm_w"]).then_inc(small_in, 16)
            sp.dma_start(q_gain[:], io["q_gain"].partition_broadcast(P)).then_inc(small_in, 16)
            sp.dma_start(k_gain[:], io["k_gain"].partition_broadcast(P)).then_inc(small_in, 16)
            sp.dma_start(bout[:], io["bout"].partition_broadcast(P)).then_inc(small_in, 16)
            sp.dma_start(mask8[:], io["mask8"]).then_inc(mask_in, 16)
            sp.dma_start(wq[:], io["wq1"]).then_inc(wq_in, 16)
            sp.dma_start(wkv[:], io["wkv1"]).then_inc(wkv_in, 16)
            sp.dma_start(keep["wout"][:], io["wout"]).then_inc(keep["wout_in"], 16)
            sp.wait_ge(mask_done, 1)
            sp.dma_start(io["mask_bias"], mask_bias[:]).then_inc(mask_out, 16)
            sp.wait_ge(mask_out, 16)

        @block.gpsimd
        def _(pool):
            pool.wait_ge(mask_in, 16)
            nc.gpsimd.tensor_scalar(mask_bias[:], mask8[:], 0.0, MASKED, ALU.is_equal, ALU.mult).then_inc(mask_done, 1)
            pool.wait_ge(w_hi_done, 1)
            nc.gpsimd.tensor_tensor(wq_lo[:], wq[:], wq_hi[:], ALU.subtract).then_inc(mask_done, 1)
            pool.wait_ge(w_hi_done, 2)
            nc.gpsimd.tensor_tensor(wkv_lo[:], wkv[:], wkv_hi[:], ALU.subtract).then_inc(mask_done, 1)
            pool.wait_ge(mask_done, 3)

        @block.scalar
        def _(act):
            layer_norm_all_act(act, centred, squared, var_done, root_done, ctx_nrm, squares, small, 1)
            act.wait_ge(wq_in, 16)
            act.copy(wq_hi[:], wq[:]).then_inc(w_hi_done, 1)
            act.wait_ge(wkv_in, 16)
            act.copy(wkv_hi[:], wkv[:]).then_inc(w_hi_done, 1)
            layer_norm_all_act(act, centred, squared, var_done, root_done, nrm, squares, small, 2)
            layer_norm_all_act(act, centred, squared, var_done, root_done, lat_nrm, squares, small, 3)
            for n in range(8):
                hi = keep["ctx_hi"] if n < 4 else keep["lat_hi"]
                act.wait_ge(bank_taken, n + 1)
                act.copy(hi[:, 512 * (n % 4):512 * (n % 4) + 512], turned[n % 2][:]).then_inc(hi_done, 1)

        @block.tensor
        def _(pe):
            for n in range(8):
                pe.wait_ge(ctx_done if n < 4 else lat_done, 1)
                if n >= 4:
                    pe.wait_ge(bank_taken, n - 3)
                rows = ctx_nrm if n < 4 else lat_nrm
                for i in range(4):
                    mm = pe.transpose(banks[n % 4][:, P * i:P * i + P], rows[:, 4 * (n % 4) + i, :], ident32[:])
                mm.then_inc(bank_ready, 1)

        @block.vector
        def _(dve):
            chain = Chain(dve, steps)
            dve.wait_ge(ctx_in, 16)
            inv = layer_norm_all(dve, chain, centred, squared, var_done, root_done, ctx_rows, ctx_nrm, squares, small, 1)
            dve.tensor_tensor(ctx_nrm[:], ctx_nrm[:], bc(inv, (P, NT, D), 2), ALU.mult).then_inc(ctx_done, 1)
            inv = layer_norm_all(dve, chain, centred, squared, var_done, root_done, xr, nrm, squares, small, 2)
            chain.then(dve.tensor_tensor(nrm[:], nrm[:], bc(inv, (P, NT, D), 2), ALU.mult))
            dve.wait_ge(small_in, 64)
            chain.then(dve.tensor_tensor(xr[:], xr[:], bc(bout[:], (P, NT, D), 1), ALU.add))
            inv = layer_norm_all(dve, chain, centred, squared, var_done, root_done, nrm, lat_nrm, squares, small, 3)
            dve.tensor_tensor(lat_nrm[:], lat_nrm[:], bc(inv, (P, NT, D), 2), ALU.mult).then_inc(lat_done, 1)
            chain.then(dve.tensor_tensor(keep["qk_gain"][:], q_gain[:], k_gain[:], ALU.mult))
            chain.then(dve.tensor_scalar(keep["qk_gain"][:], keep["qk_gain"][:], D1 ** -0.5, None, ALU.mult))

            def take(n):
                at = 0 if n < 4 else 2
                dve.wait_ge(bank_ready, n + 1)
                if n >= 2:
                    dve.wait_ge(hi_done, n - 1)
                    dve.wait_ge(lo_done, n - 1)
                dve.tensor_scalar(turned[n % 2][:], banks[n % 4][:], norm_w[:, at:at + 1], norm_w[:, at + 1:at + 2],
                                  ALU.mult, ALU.add).then_inc(bank_taken, 1)

            def low(n):
                hi, lo = (keep["ctx_hi"], keep["ctx_lo"]) if n < 4 else (keep["lat_hi"], keep["lat_lo"])
                cols = slice(512 * (n % 4), 512 * (n % 4) + 512)
                dve.wait_ge(hi_done, n + 1)
                dve.tensor_tensor(lo[:, cols], turned[n % 2][:], hi[:, cols], ALU.subtract).then_inc(lo_done, 1)

            take(0)
            for n in range(8):
                if n < 7:
                    take(n + 1)
                low(n)


def plan_step(s, first, last):
    p = s % PU
    prepare = not (last and s >= PU)
    ahead = not (last and s == 2 * PU - 1)
    rows = [("r", i, qt) for i in range(2) for qt in range(QT)] + [("neg",)] if ahead else []
    before = [] if first and s == 0 else [("w", -1, kt) for kt in range(KT)]
    jobs = []
    if prepare:
        jobs = [[("k", t) for t in range(KT)] + [("q", t) for t in range(QT)],
                [("v", t) for t in range(KT)],
                [("tk", t) for t in range(KT)] + [("tq", t) for t in range(QT)],
                []][p]
    if s == 1 and not first:
        jobs = [("o",)] + jobs
    head = [("s", 0, 0), ("s", 0, 1)]
    tail = [("s", 1, 0), ("s", 1, 1)] + [("w", 0, kt) for kt in range(KT)]
    if p == PU - 1:
        atoms = head + rows[:2] + before[:2] + rows[2:] + before[2:] + tail
    else:
        atoms = rows[:2] + before + rows[2:] + head + tail
    out, done = [], 0
    for n, atom in enumerate(atoms):
        out.append(atom)
        due = (n + 1) * len(jobs) // len(atoms)
        while done < due:
            out.append(jobs[done])
            done += 1
    out += jobs[done:]
    if prepare and p == 1:
        at = out.index(("s", 0, 1)) + 1
        out[at:at] = [("root",)]
        out += [("split", j) for j in range(4)]
    if prepare and p == 2:
        at = out.index(("neg",)) + 1
        out[at:at] = [("split", j) for j in range(4, 6)]
    if ahead:
        out.append(("m",))
    return out


MISC = ("k", "q", "v", "tk", "tq", "o", "m")
START = [("k", t) for t in range(KT)] + [("q", t) for t in range(QT)] + [("root",)] + [("v", t) for t in range(KT)] \
    + [("split", j) for j in range(6)] + [("tk", t) for t in range(KT)] + [("tq", t) for t in range(QT)] \
    + [("r", i, qt) for i in range(2) for qt in range(QT)] + [("neg",), ("m",)]


def misc_uses(events):
    return sum(1 for e in events if e[0] in MISC)


class Batch:

    STEPS = 2 * PU

    def __init__(self, b, first=False, last=False):
        self.b, self.first, self.last = b, first, last
        whole = sum(misc_uses(plan_step(s, False, False)) for s in range(self.STEPS))
        self.misc = misc_uses(START) if first else misc_uses(START) - 1 + whole * b

    def steps(self):
        use = self.misc
        for s in range(self.STEPS):
            events = []
            for e in plan_step(s, self.first, self.last):
                events.append((e, use))
                if e[0] in MISC:
                    use = use + 1
            yield s, events


def attend_layer1(nc, io, keep):
    with ExitStack() as ctx:
        def sb(name, shape, dt):
            return ctx.enter_context(nc.sbuf_tensor("e_" + name, shape, dt))

        def psum(name, shape):
            return ctx.enter_context(nc.psum_tensor("e_" + name, shape, F32))

        def sem(name):
            return ctx.enter_context(nc.semaphore("e_" + name))

        xr, ident32, ident16 = keep["xr"], keep["ident32"], keep["ident16"]
        q_stack = [sb(f"q_stack{i}", [P, HU, S], F16) for i in range(2)]
        k_stack = [sb(f"k_stack{i}", [P, HU, NK1], F16) for i in range(2)]
        q_high = [sb(f"q_high{i}", [P, HU, S], F16) for i in range(2)]
        k_high = [sb(f"k_high{i}", [P, HU, NK1], F16) for i in range(2)]
        v_ones = [sb(f"v_ones{i}", [P, KT, HU, P], F32) for i in range(2)]
        raw = sb("raw", [P, 6, HU, D1], F32)
        squares = [sb(f"squares{i}", [P, HU, D1], F32) for i in range(2)]
        sum_sq = sb("sum_sq", [P, 6 * HU], F32)
        inv = sb("inv", [P, 6 * HU], F32)
        natural = sb("natural", [P, 6, HU, P], F16)
        probs = [sb(f"probs{i}", [P, KT, S], F32) for i in range(2)]
        row_max = sb("row_max", [P, 2, QT], F32)
        neg_max = sb("neg_max", [P, 2 * QT], F32)
        neg_rows = [sb(f"neg_rows{i}", [2 * QT, P], F16) for i in range(2)]
        mixed = sb("mixed", [P, S], F32)
        summed = sb("summed", [P, S], F32)
        inverse = sb("inverse", [P, S], F32)
        attended = sb("attended", [P, H1 // 2, S], F32)

        row_scores = [psum(f"row_scores{i}", [P, NK1]) for i in range(QT)]
        scores = [psum(f"scores{i}", [P, KT, S]) for i in range(2)]
        mix = psum("mix", [P, 512])
        misc = psum("misc", [P, 512])

        cleared, fixed = sem("cleared"), sem("fixed")
        misc_ready, misc_taken = sem("misc_ready"), sem("misc_taken")
        squared, summed_sq, root_done, inv_steps, inv_done, normed, gained, hi_done, lo_done = (sem(n) for n in (
            "squared", "summed_sq", "root_done", "inv_steps", "inv_done", "normed", "gained", "hi_done", "lo_done"))
        copied = [sem(f"copied{i}") for i in range(2)]
        rows_ready, max_done, neg_done, max_in = (sem(n) for n in ("rows_ready", "max_done", "neg_done", "max_in"))
        scored, exp_done, weighed, mix_taken, inverted, att_done = (sem(n) for n in (
            "scored", "exp_done", "weighed", "mix_taken", "inverted", "att_done"))
        COPIES = 5
        UB = 2

        block = ctx.enter_context(nc.Block())

        def flow(engine, program):
            program(Batch(0, first=True))
            with engine.Fori(1, B - 1) as b:
                program(Batch(b))
            program(Batch(B - 1, last=True))

        @block.sync
        def _(sp):
            def finish(b, par, unit):
                if not (isinstance(unit, int) and unit < 2):
                    sp.wait_ge(scored, HU * (unit - 1))
                sp.dma_start(k_high[par][0:D1, :, :], k_stack[par][0:D1, :, :]).then_inc(copied[par], 16)
                sp.dma_start(q_high[par][0:D1, :, :], q_stack[par][D1:P, :, :]).then_inc(copied[par], 16)
                sp.dma_start(q_high[par][MROW1:MROW1 + 1, :, :], io["zeros"][:, 0:HU, :]).then_inc(copied[par], 16)
                mask = io["mask_bias"][ds(b, 1), :].unsqueeze(1)
                for half in range(2):
                    sp.dma_start(k_high[par][MROW1 + 1:MROW1 + 2, HU // 2 * half:HU // 2 * half + HU // 2, 0:S],
                                 mask.to_broadcast((1, HU // 2, S))).then_inc(copied[par], 16)

            def place_max(q, par, p, rows):
                sp.dma_start(q_high[par][MROW1:MROW1 + 1, 2 * p:2 * p + 2, :].rearrange("o h (t c) -> o (h t) c", t=QT), neg_rows[rows][:]).then_inc(max_in, 16)

            for par in range(2):
                sp.wait_ge(cleared, 6)
                sp.dma_start(q_high[par][MROW1 + 1:MROW1 + 2, :, :], io["ones"]).then_inc(fixed, 16)
            sp.wait_ge(misc_taken, misc_uses(START) - 1)
            finish(0, 0, 0)
            sp.wait_ge(misc_taken, misc_uses(START))
            place_max(0, 0, 0, 0)

            def batch(bt):
                for s, events in bt.steps():
                    b, hf, p = bt.b, s // PU, s % PU
                    for (name, *rest), use in events:
                        if name == "tq" and rest[0] == QT - 1:
                            sp.wait_ge(misc_taken, use + 1)
                            finish(b + hf, 1 - hf, UB * b + hf + 1)
                        if name == "m":
                            sp.wait_ge(misc_taken, use + 1)
                            q = 2 * PU * b + s + 1
                            place_max(q, hf if p < PU - 1 else 1 - hf, (p + 1) % PU, (s + 1) % 2)

            flow(sp, batch)

        @block.gpsimd
        def _(pool):
            for par in range(2):
                nc.gpsimd.memset(q_high[par][:].bitcast(F32), 0.0).then_inc(cleared, 1)
                nc.gpsimd.memset(k_high[par][:].bitcast(F32), 0.0).then_inc(cleared, 1)

            def unit(u):
                def norm(j):
                    pool.wait_ge(inv_done, u + 1)
                    nc.gpsimd.tensor_tensor(raw[:, j], raw[:, j], bc(inv[:, HU * j:HU * j + HU], (P, HU, D1), 2),
                                            ALU.mult).then_inc(normed, 1)

                def low(j):
                    at = slice(D1, P) if j < KT else slice(0, D1)
                    hi = slice(0, D1) if j < KT else slice(D1, P)
                    pool.wait_ge(hi_done, 6 * u + j + 1)
                    nc.gpsimd.tensor_tensor(natural[:, j, :, at], raw[:, j], natural[:, j, :, hi],
                                            ALU.subtract).then_inc(lo_done, 1)

                norm(0)
                for j in range(1, 6):
                    norm(j)
                    low(j - 1)
                low(5)

            with pool.Fori(0, UB * B) as u:
                unit(u)

        @block.tensor
        def _(pe):
            def three(out, a_hi, a_lo, b_hi, b_lo):
                pe.matmul(out, a_hi, b_hi, start=True, stop=False)
                pe.matmul(out, a_lo, b_hi, start=False, stop=False)
                return pe.matmul(out, a_hi, b_lo, start=False, stop=True)

            def shared(event, use, b, hf):
                name, *rest = event
                if not (isinstance(use, int) and use == 0):
                    pe.wait_ge(misc_taken, use)
                if name in ("k", "v", "q"):
                    t = rest[0]
                    of_ctx = name != "q" and t < QT
                    hi, lo = (keep["ctx_hi"], keep["ctx_lo"]) if of_ctx else (keep["lat_hi"], keep["lat_lo"])
                    at = ds(S * b + P * (t % QT), P)
                    w = ("wq_hi", "wq_lo") if name == "q" else ("wkv_hi", "wkv_lo")
                    col = (H1 * D1 if name == "v" else 0) + HU * D1 * hf
                    cols = slice(col, col + HU * D1)
                    three(misc[:], hi[:, at], lo[:, at], keep[w[0]][:, cols], keep[w[1]][:, cols]).then_inc(misc_ready, 1)

            def turn(j, use, u):
                pe.wait_ge(misc_taken, use)
                pe.wait_ge(lo_done, 6 * u + j + 1)
                for h in range(HU):
                    mm = pe.transpose(misc[:].bitcast(F16)[:, P * h:P * h + P], natural[:, j, h, :], ident16[:])
                mm.then_inc(misc_ready, 1)

            def turn_max(use, q):
                pe.wait_ge(misc_taken, use)
                pe.wait_ge(neg_done, q + 1)
                pe.transpose(misc[0:2 * QT, 0:P], neg_max[:], ident32[:]).then_inc(misc_ready, 1)

            def rows(q, par, p, i, qt):
                if not (isinstance(q, int) and q == 0 and i == 0):
                    pe.wait_ge(max_done, 4 * q + 2 * i + qt - 1)
                h = 2 * p + i
                pe.matmul(row_scores[qt][:], q_high[par][:, h, P * qt:P * qt + P], k_high[par][:, h, :],
                          start=True, stop=True).then_inc(rows_ready, 1)

            pe.wait_ge(keep["wout_in"], 16)
            use = 0
            for e in START:
                if e[0] in ("k", "q", "v"):
                    shared(e, use, 0, 0)
                elif e[0] in ("tk", "tq"):
                    turn(e[1] + (KT if e[0] == "tq" else 0), use, 0)
                elif e[0] == "r":
                    if e[1:] == (0, 0):
                        pe.wait_ge(copied[0], 16 * COPIES)
                        pe.wait_ge(fixed, 32)
                        pe.wait_ge(cleared, 8)
                    rows(0, 0, 0, *e[1:])
                elif e[0] == "m":
                    turn_max(use, 0)
                use += e[0] in MISC

            def batch(bt):
                b = bt.b
                for s, events in bt.steps():
                    hf, p = s // PU, s % PU
                    q = 2 * PU * b + s
                    for event, use in events:
                        name, *rest = event
                        if name in ("k", "q", "v"):
                            shared(event, use, b + hf, 1 - hf)
                        elif name in ("tk", "tq"):
                            turn(rest[0] + (KT if name == "tq" else 0), use, UB * b + hf + 1)
                        elif name == "m":
                            turn_max(use, q + 1)
                        elif name == "o":
                            pe.wait_ge(misc_taken, use)
                            project(b)
                        elif name == "r":
                            par = hf if p < PU - 1 else 1 - hf
                            if p == PU - 1 and tuple(rest) == (0, 0):
                                pe.wait_ge(copied[par], 16 * COPIES * (b + 1 if par else b + 2))
                            rows(q + 1, par, (p + 1) % PU, *rest)
                        elif name == "s":
                            i, half = rest
                            g, h = 2 * q + i, 2 * p + i
                            if i == 0 and half == 0:
                                pe.wait_ge(max_in, 16 * (q + 1))
                            if half == 0 and not (bt.first and s == 0):
                                pe.wait_ge(exp_done, g - 1)
                            for kt in (2 * half, 2 * half + 1):
                                out = scores[i][:, kt, :]
                                cols = slice(P * kt, P * kt + P)
                                pe.matmul(out, k_stack[hf][:, h, cols], q_stack[hf][:, h, :], start=True, stop=False)
                                mm = pe.matmul(out, k_high[hf][:, h, cols], q_high[hf][:, h, :], start=False, stop=True)
                            if half:
                                mm.then_inc(scored, 1)
                        elif name == "w":
                            weigh(2 * q + rest[0], (hf if rest[0] == 0 or p else 1 - hf), (2 * p + rest[0]) % HU, rest[0] % 2, rest[1])

            def weigh(g, par, h, buf, kt):
                if kt == 0:
                    pe.wait_ge(exp_done, g + 1)
                    if not (isinstance(g, int) and g == 0):
                        pe.wait_ge(mix_taken, g)
                mm = pe.matmul(mix[:, 0:S], v_ones[par][:, kt, h, :], probs[buf][:, kt, :], start=(kt == 0), stop=(kt == KT - 1))
                if kt == KT - 1:
                    mm.then_inc(weighed, 1)

            def project(b):
                pe.wait_ge(att_done, H1 // 2 * b)
                for qt in range(QT):
                    for pair in range(H1 // 2):
                        mm = pe.matmul(misc[:, P * qt:P * qt + P], attended[:, pair, P * qt:P * qt + P], keep["wout"][:, pair, :],
                                       start=(pair == 0), stop=(pair == H1 // 2 - 1))
                mm.then_inc(misc_ready, 1)

            flow(pe, batch)
            for kt in range(KT):
                weigh(H1 * B - 1, 1, HU - 1, 1, kt)
            pe.wait_ge(misc_taken, FINAL_USE)
            project(B)

        @block.scalar
        def _(act):
            def shared(event, use, par, u):
                name, *rest = event
                act.wait_ge(misc_ready, use + 1)
                if name in ("k", "q"):
                    j = rest[0] + (KT if name == "q" else 0)
                    if not (isinstance(u, int) and u == 0):
                        act.wait_ge(lo_done, 6 * u)
                    act.copy(raw[:, j], misc[:].rearrange("p (h d) -> p h d", h=HU)).then_inc(misc_taken, 1)
                    act.wait_ge(misc_taken, use + 1)
                    if not (isinstance(u, int) and u == 0 and j < 2):
                        act.wait_ge(summed_sq, 6 * u + j - 1)
                    act.activation(squares[j % 2][:], raw[:, j], ACT.Square).then_inc(squared, 1)
                elif name == "v":
                    act.copy(v_ones[par][:, rest[0], :, 0:D1], misc[:].rearrange("p (h d) -> p h d", h=HU)).then_inc(misc_taken, 1)
                elif name in ("tk", "tq"):
                    stack = k_stack[par] if name == "tk" else q_stack[par]
                    act.copy(stack[:, :, P * rest[0]:P * rest[0] + P],
                             misc[:].bitcast(F16).rearrange("p (h t) -> p h t", h=HU)).then_inc(misc_taken, 1)

            def take_rows(use, q, buf):
                act.wait_ge(misc_ready, use + 1)
                if not (isinstance(q, int) and q < 2):
                    act.wait_ge(max_in, 16 * (q - 1))
                act.copy(neg_rows[buf][:], misc[0:2 * QT, 0:P]).then_inc(misc_taken, 1)

            def roots(u):
                act.wait_ge(summed_sq, 6 * (u + 1))
                act.activation(sum_sq[:], sum_sq[:], ACT.Sqrt, scale=1.0 / D1).then_inc(root_done, 1)

            use = 0
            for e in START:
                if e[0] == "m":
                    take_rows(use, 0, 0)
                elif e[0] in MISC:
                    shared(e, use, 0, 0)
                elif e[0] == "root":
                    roots(0)
                use += e[0] in MISC

            def take_mix(q, g, i):
                act.wait_ge(weighed, g + 1)
                if i == 0 and not (isinstance(q, int) and q == 0):
                    act.wait_ge(att_done, q)
                at = slice(D1 * i, D1 * i + D1)
                act.copy(summed[at, :], mix[D1:P, 0:S])
                act.copy(mixed[at, :], mix[0:D1, 0:S]).then_inc(mix_taken, 1)

            def batch(bt):
                b = bt.b
                for s, events in bt.steps():
                    hf, p = s // PU, s % PU
                    q = 2 * PU * b + s
                    for event, use in events:
                        name, *rest = event
                        if name == "m":
                            take_rows(use, q + 1, (s + 1) % 2)
                        elif name == "o":
                            pass
                        elif name in MISC:
                            shared(event, use, 1 - hf, UB * b + hf + 1)
                        elif name == "root":
                            roots(UB * b + hf + 1)
                        elif name == "s" and rest[1] == 1:
                            g = 2 * q + rest[0]
                            act.wait_ge(scored, g + 1)
                            if not (bt.first and s == 0):
                                act.wait_ge(weighed, g - 1)
                            act.activation(probs[rest[0]][:], scores[rest[0]][:], ACT.Exp).then_inc(exp_done, 1)
                        elif name == "w" and rest[1] == KT - 1:
                            take_mix(q, 2 * q + rest[0], rest[0] % 2)

            flow(act, batch)
            take_mix(2 * PU * B - 1, H1 * B - 1, 1)

        @block.vector
        def _(dve):
            for par in range(2):
                dve.memset(v_ones[par][:, :, :, D1:P], 1.0).then_inc(cleared, 1)
            dve.wait_ge(cleared, 6)
            for par in range(2):
                dve.memset(k_high[par][MROW1:MROW1 + 1, :, :], 1.0).then_inc(cleared, 1)
            chain = Chain(dve, inv_steps)

            def sum_squares(u, j):
                dve.wait_ge(squared, 6 * u + j + 1)
                if j == 0 and not (isinstance(u, int) and u == 0):
                    dve.wait_ge(inv_done, u)
                dve.tensor_reduce(sum_sq[:, HU * j:HU * j + HU], squares[j % 2][:], AX.X, ALU.add).then_inc(summed_sq, 1)

            def invert(u):
                dve.wait_ge(root_done, u + 1)
                if not (isinstance(u, int) and u == 0):
                    dve.wait_ge(normed, 6 * u)
                chain.start(u)
                chain.then(dve.tensor_scalar(inv[:], sum_sq[:], 1e-8, None, ALU.max))
                dve.reciprocal(inv[:], inv[:]).then_inc(inv_done, 1)

            def high(u, j):
                dve.wait_ge(normed, 6 * u + j + 1)
                at = slice(0, D1) if j < KT else slice(D1, P)
                if j >= KT:
                    dve.tensor_tensor(raw[:, j], raw[:, j], bc(keep["qk_gain"][:], (P, HU, D1), 1), ALU.mult).then_inc(gained, 1)
                    dve.wait_ge(gained, QT * u + j - KT + 1)
                dve.tensor_copy(natural[:, j, :, at], raw[:, j]).then_inc(hi_done, 1)

            def maximum(q, i, qt):
                dve.wait_ge(rows_ready, 4 * q + 2 * i + qt + 1)
                if i == 0 and qt == 0 and not (isinstance(q, int) and q == 0):
                    dve.wait_ge(neg_done, q)
                dve.tensor_reduce(row_max[:, i, qt:qt + 1], row_scores[qt][:], AX.X, ALU.max).then_inc(max_done, 1)

            def negate(q, use_before):
                dve.wait_ge(max_done, 4 * (q + 1))
                if use_before is not None:
                    dve.wait_ge(misc_ready, use_before)
                dve.tensor_scalar(neg_max[:], row_max[:].rearrange("p i t -> p (i t)"), -1.0, None, ALU.mult).then_inc(neg_done, 1)

            for e in START:
                if e[0] in ("k", "q"):
                    sum_squares(0, e[1] + (KT if e[0] == "q" else 0))
                elif e[0] == "root":
                    invert(0)
                elif e[0] == "split":
                    high(0, e[1])
                elif e[0] == "r":
                    maximum(0, *e[1:])
                elif e[0] == "neg":
                    negate(0, None)

            def scale(q, pair):
                dve.wait_ge(mix_taken, 2 * (q + 1))
                dve.reciprocal(inverse[:], summed[:]).then_inc(inverted, 1)
                dve.wait_ge(inverted, q + 1)
                dve.tensor_tensor(attended[:, pair, :], mixed[:], inverse[:], ALU.mult).then_inc(att_done, 1)

            def add(b, use):
                dve.wait_ge(misc_ready, use + 1)
                rows = xr[:, ds(QT * (b - 1), QT), :]
                dve.tensor_tensor(rows, misc[:, 0:S].rearrange("p (t d) -> p t d", t=QT), rows, ALU.add).then_inc(misc_taken, 1)

            def batch(bt):
                b = bt.b
                for s, events in bt.steps():
                    hf, p = s // PU, s % PU
                    q = 2 * PU * b + s
                    u = UB * b + hf + 1
                    start = events[0][1]
                    waiting = False
                    for event, use in events:
                        name, *rest = event
                        if name == "o":
                            if s == 1:
                                add(b, use)
                                if waiting:
                                    scale(q - 1, 0)
                                    waiting = False
                        elif name in ("k", "q"):
                            sum_squares(u, rest[0] + (KT if name == "q" else 0))
                        elif name == "root":
                            invert(u)
                        elif name == "split":
                            if rest[0] == 0:
                                dve.wait_ge(misc_taken, start)
                            high(u, rest[0])
                        elif name == "r":
                            maximum(q + 1, *rest)
                        elif name == "neg":
                            negate(q + 1, start)
                        elif name == "w" and rest == [-1, KT - 1]:
                            if s == 1 and not bt.first and ("o",) in [e for e, _ in events[events.index((event, use)):]]:
                                waiting = True
                            else:
                                scale(q - 1, (s - 1) % (2 * PU))

            flow(dve, batch)
            scale(2 * PU * B - 1, H1 // 2 - 1)
            dve.wait_ge(misc_ready, FINAL_USE + 1)
            rows = xr[:, QT * (B - 1):QT * B, :]
            dve.tensor_tensor(rows, misc[:, 0:S].rearrange("p (t d) -> p t d", t=QT), rows, ALU.add).then_inc(misc_taken, 1)


def final_use():
    uses = None
    for _, events in Batch(B - 1, last=True).steps():
        event, at = events[-1]
        uses = at + (event[0] in MISC)
    return uses


FINAL_USE = final_use()


E1 = 8
F1 = 512
FB = F1 // P
CAP = -(-T * 5 // (4 * E1))
SLOTS = (E1 - 1) * CAP
ST = -(-SLOTS // P)
OUTSIDE = 65536.0
RC = 512


def experts_layer1(nc, io, keep, out):
    with ExitStack() as ctx:
        def sb(name, shape, dt):
            return ctx.enter_context(nc.sbuf_tensor("f_" + name, shape, dt))

        def psum(name, shape, dt=F32):
            return ctx.enter_context(nc.psum_tensor("f_" + name, shape, dt))

        def sem(name):
            return ctx.enter_context(nc.semaphore("f_" + name))

        xr, nrm, ident32, ident_b = keep["xr"], keep["nrm"], keep["ident32"], keep["ident_b"]
        w1, w2, b1, b2 = keep["w1"], keep["w2"], keep["b1"], keep["b2"]
        w1_hi, w1_lo = sb("w1_hi", [P, E1, F1], F16), sb("w1_lo", [P, E1, F1], F16)
        squares = sb("squares", [P, NT, D], F32)
        small = sb("small", [P, 4 * NT], F32)
        x_hi, x_lo = sb("x_hi", [P, ST * P], F16), sb("x_lo", [P, ST * P], F16)
        router = sb("router", [P, E1], F32)
        router_hi, router_lo = sb("router_hi", [P, E1], F16), sb("router_lo", [P, E1], F16)
        counting = sb("counting", [P, E0], F32)
        below = sb("below", [P, P], F32)
        logits = sb("logits", [P, NT, E1], F32)
        top = sb("top", [P, NT, 8], F32)
        top_at = sb("top_at", [P, NT, 8], U32)
        expert = sb("expert", [P, NT], F32)
        line = [sb(f"line{i}", [P, NT], F32) for i in range(6)]
        onehot = sb("onehot", [P, NT, E1], F32)
        key = sb("key", [P, NT, E1], F32)
        parts = sb("parts", [P, NT, 2, 32], BF16)
        keys_t = sb("keys_t", [P, T], BF16)
        onehot_t = sb("onehot_t", [P, T], BF16)
        compared = sb("compared", [P, 2, RC], BF16)
        tied = sb("tied", [P, P], BF16)
        counts = sb("counts", [P, NT, 8], F32)
        place = sb("place", [P, NT], U32)
        hidden = [sb(f"hidden{i}", [P, FB, 512], F32) for i in range(2)]
        placed = sb("placed", [P, ST, D], F32)
        y_rows = [sb(f"y_rows{i}", [P, 3, D], F32) for i in range(2)]
        fetched = sb("fetched", [P, NT, D], F32)
        y0 = squares

        hid = [psum(f"hid{i}", [P, 512]) for i in range(FB)]
        yb = [psum(f"yb{i}", [P, 512]) for i in range(2)]
        rk = [psum(f"rk{i}", [P, RC]) for i in range(2)]

        small_in, empty_out = sem("small_in"), sem("empty_out")
        centred, squared, var_done, root_done = (sem(n) for n in ("centred", "squared", "var", "root"))
        steps, norm_done, turned, hi_done, lo_done, w_hi_done, w_lo_done = (sem(n) for n in (
            "steps", "norm_done", "turned", "hi_done", "lo_done", "w_hi_done", "w_lo_done"))
        router_split, logits_ready, shifted, powers = (sem(n) for n in ("router_split", "logits_ready", "shifted", "powers"))
        parts_done, parts_turned, parts_taken, cleared = (sem(n) for n in ("parts_done", "parts_turned", "parts_taken", "cleared"))
        rank_ready, rank_taken, place_done, scattered, placed_in = (sem(n) for n in (
            "rank_ready", "rank_taken", "place_done", "scattered", "placed_in"))
        hid_ready, hid_taken, y_ready, y_taken, fetched_in, result, stored = (sem(n) for n in (
            "hid_ready", "hid_taken", "y_ready", "y_taken", "fetched_in", "result", "stored"))
        y_out = [sem(f"y_out{i}") for i in range(2)]

        NCHUNK = T // 512
        pieces = []
        for c in range(NCHUNK):
            pieces += [("h", c, fb) for fb in range(FB)]
            if c:
                pieces += [("y", c - 1, i) for i in range(4)]
        pieces += [("y", NCHUNK - 1, i) for i in range(4)]
        compares = [(t, c) for t in range(NT) for c in range(T // RC)]
        tiles = [(0, P), (P, P), (2 * P, CAP - 2 * P)]

        block = ctx.enter_context(nc.Block())

        @block.sync
        def _(sp):
            sp.dma_start(router[:], io["router"]).then_inc(small_in, 16)
            sp.dma_start(counting[:], io["counting"].partition_broadcast(P)).then_inc(small_in, 16)
            sp.dma_start(below[:], io["below"]).then_inc(small_in, 16)
            sp.dma_start(io["placed"], io["no_rows"]).then_inc(empty_out, 16)
            sp.wait_ge(scattered, 16 * NT)
            sp.dma_start(placed[:], io["placed"].rearrange("(t p) d -> p t d", p=P)).then_inc(placed_in, 16)

            def rows_out(e, buf):
                sp.wait_ge(y_taken, NCHUNK + e)
                for i, (at, n) in enumerate(tiles):
                    sp.dma_start(io["answers"][ds((e - 1) * CAP + at, n), :], y_rows[buf][0:n, i, :]).then_inc(y_out[buf], 16)

            with sp.Fori(0, (E1 - 1) // 2) as j:
                rows_out(2 * j + 1, 0)
                rows_out(2 * j + 2, 1)
            rows_out(E1 - 1, 0)
            for g in range(4):
                sp.wait_ge(result, g + 1)
                sp.dma_start(out.rearrange("(t p) d -> p t d", p=P)[:, 4 * g:4 * g + 4, :], xr[:, 4 * g:4 * g + 4, :]).then_inc(stored, 16)
            sp.wait_ge(stored, 64)

        @block.gpsimd
        def _(pool):
            nc.gpsimd.memset(fetched[:], 0.0).then_inc(cleared, 1)
            pool.wait_ge(w_hi_done, 1)
            nc.gpsimd.tensor_tensor(w1_lo[:, 0], w1[:, 0], w1_hi[:, 0], ALU.subtract).then_inc(w_lo_done, 1)
            pool.wait_ge(w_hi_done, 2)
            nc.gpsimd.tensor_tensor(w1_lo[:, 1:E1], w1[:, 1:E1], w1_hi[:, 1:E1], ALU.subtract).then_inc(w_lo_done, 1)
            pool.wait_ge(place_done, 1)
            pool.wait_ge(empty_out, 16)
            for t in range(NT):
                nc.gpsimd.indirect_dma_start(
                    out=io["placed"], out_offset=bass.IndirectOffsetOnAxis(ap=place[:, t:t + 1], axis=0),
                    in_=nrm[:, t, :], in_offset=None, bounds_check=SLOTS - 1, oob_is_err=False).then_inc(scattered, 16)
            pool.wait_ge(y_out[0], 16 * len(tiles) * (E1 // 2))
            pool.wait_ge(y_out[1], 16 * len(tiles) * (E1 // 2 - 1))
            pool.wait_ge(cleared, 2)
            for t in range(NT):
                nc.gpsimd.indirect_dma_start(
                    out=fetched[:, t, :], out_offset=None, in_=io["answers"],
                    in_offset=bass.IndirectOffsetOnAxis(ap=place[:, t:t + 1], axis=0),
                    bounds_check=SLOTS - 1, oob_is_err=False).then_inc(fetched_in, 16)

        @block.tensor
        def _(pe):
            def three(o, a_hi, a_lo, b_hi, b_lo):
                pe.matmul(o, a_hi, b_hi, start=True, stop=False)
                pe.matmul(o, a_lo, b_hi, start=False, stop=False)
                return pe.matmul(o, a_hi, b_lo, start=False, stop=True)

            pe.wait_ge(norm_done, 1)
            for g in range(4):
                for i in range(4):
                    mm = pe.transpose(hid[g][:, P * i:P * i + P], nrm[:, 4 * g + i, :], ident32[:])
                mm.then_inc(turned, 1)
            pe.wait_ge(router_split, 2)
            pe.wait_ge(lo_done, 4)
            for t in range(NT):
                cols = slice(P * t, P * t + P)
                mm = three(rk[0][:, E1 * t:E1 * t + E1], x_hi[:, cols], x_lo[:, cols], router_hi[:], router_lo[:])
            mm.then_inc(logits_ready, 1)

            def run(piece):
                kind, c, i = piece
                n = FB * c
                if kind == "h":
                    if n + i >= FB:
                        pe.wait_ge(hid_taken, n + i - FB + 1)
                    cols = slice(512 * c, 512 * c + 512)
                    w = slice(P * i, P * i + P)
                    three(hid[i][:], w1_hi[:, 0, w], w1_lo[:, 0, w], x_hi[:, cols], x_lo[:, cols]).then_inc(hid_ready, 1)
                else:
                    pe.wait_ge(hid_taken, n + FB)
                    if i == 0 and c >= 2:
                        pe.wait_ge(y_taken, c - 1)
                    for fb in range(FB):
                        mm = pe.matmul(yb[c % 2][:, P * i:P * i + P], hidden[c % 2][:, fb, P * i:P * i + P], w2[:, 0, fb, :],
                                       start=(fb == 0), stop=(fb == FB - 1))
                    if i == 3:
                        mm.then_inc(y_ready, 1)

            pe.wait_ge(w_lo_done, 1)
            pe.wait_ge(keep["w2_in"], 16)
            for piece in pieces[:FB]:
                run(piece)
            pe.wait_ge(parts_done, 1)
            for half in range(2):
                for g in range(2):
                    bank = rk[g][:].bitcast(BF16)
                    if half:
                        pe.wait_ge(parts_taken, g + 1)
                    for i in range(8):
                        mm = pe.transpose(bank[0:32, P * i:P * i + P], parts[:, 8 * g + i, half, :], ident_b[:])
                    mm.then_inc(parts_turned, 1)
            pe.wait_ge(parts_taken, 4)
            pe.wait_ge(cleared, 2)
            left = pieces[FB:]
            for n, (t, c) in enumerate(compares):
                if n >= 2:
                    pe.wait_ge(rank_taken, n - 1)
                pe.matmul(rk[n % 2][:], onehot_t[:, P * t:P * t + P], keys_t[:, RC * c:RC * c + RC], start=True, stop=True).then_inc(rank_ready, 1)
                if n % 2 and left:
                    run(left.pop(0))
            while left:
                run(left.pop(0))
            pe.wait_ge(placed_in, 16)
            for g in range(-(-ST // 4)):
                if g == 0:
                    pe.wait_ge(hid_taken, FB * NCHUNK)
                if g == 4:
                    pe.wait_ge(hi_done, 5)
                    pe.wait_ge(lo_done, 5)
                for i in range(min(4, ST - 4 * g)):
                    mm = pe.transpose(hid[g % 4][:, P * i:P * i + P], placed[:, 4 * g + i, :], ident32[:])
                mm.then_inc(turned, 1)
            pe.wait_ge(hi_done, 4 + -(-ST // 4))
            pe.wait_ge(lo_done, 4 + -(-ST // 4))
            pe.wait_ge(w_lo_done, 2)

            def hiddens(e):
                for fb in range(FB):
                    pe.wait_ge(hid_taken, FB * (NCHUNK + e - 1) + fb - FB + 1)
                    cols = ds((e - 1) * CAP, CAP)
                    w = slice(P * fb, P * fb + P)
                    at = ds(e, 1)
                    three(hid[fb][:, 0:CAP], w1_hi[:, at, w].rearrange("p e f -> p (e f)"), w1_lo[:, at, w].rearrange("p e f -> p (e f)"),
                          x_hi[:, cols], x_lo[:, cols]).then_inc(hid_ready, 1)

            def answers(e, buf):
                pe.wait_ge(hid_taken, FB * (NCHUNK + e))
                pe.wait_ge(y_taken, NCHUNK + e - 2)
                for i, (at, n) in enumerate(tiles):
                    for fb in range(FB):
                        mm = pe.matmul(yb[buf][0:n, P * i:P * i + P], hidden[buf][:, fb, at:at + n],
                                       w2[:, ds(e, 1), fb, :].rearrange("p e d -> p (e d)"),
                                       start=(fb == 0), stop=(fb == FB - 1))
                mm.then_inc(y_ready, 1)

            hiddens(1)
            with pe.Fori(0, (E1 - 1) // 2) as j:
                hiddens(2 * j + 2)
                answers(2 * j + 1, 0)
                hiddens(2 * j + 3)
                answers(2 * j + 2, 1)
            answers(E1 - 1, 0)

        @block.scalar
        def _(act):
            act.wait_ge(keep["w1_in"], 16)
            act.copy(w1_hi[:, 0], w1[:, 0]).then_inc(w_hi_done, 1)
            layer_norm_all_act(act, centred, squared, var_done, root_done, nrm, squares, small, 1)
            act.copy(w1_hi[:, 1:E1], w1[:, 1:E1]).then_inc(w_hi_done, 1)
            for g in range(4):
                act.wait_ge(turned, g + 1)
                act.copy(x_hi[:, 512 * g:512 * g + 512], hid[g][:]).then_inc(hi_done, 1)

            def relu(e, n, fb, buf, width):
                act.wait_ge(hid_ready, n + 1)
                act.activation(hidden[buf][:, fb, 0:width], hid[fb][:, 0:width], ACT.Relu,
                               bias=b1[:, ds(e * FB + fb, 1)]).then_inc(hid_taken, 1)

            act.wait_ge(keep["b1_in"], 16)
            relus = [p for p in pieces if p[0] == "h"]
            for n, (_, c, fb) in enumerate(relus):
                if n == FB:
                    act.wait_ge(shifted, 1)
                    act.activation(logits[:], logits[:], ACT.Exp).then_inc(powers, 1)
                if c >= 2:
                    act.wait_ge(y_ready, c - 1)
                relu(0, n, fb, c % 2, 512)
            for g in range(-(-ST // 4)):
                n = min(4, ST - 4 * g) * P
                act.wait_ge(turned, 5 + g)
                if g == 0:
                    act.wait_ge(hid_ready, FB * NCHUNK)
                act.copy(x_hi[:, 512 * g:512 * g + n], hid[g % 4][:, 0:n]).then_inc(hi_done, 1)

            def relus_of(e, buf):
                act.wait_ge(y_ready, NCHUNK + e - 2)
                for fb in range(FB):
                    relu(e, FB * (NCHUNK + e - 1) + fb, fb, buf, CAP)

            with act.Fori(0, (E1 - 1) // 2) as j:
                relus_of(2 * j + 1, 0)
                relus_of(2 * j + 2, 1)
            relus_of(E1 - 1, 0)

        @block.vector
        def _(dve):
            chain = Chain(dve, steps)
            inv = layer_norm_all(dve, chain, centred, squared, var_done, root_done, xr, nrm, squares, small, 1)
            dve.tensor_tensor(nrm[:], nrm[:], bc(inv, (P, NT, D), 2), ALU.mult).then_inc(norm_done, 1)
            dve.wait_ge(small_in, 48)
            dve.tensor_copy(router_hi[:], router[:]).then_inc(router_split, 1)
            dve.wait_ge(router_split, 1)
            dve.tensor_tensor(router_lo[:], router[:], router_hi[:], ALU.subtract).then_inc(router_split, 1)
            chain.then(dve.memset(keys_t[:].bitcast(F32), 0.0))
            chain.then(dve.memset(onehot_t[:].bitcast(F32), 0.0))
            chain.then(dve.memset(counts[:], 0.0))
            dve.memset(parts[:], 0.0).then_inc(cleared, 1)
            for g in range(4):
                cols = slice(512 * g, 512 * g + 512)
                dve.wait_ge(hi_done, g + 1)
                dve.tensor_tensor(x_lo[:, cols], hid[g][:], x_hi[:, cols], ALU.subtract).then_inc(lo_done, 1)
            total, prob, rank, kept, named, away = (x[:] for x in line)
            dve.wait_ge(logits_ready, 1)
            chain.then(dve.tensor_reduce(total, rk[0][:, 0:NT * E1].rearrange("p (t e) -> p t e", e=E1), AX.X, ALU.max))
            dve.tensor_tensor(logits[:], rk[0][:, 0:NT * E1].rearrange("p (t e) -> p t e", e=E1),
                              bc(total, (P, NT, E1), 2), ALU.subtract).then_inc(shifted, 1)
            dve.wait_ge(powers, 1)
            chain.then(dve.tensor_reduce(prob, logits[:], AX.X, ALU.add))
            chain.then(dve.reciprocal(prob, prob))
            for t in range(NT):
                ins = dve.max(top[:, t, :], logits[:, t, :])
            chain.then(ins)
            for t in range(NT):
                ins = dve.max_index(top_at[:, t, :], top[:, t, :], logits[:, t, :])
            chain.then(ins)
            chain.then(dve.tensor_copy(expert[:], top_at[:, :, 0]))
            chain.then(dve.tensor_tensor(onehot[:], bc(counting[:, 0:E1], (P, NT, E1), 1), bc(expert[:], (P, NT, E1), 2), ALU.is_equal))
            chain.then(dve.tensor_tensor(key[:], onehot[:], bc(prob, (P, NT, E1), 2), ALU.mult))
            dve.wait_ge(cleared, 2)
            for i in range(3):
                chain.then(dve.tensor_copy(parts[:, :, 0, E1 * i:E1 * i + E1], onehot[:]))
                step = dve.tensor_copy(parts[:, :, 1, E1 * i:E1 * i + E1], key[:])
                if i == 2:
                    step.then_inc(parts_done, 1)
                else:
                    chain.then(step)
                if i < 2:
                    chain.then(dve.tensor_tensor(key[:], key[:], parts[:, :, 1, E1 * i:E1 * i + E1], ALU.subtract))
            for half in range(2):
                dest = (onehot_t, keys_t)[half]
                for g in range(2):
                    dve.wait_ge(parts_turned, 2 * half + g + 1)
                    dve.tensor_copy(dest[0:32, 8 * P * g:8 * P * g + 8 * P], rk[g][:].bitcast(BF16)[0:32, :]).then_inc(parts_taken, 1)
            def rows_of_0(c):
                dve.wait_ge(y_ready, c + 1)
                dve.tensor_tensor(y0[:, 4 * c:4 * c + 4, :], yb[c % 2][:].rearrange("p (t d) -> p t d", t=4),
                                  bc(b2[:, 0, :], (P, 4, D), 1), ALU.add).then_inc(y_taken, 1)

            dve.wait_ge(keep["b2_in"], 16)
            for n, (t, c) in enumerate(compares):
                dve.wait_ge(rank_ready, n + 1)
                bank = rk[n % 2]
                own = P * t - RC * c
                cut = min(max(own, 0), RC)
                mine = prob[:, t:t + 1]
                ops = []
                if cut > 0:
                    ops.append((slice(0, cut), ALU.is_ge, c))
                if cut < RC:
                    ops.append((slice(cut, RC), ALU.is_gt, 4 + c))
                if n >= 2:
                    dve.wait_ge(rank_taken, n - 1)
                for cells, op, at in ops:
                    ins = dve.tensor_scalar(compared[:, n % 2, cells], bank[:, cells], mine, None, op, ALU.add, accum_out=counts[:, t, at:at + 1])
                if 0 <= own < RC:
                    ins = dve.scalar_tensor_tensor(out=tied[:], in0=bank[:, own:own + P], scalar=mine, in1=below[:],
                                                   op0=ALU.is_equal, op1=ALU.mult, accum_out=line[5][:, t:t + 1])
                ins.then_inc(rank_taken, 1)
                if n in (18, 34, 50):
                    rows_of_0((n - 18) // 16)
            dve.wait_ge(rank_taken, len(compares))
            chain.then(dve.tensor_reduce(rank, counts[:], AX.X, ALU.add))
            chain.then(dve.tensor_tensor(rank, rank, away, ALU.add))
            chain.then(dve.tensor_scalar(kept, rank, float(CAP), None, ALU.is_lt))
            chain.then(dve.tensor_scalar(named, expert[:], 0.0, None, ALU.is_gt))
            chain.then(dve.tensor_tensor(kept, kept, named, ALU.mult))
            chain.then(dve.tensor_scalar(named, expert[:], float(CAP), float(OUTSIDE - CAP), ALU.mult, ALU.add))
            chain.then(dve.tensor_tensor(named, named, rank, ALU.add))
            chain.then(dve.tensor_scalar(away, kept, -OUTSIDE, None, ALU.mult))
            chain.then(dve.tensor_tensor(named, named, away, ALU.add))
            dve.tensor_copy(place[:], named).then_inc(place_done, 1)
            rows_of_0(NCHUNK - 1)
            chain.then(dve.tensor_scalar(kept, kept, -1.0, 1.0, ALU.mult, ALU.add))
            dve.wait_ge(y_taken, NCHUNK)
            chain.then(dve.tensor_tensor(y0[:], y0[:], bc(kept, (P, NT, D), 2), ALU.mult))
            chain.then(dve.tensor_tensor(xr[:], xr[:], y0[:], ALU.add))
            for g in range(-(-ST // 4)):
                n = min(4, ST - 4 * g) * P
                dve.wait_ge(hi_done, 5 + g)
                dve.tensor_tensor(x_lo[:, 512 * g:512 * g + n], hid[g % 4][:, 0:n], x_hi[:, 512 * g:512 * g + n], ALU.subtract).then_inc(lo_done, 1)

            def rows_of(e, buf, uses=None):
                dve.wait_ge(y_ready, NCHUNK + e)
                if uses is not None:
                    dve.wait_ge(y_out[buf], 16 * len(tiles) * uses)
                bias = b2[:, ds(e, 1), :]
                dve.tensor_tensor(y_rows[buf][:, 0:2, :], yb[buf][:, 0:2 * P].rearrange("p (t d) -> p t d", t=2),
                                  bias.to_broadcast((P, 2, D)), ALU.add)
                n = tiles[2][1]
                dve.tensor_tensor(y_rows[buf][0:n, 2, :], yb[buf][0:n, 2 * P:3 * P], bias[0:n].rearrange("p e d -> p (e d)"),
                                  ALU.add).then_inc(y_taken, 1)

            rows_of(1, 0)
            rows_of(2, 1)
            with dve.Fori(1, (E1 - 1) // 2) as j:
                rows_of(2 * j + 1, 0, j)
                rows_of(2 * j + 2, 1, j)
            rows_of(E1 - 1, 0, (E1 - 1) // 2)
            dve.wait_ge(fetched_in, 16 * NT)
            for g in range(4):
                cols = slice(4 * g, 4 * g + 4)
                dve.tensor_tensor(xr[:, cols, :], xr[:, cols, :], fetched[:, cols, :], ALU.add).then_inc(result, 1)


def build(nc, io, out, stop=99):
    with ExitStack() as ctx:
        def sb(name, shape, dt):
            return ctx.enter_context(nc.sbuf_tensor(name, shape, dt))

        keep = {
            "xr": sb("xr", [P, NT, D], F32),
            "nrm": sb("nrm", [P, NT, D], F32),
            "ident32": sb("ident32", [P, P], F32),
            "ident16": sb("ident16", [P, P], F16),
            "ident_b": sb("ident_b", [P, P], BF16),
            "nothing": sb("nothing", [P, 8], F32),
            "wo0": sb("wo0", [P, D], F32),
            "wo0_in": ctx.enter_context(nc.semaphore("wo0_in")),
        }
        io["parts"] = nc.dram_tensor("parts_scratch", (4, P, T), F16, kind="Internal").ap()
        with ExitStack() as layer0:
            keep["bias_q"] = layer0.enter_context(nc.sbuf_tensor("bias_q", [P, NT, S], F16))
            keep["bias_k"] = layer0.enter_context(nc.sbuf_tensor("bias_k", [P, NT, S], F16))
            keep["v_all"] = layer0.enter_context(nc.sbuf_tensor("v_all", [P, NT, D], F32))
            project_layer0(nc, io, keep)
            attend_layer0(nc, io, keep)
        if stop <= 1:
            store(nc, keep, out)
            return
        experts_layer0(nc, io, keep)
        if stop <= 2:
            store(nc, keep, out)
            return
        io["mask_bias"] = nc.dram_tensor("mask_scratch", (B, S), F16, kind="Internal").ap()
        with ExitStack() as layer1:
            def sb1(name, shape, dt):
                return layer1.enter_context(nc.sbuf_tensor(name, shape, dt))

            for name in ("ctx_hi", "ctx_lo", "lat_hi", "lat_lo"):
                keep[name] = sb1(name, [P, T], F16)
            for name in ("wq_hi", "wq_lo"):
                keep[name] = sb1(name, [P, H1 * D1], F16)
            for name in ("wkv_hi", "wkv_lo"):
                keep[name] = sb1(name, [P, 2 * H1 * D1], F16)
            keep["wout"] = sb1("wout", [P, H1 // 2, D], F32)
            keep["qk_gain"] = sb1("qk_gain", [P, D1], F32)
            keep["wout_in"] = layer1.enter_context(nc.semaphore("wout_in"))
            prepare_layer1(nc, io, keep)
            attend_layer1(nc, io, keep)
        if stop <= 3:
            store(nc, keep, out)
            return
        io["placed"] = nc.dram_tensor("placed_scratch", (ST * P, D), F32, kind="Internal").ap()
        io["answers"] = nc.dram_tensor("answers_scratch", (SLOTS, D), F32, kind="Internal").ap()
        keep["w1"] = sb("w1", [P, E1, F1], F32)
        keep["w2"] = sb("w2", [P, E1, FB, D], F32)
        keep["b1"] = sb("b1", [P, E1 * FB], F32)
        keep["b2"] = sb("b2", [P, E1, D], F32)
        for name in ("w1_in", "w2_in", "b1_in", "b2_in"):
            keep[name] = ctx.enter_context(nc.semaphore(name))
        with nc.Block() as block:
            @block.sync
            def _(sp):
                sp.dma_start(keep["w1"][:], io["w1"]).then_inc(keep["w1_in"], 16)
                sp.dma_start(keep["b1"][:], io["b1"]).then_inc(keep["b1_in"], 16)
                sp.dma_start(keep["w2"][:], io["w2"]).then_inc(keep["w2_in"], 16)
                sp.dma_start(keep["b2"][:], io["b2"].partition_broadcast(P)).then_inc(keep["b2_in"], 16)
        experts_layer1(nc, io, keep, out)


def store(nc, keep, out):
    with nc.semaphore("stored") as stored, nc.Block() as block:
        @block.sync
        def _(sp):
            sp.dma_start(out.rearrange("(t p) d -> p t d", p=P), keep["xr"][:]).then_inc(stored, 16)
            sp.wait_ge(stored, 16)


def layout(inputs):
    a = {k: np.asarray(v) for k, v in inputs.items()}
    mask = a["mask_BxSxS2_ik1"]

    def rows(x):
        return x.reshape(NT, P, D).transpose(1, 0, 2)

    gate_up = a["L0_ffn_experts_gate_up"].reshape(PAIRS, 2, 2, I0, D)
    w0 = np.concatenate([
        np.stack([a["L0_ffn_shared_gate_w"].T, a["L0_ffn_shared_up_w"].T, a["L0_ffn_shared_down_w"].T], 1)[None],
        np.stack([gate_up[:, :, 0].reshape(PAIRS, P, D).transpose(0, 2, 1),
                  gate_up[:, :, 1].reshape(PAIRS, P, D).transpose(0, 2, 1),
                  a["L0_ffn_experts_down"].transpose(0, 2, 1).reshape(PAIRS, P, D)], 2)])
    return {
        "w1": a["L1_ffn_W1"].transpose(1, 0, 2),
        "w2": a["L1_ffn_W2"].reshape(E1, FB, P, D).transpose(2, 0, 1, 3),
        "b1": a["L1_ffn_b1"].reshape(E1, FB, P).transpose(2, 0, 1).reshape(P, E1 * FB),
        "b2": a["L1_ffn_b2"],
        "router": a["L1_ffn_router_w"].T,
        "below": np.tril(np.ones((P, P), np.float32), -1),
        "no_rows": np.zeros((ST * P, D), np.float32),
        "ctx_rows": rows(a["ctx_1024"]),
        "norm_w": np.stack([a["L1_xattn_ln_x_g"], a["L1_xattn_ln_x_b"], a["L1_xattn_ln_l_g"], a["L1_xattn_ln_l_b"]], 1),
        "q_gain": a["L1_xattn_qn_g"], "k_gain": a["L1_xattn_kn_g"], "bout": a["L1_xattn_bout"],
        "mask8": a["mask_BxS2_bf1"].view(np.uint8),
        "wq1": a["L1_xattn_Wq"], "wkv1": a["L1_xattn_Wkv"],
        "wout": a["L1_xattn_Wout"].reshape(H1 // 2, P, D).transpose(1, 0, 2),
        "ones": np.ones((1, HU, S), np.float16),
        "w0": w0,
        "gate0": a["L0_ffn_gate_weight"].T,
        "bias0": a["L0_ffn_e_score_correction_bias"],
        "counting": np.arange(E0, dtype=np.float32),
        "spread0": np.tile(np.kron(np.eye(E0), np.ones((1, I0))), (3, 1)).astype(np.float16),
        "x_rows": rows(a["x"]),
        "ctx_t": a["ctx_1024"].reshape(T, D).T,
        "wq0": a["L0_xattn_w_q"].T, "wk0": a["L0_xattn_w_k"].T, "wv0": a["L0_xattn_w_v"].T, "wo0": a["L0_xattn_w_o"].T,
        "mask_q": mask.reshape(NT, P, S).transpose(1, 0, 2),
        "mask_k": mask.transpose(0, 2, 1).reshape(NT, P, S).transpose(1, 0, 2),
        "zeros": np.zeros((1, H0, S), np.float16),
    }


def kernel(**inputs):
    import concourse.bacc as bacc
    from concourse.bass_utils import run_bass_kernel_spmd

    nc = bacc.Bacc("TRN2", target_bir_lowering=False, num_devices=1)
    arrays = {f"in_{k}": np.ascontiguousarray(v) for k, v in layout(inputs).items()}
    io = {k[3:]: nc.dram_tensor(k, v.shape, mybir.dt.from_np(v.dtype), kind="ExternalInput").ap() for k, v in arrays.items()}
    out = nc.dram_tensor("out", (T, D), F32, kind="ExternalOutput").ap()
    build(nc, io, out)
    got = run_bass_kernel_spmd(nc, [arrays], core_ids=[0])
    return got.results[0]["out"].reshape(B, S, D)
```

```python
from contextlib import ExitStack

import numpy as np

import concourse.bass as bass
from concourse import mybir

F32 = mybir.dt.float32
F16 = mybir.dt.float16
BF16 = mybir.dt.bfloat16
I32 = mybir.dt.int32
U32 = mybir.dt.uint32
U8 = mybir.dt.uint8
ALU = mybir.AluOpType
ACT = mybir.ActivationFunctionType
AX = mybir.AxisListType
ds = bass.ds

P = 128
D = 128
B = 8
S = 256
T = B * S
NT = T // P
QT = S // P
EPS = 1e-5

H0 = 16
K0 = D // H0
NP0 = H0 // 2
MROW = 32
RING = 3
MASKED = -32768.0


AHEAD = [(0,), (1,), (2,), (3,), (4, 5), (6, 7), (), ()]
LAST_ROWS = 5
TURN = 6
STACK_DMAS = 4


class Chain:

    def __init__(self, engine, sem):
        self.engine, self.sem, self.base, self.steps = engine, sem, 0, 0

    def start(self, base):
        self.base, self.steps = base, 0

    def then(self, instruction):
        instruction.then_inc(self.sem, 1)
        self.steps += 1
        self.engine.wait_ge(self.sem, self.base + self.steps)


def bc(ap, shape, axis):
    return ap.unsqueeze(axis).to_broadcast(shape)


def layer_norm_all(dve, chain, sem_centred, sem_squared, sem_var, sem_root, src, out, squares, small, count, meanwhile=None):
    total, shift, var, inv = (small[:, i * NT:(i + 1) * NT] for i in range(4))
    chain.then(dve.tensor_reduce(total, src[:], AX.X, ALU.add))
    chain.then(dve.tensor_scalar(shift, total, -1.0 / D, None, ALU.mult))
    dve.tensor_tensor(out[:], src[:], bc(shift, (P, NT, D), 2), ALU.add).then_inc(sem_centred, 1)
    if meanwhile:
        meanwhile()
    dve.wait_ge(sem_squared, count)
    chain.then(dve.tensor_reduce(var, squares[:], AX.X, ALU.add))
    dve.tensor_scalar(var, var, 1.0 / D, EPS, ALU.mult, ALU.add).then_inc(sem_var, 1)
    dve.wait_ge(sem_root, count)
    chain.then(dve.reciprocal(inv, var))
    return inv


def layer_norm_all_act(act, sem_centred, sem_squared, sem_var, sem_root, out, squares, small, count):
    var = small[:, 2 * NT:3 * NT]
    act.wait_ge(sem_centred, count)
    act.activation(squares[:], out[:], ACT.Square).then_inc(sem_squared, 1)
    act.wait_ge(sem_var, count)
    act.activation(var, var, ACT.Sqrt).then_inc(sem_root, 1)


def identity(nc, pool, ident32, ident16, ident_b, sem, done):
    pool.memset(ident32[:], 0.0).then_inc(sem, 1)
    pool.wait_ge(sem, 1)
    pool.affine_select(out=ident32[:], in_=ident32[:], compare_op=ALU.not_equal, fill=1.0, base=0,
                       pattern=[[-1, P]], channel_multiplier=1).then_inc(sem, 1)
    pool.wait_ge(sem, 2)
    pool.tensor_copy(ident_b[:], ident32[:]).then_inc(done, 1)
    pool.tensor_copy(ident16[:], ident32[:]).then_inc(done, 1)


def project_layer0(nc, io, keep):
    with ExitStack() as ctx:
        def sb(name, shape, dt):
            return ctx.enter_context(nc.sbuf_tensor(name, shape, dt))

        def sem(name):
            return ctx.enter_context(nc.semaphore(name))

        xr, nrm, ident32, ident16 = keep["xr"], keep["nrm"], keep["ident32"], keep["ident16"]
        bias_q, bias_k, v_all = keep["bias_q"], keep["bias_k"], keep["v_all"]
        squares = sb("a_squares", [P, NT, D], F32)
        small = sb("a_small", [P, 6 * NT], F32)
        mask_q = sb("a_mask_q", [P, NT, S], I32)
        mask_k = sb("a_mask_k", [P, NT, S], I32)
        ctx_t = sb("a_ctx_t", [P, T], F32)
        w3 = sb("a_w3", [P, 3, D], F32)
        w3_hi = sb("a_w3_hi", [P, 3, D], F16)
        w3_lo = sb("a_w3_lo", [P, 3, D], F16)
        ctx_hi = sb("a_ctx_hi", [P, T], F16)
        ctx_lo = sb("a_ctx_lo", [P, T], F16)
        x_hi = sb("a_x_hi", [P, T], F16)
        x_lo = sb("a_x_lo", [P, T], F16)
        parts = sb("a_parts", [P, 4, T], F16)
        banks = [ctx.enter_context(nc.psum_tensor(f"a_bank{i}", [P, 512], F32)) for i in range(4)]

        x_in, ctx_in, w_in, mask_in, mask_k_in = (sem(f"a_{n}") for n in ("x_in", "ctx_in", "w_in", "mask_in", "mask_k_in"))
        made, ident_done = sem("a_made"), sem("a_ident_done")
        centred, squared, var_done, root_done = keep["norm_sems"]
        q_stack, k_stack, loaded = keep["q_stack"], keep["k_stack"], keep["loaded"]
        zeroed, ctx_hi_done = sem("a_zeroed"), sem("a_ctx_hi_done")
        steps, operands, norm_done = sem("a_steps"), sem("a_operands"), sem("a_norm_done")
        bank_ready, hi_done, lo_done, stored = (sem(f"a_{n}") for n in ("bank_ready", "hi_done", "lo_done", "stored"))
        masks_done = sem("a_masks_done")

        jobs = [("k", g) for g in range(4)] + [("v", g) for g in range(4)]
        jobs += [(kind, g) for g in range(4) for kind in ("t", "q")]
        order = {job: n for n, job in enumerate(jobs)}
        split = [n for n, job in enumerate(jobs) if job[0] != "v"]

        def lows(n):
            return sum(1 for m in split if m <= n)

        block = ctx.enter_context(nc.Block())

        @block.sync
        def _(sp):
            sp.dma_start(xr[:], io["x_rows"]).then_inc(x_in, 16)
            sp.dma_start(ctx_t[:], io["ctx_t"]).then_inc(ctx_in, 16)
            sp.dma_start(w3[:, 0, :], io["wq0"]).then_inc(w_in, 16)
            sp.dma_start(w3[:, 1, :], io["wk0"]).then_inc(w_in, 16)
            sp.dma_start(w3[:, 2, :], io["wv0"]).then_inc(w_in, 16)
            sp.dma_start(mask_q[:], io["mask_q"]).then_inc(mask_in, 16)
            sp.dma_start(mask_k[:], io["mask_k"]).then_inc(mask_k_in, 16)
            sp.dma_start(keep["wo0"][:], io["wo0"]).then_inc(keep["wo0_in"], 16)
            for i, name in enumerate(("k", "q")):
                sp.wait_ge(hi_done, order[(name, 3)] + 1)
                sp.wait_ge(lo_done, lows(order[(name, 3)]))
                at = 2 if name == "k" else 0
                sp.dma_start(io["parts"].rearrange("a p t -> p a t")[:, at:at + 2, :],
                             parts[:, at:at + 2, :]).then_inc(stored, 16)
                sp.wait_ge(stored, 16 * (i + 1))
                sp.wait_ge(zeroed, 2 * RING)
                for b in range(RING):
                    load_stack(sp, io, (k_stack if name == "k" else q_stack)[b], name, b, loaded[b])

        @block.gpsimd
        def _(pool):
            nc.gpsimd.memset(keep["nothing"][:], 0.0)
            identity(nc, nc.gpsimd, ident32, ident16, keep["ident_b"], made, ident_done)
            for stack in k_stack + q_stack:
                nc.gpsimd.memset(stack[:].bitcast(F32), 0.0).then_inc(zeroed, 1)
            pool.wait_ge(mask_in, 16)
            nc.gpsimd.tensor_scalar(bias_q[:], mask_q[:], 0.0, MASKED, ALU.is_equal, ALU.mult).then_inc(masks_done, 1)
            pool.wait_ge(masks_done, 2)

        @block.scalar
        def _(act):
            act.wait_ge(ctx_in, 16)
            act.copy(ctx_hi[:], ctx_t[:]).then_inc(ctx_hi_done, 1)
            layer_norm_all_act(act, centred, squared, var_done, root_done, nrm, squares, small, 1)
            for n, (kind, g) in enumerate(jobs):
                act.wait_ge(bank_ready, n + 1)
                if kind == "v":
                    act.copy(v_all[:, 4 * g:4 * g + 4, :], banks[n % 4][:].rearrange("p (t d) -> p t d", t=4)).then_inc(hi_done, 1)
                    continue
                out = x_hi if kind == "t" else parts[:, 0 if kind == "q" else 2, :]
                act.copy(out[:, 512 * g:512 * g + 512], banks[n % 4][:]).then_inc(hi_done, 1)

        @block.tensor
        def _(pe):
            def three(out, a_hi, a_lo, b_hi, b_lo):
                pe.matmul(out, a_hi, b_hi, start=True, stop=False)
                pe.matmul(out, a_lo, b_hi, start=False, stop=False)
                return pe.matmul(out, a_hi, b_lo, start=False, stop=True)

            for n, (kind, g) in enumerate(jobs):
                bank = banks[n % 4]
                if n >= 4:
                    pe.wait_ge(hi_done, n - 3)
                    pe.wait_ge(lo_done, lows(n - 4))
                cols = slice(512 * g, 512 * g + 512)
                if kind == "k":
                    pe.wait_ge(operands, 3)
                    mm = three(bank[:], w3_hi[:, 1, :], w3_lo[:, 1, :], ctx_hi[:, cols], ctx_lo[:, cols])
                elif kind == "q":
                    pe.wait_ge(hi_done, order[("t", g)] + 1)
                    pe.wait_ge(lo_done, lows(order[("t", g)]))
                    mm = three(bank[:], w3_hi[:, 0, :], w3_lo[:, 0, :], x_hi[:, cols], x_lo[:, cols])
                elif kind == "v":
                    for i in range(4):
                        t = slice(512 * g + P * i, 512 * g + P * i + P)
                        mm = three(bank[:, P * i:P * i + P], ctx_hi[:, t], ctx_lo[:, t], w3_hi[:, 2, :], w3_lo[:, 2, :])
                else:
                    pe.wait_ge(ident_done, 2)
                    pe.wait_ge(norm_done, 1)
                    for i in range(4):
                        mm = pe.transpose(bank[:, P * i:P * i + P], nrm[:, 4 * g + i, :], ident32[:])
                mm.then_inc(bank_ready, 1)

        @block.vector
        def _(dve):
            chain = Chain(dve, steps)

            def split():
                dve.wait_ge(w_in, 48)
                dve.tensor_copy(w3_hi[:], w3[:]).then_inc(operands, 1)
                dve.wait_ge(ctx_hi_done, 1)
                dve.tensor_tensor(ctx_lo[:], ctx_t[:], ctx_hi[:], ALU.subtract).then_inc(operands, 1)
                dve.wait_ge(operands, 1)
                dve.tensor_tensor(w3_lo[:], w3[:], w3_hi[:], ALU.subtract).then_inc(operands, 1)

            dve.wait_ge(x_in, 16)
            inv = layer_norm_all(dve, chain, centred, squared, var_done, root_done, xr, nrm, squares, small, 1, split)
            any_key, seen = small[:, 4 * NT:5 * NT], small[:, 5 * NT:6 * NT]
            dve.wait_ge(mask_in, 16)
            chain.then(dve.tensor_reduce(any_key, mask_q[:], AX.X, ALU.max, apply_absolute_value=True))
            chain.then(dve.tensor_scalar(seen, any_key, 0.0, None, ALU.is_gt))
            chain.then(dve.tensor_tensor(inv, inv, seen, ALU.mult))
            dve.tensor_tensor(nrm[:], nrm[:], bc(inv, (P, NT, D), 2), ALU.mult).then_inc(norm_done, 1)
            for n, (kind, g) in enumerate(jobs):
                if kind == "v":
                    continue
                dve.wait_ge(hi_done, n + 1)
                hi, lo = (x_hi, x_lo) if kind == "t" else (parts[:, i + (0 if kind == "q" else 2), :] for i in range(2))
                cols = slice(512 * g, 512 * g + 512)
                dve.tensor_tensor(lo[:, cols], banks[n % 4][:], hi[:, cols], ALU.subtract).then_inc(lo_done, 1)
            dve.wait_ge(mask_k_in, 16)
            dve.tensor_scalar(bias_k[:], mask_k[:], 0.0, MASKED, ALU.is_equal, ALU.mult).then_inc(masks_done, 1)


def load_stack(sp, io, stack, name, b, loaded):
    hi, lo = (io["parts"][i + (2 if name == "k" else 0)].rearrange("(h j) t -> j h t", j=K0)[:, :, b * S:b * S + S]
              for i in range(2))
    for i, part in enumerate((hi, lo, hi) if name == "k" else (hi, hi, lo)):
        sp.dma_start(stack[K0 * i:K0 * i + K0, :, :], part).then_inc(loaded, 16)
    sp.dma_start(stack[MROW:MROW + 1, :, :], io["ones"] if name == "k" else io["zeros"]).then_inc(loaded, 16)


def attend_layer0(nc, io, keep):
    with ExitStack() as ctx:
        def sb(name, shape, dt):
            return ctx.enter_context(nc.sbuf_tensor(name, shape, dt))

        def psum(name, shape):
            return ctx.enter_context(nc.psum_tensor(name, shape, F32))

        def sem(name):
            return ctx.enter_context(nc.semaphore("b_" + name))

        xr, ident32, ident16 = keep["xr"], keep["ident32"], keep["ident16"]
        bias_q, bias_k, v_all, wo0 = keep["bias_q"], keep["bias_k"], keep["v_all"], keep["wo0"]
        nothing = keep["nothing"]
        q_stack, k_stack, loaded = keep["q_stack"], keep["k_stack"], keep["loaded"]
        VW = QT * H0 * P
        v_wide = [sb(f"b_v_wide{i}", [P, VW + P], F32) for i in range(RING)]
        probs = [sb(f"b_probs{i}", [P, QT, 2, S], F32) for i in range(2)]
        row_max = sb("b_row_max", [P, QT, H0], F32)
        neg_max = sb("b_neg_max", [P, QT * H0], F32)
        neg_rows = sb("b_neg_rows", [QT * H0, P], F16)
        summed = sb("b_summed", [P, S], F32)
        inverse = sb("b_inverse", [P, S], F32)
        mixed = sb("b_mixed", [P, S], F32)
        attended = sb("b_attended", [P, S], F32)

        row_scores = [psum(f"b_row_scores{i}", [P, 2, S]) for i in range(QT)]
        scores = [psum(f"b_scores{i}", [P, QT, 2, S]) for i in range(2)]
        mix = psum("b_mix", [P, 512])
        misc = psum("b_misc", [P, 512])

        zeroed, ones_done, v_ready = sem("zeroed"), sem("ones_done"), sem("v_ready")
        rows_ready, max_done, neg_done, turned, rows_done, max_in = (sem(n) for n in (
            "rows_ready", "max_done", "neg_done", "turned", "rows_done", "max_in"))
        scored, exp_done, weighed, mix_taken = (sem(n) for n in (
            "scored", "exp_done", "weighed", "mix_taken"))
        inverted, att_done, out_ready, added = sem("inverted"), sem("att_done"), sem("out_ready"), sem("added")

        block = ctx.enter_context(nc.Block())

        def wide(buf, kt, g):
            at = (kt * 2 + g) * 8 * P
            return v_wide[buf][:, at:at + 8 * (P + K0)].rearrange("p (h s) -> p h s", s=P + K0)[:, :, 0:K0]

        @block.sync
        def _(sp):
            def place_max(b):
                sp.wait_ge(rows_done, b + 1)
                for qt in range(QT):
                    sp.dma_start(q_stack[b % RING][MROW:MROW + 1, :, P * qt:P * qt + P],
                                 neg_rows[H0 * qt:H0 * qt + H0, :]).then_inc(max_in, 16)

            place_max(0)
            for b in range(B - 1):
                place_max(b + 1)
                if b + RING < B:
                    sp.wait_ge(scored, (b + 1) * NP0)
                    for name, stack in (("k", k_stack), ("q", q_stack)):
                        load_stack(sp, io, stack[b % RING], name, b + RING, loaded[b % RING])

        @block.gpsimd
        def _(pool):
            for b in range(B):
                if b < RING:
                    nc.gpsimd.memset(v_wide[b][:], 0.0).then_inc(zeroed, 1)
                    pool.wait_ge(zeroed, b + 1)
                    for half in range(2 * QT):
                        at = half * 8 * P + 64
                        ones = v_wide[b][:, at:at + 8 * (P + K0)].rearrange("p (h s) -> p h s", s=P + K0)
                        nc.gpsimd.memset(ones[:, :, 0:K0], 1.0).then_inc(ones_done, 1)
                else:
                    pool.wait_ge(weighed, NP0 * (b - RING + 1))
                for kt in range(QT):
                    for g in range(2):
                        values = v_all[:, QT * b + kt, 64 * g:64 * g + 64].rearrange("p (h j) -> p h j", j=K0)
                        nc.gpsimd.tensor_tensor(wide(b % RING, kt, g), values, bc(nothing[:], (P, 8, K0), 2), ALU.add).then_inc(v_ready, 1)

        @block.tensor
        def _(pe):
            def row_scores_of(b, par, p):
                for qt in range(QT):
                    first = isinstance(b, int) and b == 0 and p == 0
                    if not first:
                        pe.wait_ge(max_done, b * 2 * NP0 + 2 * p + qt - 1)
                    for i in range(2):
                        pe.matmul(row_scores[qt][:, i, :], q_stack[par][:, 2 * p + i, P * qt:P * qt + P],
                                  k_stack[par][:, 2 * p + i, :], start=(i == 0), stop=False, skip_group_check=True)
                    mm = pe.matmul(row_scores[qt][:], ident16[:], bias_q[:, ds(QT * b + qt, 1), :].to_broadcast((P, 2, S)),
                                   start=False, stop=True, skip_group_check=True)
                    mm.then_inc(rows_ready, 1)

            def turn_max(b):
                pe.wait_ge(neg_done, b + 1)
                if not (isinstance(b, int) and b < 2):
                    pe.wait_ge(added, b - 1)
                pe.transpose(misc[0:QT * H0, 0:P], neg_max[:], ident32[:]).then_inc(turned, 1)

            def scores_of(b, par, p):
                if not (isinstance(b, int) and b == 0 and p < 2):
                    pe.wait_ge(exp_done, b * NP0 + p - 1)
                for kt in range(QT):
                    for i in range(2):
                        pe.matmul(scores[p % 2][:, kt, i, :], k_stack[par][:, 2 * p + i, P * kt:P * kt + P],
                                  q_stack[par][:, 2 * p + i, :], start=(i == 0), stop=False, skip_group_check=True)
                    mm = pe.matmul(scores[p % 2][:, kt], ident16[:], bias_k[:, ds(QT * b + kt, 1), :].to_broadcast((P, 2, S)),
                                   start=False, stop=True, skip_group_check=True)
                mm.then_inc(scored, 1)

            def weigh(b, par, p):
                pe.wait_ge(exp_done, b * NP0 + p + 1)
                g = p // 4
                if p % 4 == 0 and not (isinstance(b, int) and b == 0 and g == 0):
                    pe.wait_ge(mix_taken, 2 * b + g)
                for i in range(2):
                    for kt in range(QT):
                        at = ((kt * 2 + g) * 8 + (2 * p + i) % 8) * P
                        mm = pe.matmul(mix[:, 0:S], v_wide[par][:, at:at + P], probs[p % 2][:, kt, i, :],
                                       start=(p % 4 == 0 and i == 0 and kt == 0), stop=(p % 4 == 3 and i == 1 and kt == 1))
                mm.then_inc(weighed, 1)

            def project(b):
                pe.wait_ge(att_done, b + 1)
                for qt in range(QT):
                    mm = pe.matmul(misc[:, P * qt:P * qt + P], attended[:, P * qt:P * qt + P], wo0[:], start=True, stop=True)
                mm.then_inc(out_ready, 1)

            def step(b, buf, turn=0, ahead=True, behind=True):
                pe.wait_ge(max_in, 16 * QT * (b + 1))
                pe.wait_ge(v_ready, 2 * QT * (b + 1))
                if isinstance(b, int) and b == 0:
                    pe.wait_ge(ones_done, 2 * QT * RING)
                after = (buf + 1) % RING
                if ahead:
                    pe.wait_ge(loaded[after], 16 * 2 * STACK_DMAS * (turn + (buf + 1) // RING + 1))
                for p in range(NP0):
                    rows = AHEAD[p] if ahead else ()
                    if rows:
                        row_scores_of(b + 1, after, rows[0])
                    scores_of(b, buf, p)
                    if rows[1:]:
                        row_scores_of(b + 1, after, rows[1])
                    if p:
                        weigh(b, buf, p - 1)
                    if p == 2 and behind:
                        pe.wait_ge(rows_done, b + 1)
                        project(b - 1)
                    if ahead and p == TURN:
                        turn_max(b + 1)
                weigh(b, buf, NP0 - 1)

            pe.wait_ge(keep["wo0_in"], 16)
            pe.wait_ge(loaded[0], 16 * 2 * STACK_DMAS)
            for p in range(NP0):
                row_scores_of(0, 0, p)
            turn_max(0)
            step(0, 0, behind=False)
            with pe.Fori(0, (B - 2) // RING) as j:
                for i in range(RING):
                    step(RING * j + i + 1, (i + 1) % RING, j + (i + 1) // RING)
            step(B - 1, (B - 1) % RING, ahead=False)
            project(B - 1)

        @block.scalar
        def _(act):
            def take_mix(b, g):
                act.wait_ge(weighed, NP0 * b + 4 * g + 4)
                if not (isinstance(b, int) and b == 0):
                    act.wait_ge(att_done, b)
                act.copy(summed[64 * g:64 * g + 64, :], mix[64:128, 0:S])
                act.copy(mixed[64 * g:64 * g + 64, :], mix[0:64, 0:S]).then_inc(mix_taken, 1)

            def take_rows(b):
                act.wait_ge(turned, b + 1)
                if not (isinstance(b, int) and b == 0):
                    act.wait_ge(max_in, 16 * QT * b)
                act.copy(neg_rows[:], misc[0:QT * H0, 0:P]).then_inc(rows_done, 1)

            def step(b, ahead=True):
                for p in range(NP0):
                    act.wait_ge(scored, b * NP0 + p + 1)
                    if not (isinstance(b, int) and b == 0 and p < 2):
                        act.wait_ge(weighed, b * NP0 + p - 1)
                    act.activation(probs[p % 2][:], scores[p % 2][:], ACT.Exp, scale=K0 ** -0.5).then_inc(exp_done, 1)
                    if p == 5:
                        take_mix(b, 0)
                    if ahead and p == TURN:
                        take_rows(b + 1)
                take_mix(b, 1)

            take_rows(0)
            step(0)
            with act.Fori(0, (B - 2) // RING) as j:
                for i in range(RING):
                    step(RING * j + i + 1)
            step(B - 1, ahead=False)

        @block.vector
        def _(dve):
            def maxima(b, p):
                for qt in range(QT):
                    dve.wait_ge(rows_ready, b * 2 * NP0 + 2 * p + qt + 1)
                    if p == 0 and qt == 0 and not (isinstance(b, int) and b == 0):
                        dve.wait_ge(neg_done, b)
                    dve.tensor_reduce(row_max[:, qt, 2 * p:2 * p + 2], row_scores[qt][:], AX.X,
                                      ALU.max).then_inc(max_done, 1)

            def negate(b):
                dve.wait_ge(max_done, (b + 1) * 2 * NP0)
                if not (isinstance(b, int) and b == 0):
                    dve.wait_ge(turned, b)
                dve.tensor_scalar(neg_max[:], row_max[:].rearrange("p a h -> p (a h)"), -1.0, None,
                                  ALU.mult).then_inc(neg_done, 1)

            def normalise(b):
                dve.wait_ge(mix_taken, 2 * (b + 1))
                dve.reciprocal(inverse[:], summed[:]).then_inc(inverted, 1)
                dve.wait_ge(inverted, b + 1)
                if not (isinstance(b, int) and b == 0):
                    dve.wait_ge(out_ready, b)
                dve.tensor_tensor(attended[:], mixed[:], inverse[:], ALU.mult).then_inc(att_done, 1)

            def add(b):
                dve.wait_ge(out_ready, b + 1)
                rows = xr[:, ds(QT * b, QT), :]
                dve.tensor_tensor(rows, misc[:, 0:S].rearrange("p (t d) -> p t d", t=QT), rows,
                                  ALU.add).then_inc(added, 1)

            def step(b, ahead=True, behind=True):
                for p in range(NP0):
                    for row in AHEAD[p] if ahead else ():
                        maxima(b + 1, row)
                    if ahead and p == LAST_ROWS:
                        negate(b + 1)
                    if p == 0 and behind:
                        normalise(b - 1)
                    if p == 3 and behind:
                        add(b - 1)

            for p in range(NP0):
                maxima(0, p)
            negate(0)
            step(0, behind=False)
            with dve.Fori(0, (B - 2) // RING) as j:
                for i in range(RING):
                    step(RING * j + i + 1)
            step(B - 1, ahead=False)
            normalise(B - 1)
            add(B - 1)


E0 = 32
I0 = 64
G0 = 8
TOPG = 4
TOPK = 6
SCALE0 = 2.5
PAIRS = E0 // 2
CH = 512
NCH = T // CH


def experts_layer0(nc, io, keep):
    with ExitStack() as ctx:
        def sb(name, shape, dt):
            return ctx.enter_context(nc.sbuf_tensor("c_" + name, shape, dt))

        def psum(name, shape, dt=F32):
            return ctx.enter_context(nc.psum_tensor("c_" + name, shape, dt))

        def sem(name):
            return ctx.enter_context(nc.semaphore("c_" + name))

        xr, nrm, ident32, ident_b = keep["xr"], keep["nrm"], keep["ident32"], keep["ident_b"]
        nothing = keep["nothing"]
        squares = sb("squares", [P, NT, D], F32)
        small = sb("small", [P, 6 * NT], F32)
        x_hi, x_lo = sb("x_hi", [P, T], F16), sb("x_lo", [P, T], F16)
        gate = sb("gate", [P, E0], F32)
        gate_hi, gate_lo = sb("gate_hi", [P, E0], F16), sb("gate_lo", [P, E0], F16)
        bias = sb("bias", [P, E0], F32)
        counting = sb("counting", [P, E0], F32)
        score = sb("score", [P, NT, E0], F32)
        choice = sb("choice", [P, NT, E0], F32)
        group = sb("group", [P, NT, G0], F32)
        top = sb("top", [P, NT, 8], F32)
        top_at = sb("top_at", [P, NT, 8], U32)
        top_atf = sb("top_atf", [P, NT, 8], F32)
        hits = sb("hits", [P, NT * E0 * TOPK], F32)
        picked_g = sb("picked_g", [P, NT, G0], F32)
        picked = sb("picked", [P, NT, E0], F32)
        combine = sb("combine", [P, NT, E0], F32)
        rest = sb("rest", [P, NT, E0], F32)
        total, scale = sb("total", [P, NT], F32), sb("scale", [P, NT], F32)
        parts = sb("parts", [P, NT, 3 * E0], BF16)
        combine_t = sb("combine_t", [3 * E0, T], BF16)
        spread = sb("spread", [3 * E0, T], F16)
        w = [sb(f"w{i}", [P, 3, P], F32) for i in range(2)]
        w_hi = [sb(f"w_hi{i}", [P, 2, P], F16) for i in range(2)]
        w_lo = [sb(f"w_lo{i}", [P, 2, P], F16) for i in range(2)]
        gated = [sb(f"gated{i}", [P, CH], F32) for i in range(2)]
        upped = [sb(f"upped{i}", [P, CH], F32) for i in range(2)]
        hidden = [sb(f"hidden{i}", [P, CH], F32) for i in range(2)]
        y_t = sb("y_t", [P, T], F32)

        acc = psum("acc", [P, T])
        gate_ps, up_ps, weight_ps, misc = (psum(n, [P, CH]) for n in ("gate_ps", "up_ps", "weight_ps", "misc"))
        ring = [gate_ps, up_ps, weight_ps, misc]

        w_in = [sem(f"w_in{i}") for i in range(2)]
        gate_in, bias_in, spread_in = sem("gate_in"), sem("bias_in"), sem("spread_in")
        centred, squared, var_done, root_done = keep["norm_sems"]
        steps, norm_done, turned, hi_done, lo_done = (sem(n) for n in ("steps", "norm_done", "turned", "hi_done", "lo_done"))
        gate_split, logits_done, scored, parts_done, parts_turned, parts_taken = (sem(n) for n in (
            "gate_split", "logits_done", "scored", "parts_done", "parts_turned", "parts_taken"))
        w_split, w_lo_done = sem("w_split"), sem("w_lo_done")
        gate_ready, up_ready, weight_ready, gate_taken, up_taken, hidden_done, down_done = (sem(n) for n in (
            "gate_ready", "up_ready", "weight_ready", "gate_taken", "up_taken", "hidden_done", "down_done"))
        y_taken, y_turned, y_added = sem("y_taken"), sem("y_turned"), sem("y_added")

        block = ctx.enter_context(nc.Block())

        @block.sync
        def _(sp):
            sp.dma_start(gate[:], io["gate0"]).then_inc(gate_in, 16)
            sp.dma_start(bias[:], io["bias0"].partition_broadcast(P)).then_inc(bias_in, 16)
            sp.dma_start(counting[:], io["counting"].partition_broadcast(P)).then_inc(bias_in, 16)
            sp.dma_start(spread[:], io["spread0"]).then_inc(spread_in, 16)

            def load(k, par):
                sp.dma_start(w[par][:], io["w0"].rearrange("k p a d -> k p (a d)")[ds(k, 1)].rearrange("k p c -> p (k c)")
                             ).then_inc(w_in[par], 16)

            load(0, 0)
            load(1, 1)
            with sp.Fori(0, PAIRS // 2 - 1) as j:
                sp.wait_ge(down_done, NCH * (2 * j + 1))
                load(2 * j + 2, 0)
                sp.wait_ge(down_done, NCH * (2 * j + 2))
                load(2 * j + 3, 1)
            sp.wait_ge(down_done, NCH * (PAIRS - 1))
            load(PAIRS, 0)

        @block.gpsimd
        def _(pool):
            def split(j, k, par):
                pool.wait_ge(w_in[par], 16 * (j + 1))
                if not (isinstance(k, int) and k < 2):
                    pool.wait_ge(down_done, NCH * (k - 1))
                nc.gpsimd.tensor_tensor(w_hi[par][:], w[par][:, 0:2, :], bc(nothing[:, 0:2], (P, 2, P), 2), ALU.add).then_inc(w_split, 1)
                pool.wait_ge(w_split, k + 1)
                nc.gpsimd.tensor_tensor(w_lo[par][:], w[par][:, 0:2, :], w_hi[par][:], ALU.subtract).then_inc(w_lo_done, 1)

            split(0, 0, 0)
            split(0, 1, 1)
            with pool.Fori(1, PAIRS // 2) as j:
                split(j, 2 * j, 0)
                split(j, 2 * j + 1, 1)
            split(PAIRS // 2, PAIRS, 0)

        @block.tensor
        def _(pe):
            def three(out, a_hi, a_lo, b_hi, b_lo):
                pe.matmul(out, a_hi, b_hi, start=True, stop=False)
                pe.matmul(out, a_lo, b_hi, start=False, stop=False)
                return pe.matmul(out, a_hi, b_lo, start=False, stop=True)

            pe.wait_ge(norm_done, 1)
            for g in range(4):
                for i in range(4):
                    mm = pe.transpose(ring[g][:, P * i:P * i + P], nrm[:, 4 * g + i, :], ident32[:])
                mm.then_inc(turned, 1)
            pe.wait_ge(gate_split, 2)
            pe.wait_ge(lo_done, 4)
            for t in range(NT):
                cols = slice(P * t, P * t + P)
                mm = three(misc[:, E0 * t:E0 * t + E0], x_hi[:, cols], x_lo[:, cols], gate_hi[:], gate_lo[:])
            mm.then_inc(logits_done, 1)

            def down(k, par, c):
                n = NCH * k + c
                pe.wait_ge(hidden_done, n + 1)
                first = isinstance(k, int) and k == 0
                last = isinstance(k, int) and k == PAIRS
                pe.matmul(acc[:, CH * c:CH * c + CH], w[par][:, 2, :], hidden[c % 2][:], start=first, stop=last).then_inc(down_done, 1)

            def chunk(k, par, c, routed=True):
                n = NCH * k + c
                cols = slice(CH * c, CH * c + CH)
                first = isinstance(k, int) and k == 0 and c == 0
                if not first:
                    pe.wait_ge(gate_taken, n)
                three(gate_ps[:], w_hi[par][:, 0, :], w_lo[par][:, 0, :], x_hi[:, cols], x_lo[:, cols]).then_inc(gate_ready, 1)
                if routed:
                    pe.wait_ge(hidden_done, n)
                    pe.matmul(weight_ps[:], spread[:, ds(P * (k - 1), P)], combine_t[:, cols], start=True, stop=True).then_inc(weight_ready, 1)
                if not first:
                    pe.wait_ge(up_taken, n)
                three(up_ps[:], w_hi[par][:, 1, :], w_lo[par][:, 1, :], x_hi[:, cols], x_lo[:, cols]).then_inc(up_ready, 1)

            def pair(j, k, par, routed=True):
                pe.wait_ge(w_lo_done, k + 1)
                for c in range(NCH):
                    chunk(k, par, c, routed)
                    if c:
                        down(k, par, c - 1)
                    elif not (isinstance(k, int) and k == 0):
                        down(k - 1, 1 - par, NCH - 1)

            pair(0, 0, 0, routed=False)
            pe.wait_ge(parts_done, 1)
            pe.wait_ge(scored, 1)
            for g in range(2):
                for i in range(8):
                    mm = pe.transpose(misc[:].bitcast(BF16)[0:3 * E0, P * i:P * i + P], parts[:, 8 * g + i, :], ident_b[:])
                mm.then_inc(parts_turned, 1)
                pe.wait_ge(parts_taken, g + 1)
            pe.wait_ge(spread_in, 16)
            pair(0, 1, 1)
            with pe.Fori(1, PAIRS // 2) as j:
                pair(j, 2 * j, 0)
                pair(j, 2 * j + 1, 1)
            pair(PAIRS // 2, PAIRS, 0)
            down(PAIRS, 0, NCH - 1)
            for g in range(4):
                pe.wait_ge(y_taken, g + 1)
                for i in range(4):
                    t = 4 * g + i
                    mm = pe.transpose(ring[g][:, P * i:P * i + P], y_t[:, P * t:P * t + P], ident32[:])
                mm.then_inc(y_turned, 1)

        @block.scalar
        def _(act):
            layer_norm_all_act(act, centred, squared, var_done, root_done, nrm, squares, small, 2)
            for g in range(4):
                act.wait_ge(turned, g + 1)
                act.copy(x_hi[:, CH * g:CH * g + CH], ring[g][:]).then_inc(hi_done, 1)
            act.wait_ge(logits_done, 1)
            act.activation(score[:].rearrange("p t e -> p (t e)"), misc[:], ACT.Sigmoid).then_inc(scored, 1)

            def silus(k):
                for c in range(NCH):
                    n = NCH * k + c
                    act.wait_ge(gate_ready, n + 1)
                    if not (isinstance(k, int) and k == 0 and c < 2):
                        act.wait_ge(up_taken, n - 1)
                    act.activation(gated[c % 2][:], gate_ps[:], ACT.Silu).then_inc(gate_taken, 1)

            silus(0)
            with act.Fori(1, PAIRS + 1) as k:
                silus(k)
            act.wait_ge(down_done, NCH * (PAIRS + 1))
            for g in range(4):
                act.copy(y_t[:, CH * g:CH * g + CH], acc[:, CH * g:CH * g + CH]).then_inc(y_taken, 1)

        @block.vector
        def _(dve):
            chain = Chain(dve, steps)
            inv = layer_norm_all(dve, chain, centred, squared, var_done, root_done, xr, nrm, squares, small, 2)
            dve.tensor_tensor(nrm[:], nrm[:], bc(inv, (P, NT, D), 2), ALU.mult).then_inc(norm_done, 1)
            dve.wait_ge(gate_in, 16)
            dve.tensor_copy(gate_hi[:], gate[:]).then_inc(gate_split, 1)
            dve.wait_ge(gate_split, 1)
            dve.tensor_tensor(gate_lo[:], gate[:], gate_hi[:], ALU.subtract).then_inc(gate_split, 1)
            for g in range(4):
                cols = slice(CH * g, CH * g + CH)
                dve.wait_ge(hi_done, g + 1)
                dve.tensor_tensor(x_lo[:, cols], ring[g][:], x_hi[:, cols], ALU.subtract).then_inc(lo_done, 1)

            def hiddens(k, routed=True):
                for c in range(NCH):
                    n = NCH * k + c
                    dve.wait_ge(gate_taken, n + 1)
                    dve.wait_ge(up_ready, n + 1)
                    dve.tensor_tensor(upped[c % 2][:], up_ps[:], gated[c % 2][:], ALU.mult).then_inc(up_taken, 1)
                    dve.wait_ge(up_taken, n + 1)
                    if not (isinstance(k, int) and k == 0 and c < 2):
                        dve.wait_ge(down_done, n - 1)
                    if routed:
                        dve.wait_ge(weight_ready, n - NCH + 1)
                        dve.tensor_tensor(hidden[c % 2][:], weight_ps[:], upped[c % 2][:], ALU.mult).then_inc(hidden_done, 1)
                    else:
                        dve.tensor_copy(hidden[c % 2][:], upped[c % 2][:]).then_inc(hidden_done, 1)

            dve.wait_ge(bias_in, 32)
            dve.wait_ge(scored, 1)
            chain.then(dve.tensor_tensor(choice[:], score[:], bc(bias[:], (P, NT, E0), 1), ALU.add))
            hiddens(0, routed=False)
            chain.then(dve.tensor_reduce(group[:].rearrange("p t g -> p (t g)"),
                                         choice[:].rearrange("p t (g e) -> p (t g) e", g=G0), AX.X, ALU.max))

            def pick(values, n, count, out):
                for t in range(NT):
                    ins = dve.max(top[:, t, :], values[:, t, :])
                chain.then(ins)
                for t in range(NT):
                    ins = dve.max_index(top_at[:, t, :], top[:, t, :], values[:, t, :])
                chain.then(ins)
                chain.then(dve.tensor_copy(top_atf[:], top_at[:]))
                hit = hits[:, 0:NT * n * count].rearrange("p (t e k) -> p t e k", t=NT, e=n)
                places = top_atf[:, :, 0:count].unsqueeze(2).to_broadcast((P, NT, n, count))
                numbers = counting[:, 0:n].unsqueeze(1).unsqueeze(3).to_broadcast((P, NT, n, count))
                chain.then(dve.tensor_tensor(hit, numbers, places, ALU.is_equal))
                chain.then(dve.tensor_reduce(out[:].rearrange("p t e -> p (t e)"),
                                             hits[:, 0:NT * n * count].rearrange("p (m k) -> p m k", k=count), AX.X, ALU.add))

            pick(group, G0, TOPG, picked_g)
            per = E0 // G0
            chain.then(dve.tensor_tensor(choice[:].rearrange("p t (g e) -> p t g e", g=G0),
                                         choice[:].rearrange("p t (g e) -> p t g e", g=G0),
                                         picked_g[:].unsqueeze(3).to_broadcast((P, NT, G0, per)), ALU.mult))
            pick(choice, E0, TOPK, picked)
            chain.then(dve.tensor_tensor(combine[:], score[:], picked[:], ALU.mult))
            chain.then(dve.tensor_reduce(total[:], combine[:], AX.X, ALU.add))
            chain.then(dve.tensor_scalar(total[:], total[:], 1e-20, None, ALU.add))
            chain.then(dve.reciprocal(scale[:], total[:]))
            chain.then(dve.tensor_scalar(scale[:], scale[:], SCALE0, None, ALU.mult))
            chain.then(dve.tensor_tensor(combine[:], combine[:], bc(scale[:], (P, NT, E0), 2), ALU.mult))
            chain.then(dve.tensor_copy(parts[:, :, 0:E0], combine[:]))
            chain.then(dve.tensor_tensor(rest[:], combine[:], parts[:, :, 0:E0], ALU.subtract))
            chain.then(dve.tensor_copy(parts[:, :, E0:2 * E0], rest[:]))
            dve.tensor_tensor(parts[:, :, 2 * E0:3 * E0], rest[:], parts[:, :, E0:2 * E0], ALU.subtract).then_inc(parts_done, 1)
            for g in range(2):
                dve.wait_ge(parts_turned, g + 1)
                dve.tensor_copy(combine_t[:, 8 * P * g:8 * P * g + 8 * P], misc[:].bitcast(BF16)[0:3 * E0, :]).then_inc(parts_taken, 1)
            with dve.Fori(1, PAIRS + 1) as k:
                hiddens(k)
            for g in range(4):
                dve.wait_ge(y_turned, g + 1)
                rows = xr[:, 4 * g:4 * g + 4, :]
                dve.tensor_tensor(rows, ring[g][:].rearrange("p (t d) -> p t d", t=4), rows, ALU.add).then_inc(y_added, 1)


H1 = 16
D1 = 64
HU = H1 // 2
PU = HU // 2
NK1 = 2 * S
KT = NK1 // P
MASK1 = D1
MROW1 = 96


def prepare_layer1(nc, io, keep):
    with ExitStack() as ctx:
        def sb(name, shape, dt):
            return ctx.enter_context(nc.sbuf_tensor("d_" + name, shape, dt))

        def sem(name):
            return ctx.enter_context(nc.semaphore("d_" + name))

        xr, nrm, ident32 = keep["xr"], keep["nrm"], keep["ident32"]
        wq_hi, wq_lo, wkv_hi, wkv_lo = (keep[n] for n in ("wq_hi", "wq_lo", "wkv_hi", "wkv_lo"))
        squares = sb("squares", [P, NT, D], F32)
        small = sb("small", [P, 4 * NT], F32)
        ctx_rows = sb("ctx_rows", [P, NT, D], F32)
        ctx_nrm = sb("ctx_nrm", [P, NT, D], F32)
        lat_nrm = sb("lat_nrm", [P, NT, D], F32)
        wq, wkv = sb("wq", [P, H1 * D1], F32), sb("wkv", [P, 2 * H1 * D1], F32)
        norm_w = sb("norm_w", [P, 4], F32)
        q_gain, k_gain = sb("q_gain", [P, D1], F32), sb("k_gain", [P, D1], F32)
        bout = sb("bout", [P, D], F32)
        mask8 = sb("mask8", [B, S], U8)
        mask_bias = sb("mask_bias", [B, S], F16)
        turned = [sb(f"turned{i}", [P, 512], F32) for i in range(2)]
        banks = [ctx.enter_context(nc.psum_tensor(f"d_bank{i}", [P, 512], F32)) for i in range(4)]

        ctx_in, small_in, wq_in, wkv_in, mask_in, mask_out = (sem(n) for n in ("ctx_in", "small_in", "wq_in", "wkv_in", "mask_in", "mask_out"))
        centred, squared, var_done, root_done = keep["norm_sems"]
        steps, ctx_done, lat_done, w_hi_done, mask_done = (sem(n) for n in ("steps", "ctx_done", "lat_done", "w_hi_done", "mask_done"))
        bank_ready, bank_taken, hi_done, lo_done = (sem(n) for n in ("bank_ready", "bank_taken", "hi_done", "lo_done"))

        block = ctx.enter_context(nc.Block())

        @block.sync
        def _(sp):
            sp.dma_start(ctx_rows[:], io["ctx_rows"]).then_inc(ctx_in, 16)
            sp.dma_start(norm_w[:], io["norm_w"]).then_inc(small_in, 16)
            sp.dma_start(q_gain[:], io["q_gain"].partition_broadcast(P)).then_inc(small_in, 16)
            sp.dma_start(k_gain[:], io["k_gain"].partition_broadcast(P)).then_inc(small_in, 16)
            sp.dma_start(bout[:], io["bout"].partition_broadcast(P)).then_inc(small_in, 16)
            sp.dma_start(mask8[:], io["mask8"]).then_inc(mask_in, 16)
            sp.dma_start(wq[:], io["wq1"]).then_inc(wq_in, 16)
            sp.dma_start(wkv[:], io["wkv1"]).then_inc(wkv_in, 16)
            sp.dma_start(keep["wout"][:], io["wout"]).then_inc(keep["wout_in"], 16)
            sp.wait_ge(mask_done, 1)
            sp.dma_start(io["mask_bias"], mask_bias[:]).then_inc(mask_out, 16)
            sp.wait_ge(mask_out, 16)

        @block.gpsimd
        def _(pool):
            pool.wait_ge(mask_in, 16)
            nc.gpsimd.tensor_scalar(mask_bias[:], mask8[:], 0.0, MASKED, ALU.is_equal, ALU.mult).then_inc(mask_done, 1)
            pool.wait_ge(w_hi_done, 1)
            nc.gpsimd.tensor_tensor(wq_lo[:], wq[:], wq_hi[:], ALU.subtract).then_inc(mask_done, 1)
            pool.wait_ge(w_hi_done, 2)
            nc.gpsimd.tensor_tensor(wkv_lo[:], wkv[:], wkv_hi[:], ALU.subtract).then_inc(mask_done, 1)
            pool.wait_ge(mask_done, 3)

        @block.scalar
        def _(act):
            layer_norm_all_act(act, centred, squared, var_done, root_done, ctx_nrm, squares, small, 3)
            act.wait_ge(wq_in, 16)
            act.copy(wq_hi[:], wq[:]).then_inc(w_hi_done, 1)
            act.wait_ge(wkv_in, 16)
            act.copy(wkv_hi[:], wkv[:]).then_inc(w_hi_done, 1)
            layer_norm_all_act(act, centred, squared, var_done, root_done, nrm, squares, small, 4)
            layer_norm_all_act(act, centred, squared, var_done, root_done, lat_nrm, squares, small, 5)
            for n in range(8):
                hi = keep["ctx_hi"] if n < 4 else keep["lat_hi"]
                act.wait_ge(bank_taken, n + 1)
                act.copy(hi[:, 512 * (n % 4):512 * (n % 4) + 512], turned[n % 2][:]).then_inc(hi_done, 1)

        @block.tensor
        def _(pe):
            for n in range(8):
                pe.wait_ge(ctx_done if n < 4 else lat_done, 1)
                if n >= 4:
                    pe.wait_ge(bank_taken, n - 3)
                rows = ctx_nrm if n < 4 else lat_nrm
                for i in range(4):
                    mm = pe.transpose(banks[n % 4][:, P * i:P * i + P], rows[:, 4 * (n % 4) + i, :], ident32[:])
                mm.then_inc(bank_ready, 1)

        @block.vector
        def _(dve):
            chain = Chain(dve, steps)
            dve.wait_ge(ctx_in, 16)
            inv = layer_norm_all(dve, chain, centred, squared, var_done, root_done, ctx_rows, ctx_nrm, squares, small, 3)
            dve.tensor_tensor(ctx_nrm[:], ctx_nrm[:], bc(inv, (P, NT, D), 2), ALU.mult).then_inc(ctx_done, 1)
            inv = layer_norm_all(dve, chain, centred, squared, var_done, root_done, xr, nrm, squares, small, 4)
            chain.then(dve.tensor_tensor(nrm[:], nrm[:], bc(inv, (P, NT, D), 2), ALU.mult))
            dve.wait_ge(small_in, 64)
            chain.then(dve.tensor_tensor(xr[:], xr[:], bc(bout[:], (P, NT, D), 1), ALU.add))
            inv = layer_norm_all(dve, chain, centred, squared, var_done, root_done, nrm, lat_nrm, squares, small, 5)
            dve.tensor_tensor(lat_nrm[:], lat_nrm[:], bc(inv, (P, NT, D), 2), ALU.mult).then_inc(lat_done, 1)
            chain.then(dve.tensor_tensor(keep["qk_gain"][:], q_gain[:], k_gain[:], ALU.mult))
            chain.then(dve.tensor_scalar(keep["qk_gain"][:], keep["qk_gain"][:], D1 ** -0.5, None, ALU.mult))

            def take(n):
                at = 0 if n < 4 else 2
                dve.wait_ge(bank_ready, n + 1)
                if n >= 2:
                    dve.wait_ge(hi_done, n - 1)
                    dve.wait_ge(lo_done, n - 1)
                dve.tensor_scalar(turned[n % 2][:], banks[n % 4][:], norm_w[:, at:at + 1], norm_w[:, at + 1:at + 2],
                                  ALU.mult, ALU.add).then_inc(bank_taken, 1)

            def low(n):
                hi, lo = (keep["ctx_hi"], keep["ctx_lo"]) if n < 4 else (keep["lat_hi"], keep["lat_lo"])
                cols = slice(512 * (n % 4), 512 * (n % 4) + 512)
                dve.wait_ge(hi_done, n + 1)
                dve.tensor_tensor(lo[:, cols], turned[n % 2][:], hi[:, cols], ALU.subtract).then_inc(lo_done, 1)

            take(0)
            for n in range(8):
                if n < 7:
                    take(n + 1)
                low(n)


JOBS = [[("q", t) for t in range(QT)] + [("v", t) for t in range(3)],
        [("v", t) for t in range(3, KT)] + [("tk", t) for t in range(2)],
        [("tk", t) for t in range(2, KT)] + [("tq", t) for t in range(QT)],
        [("k", t) for t in range(KT)]]
SPLITS = [[("root",)], [("split", j) for j in range(4)], [("split", j) for j in range(4, 6)], []]
ROOT_AT = 12
NEWTON = 3
RSQRT_BITS = float(0x5f3759df)
M_AT = 2


def plan_step(s, first, last):
    p = s % PU
    prepare = not (last and s >= PU)
    ahead = not (last and s == 2 * PU - 1)
    rows = [("r", i, qt) for i in range(2) for qt in range(QT)] + [("neg",)] if ahead else []
    before = [] if first and s == 0 else [("w", -1, kt) for kt in range(KT)]
    jobs = JOBS[p] if (not last if p == PU - 1 else prepare) else []
    if s == 1 and not first:
        jobs = [("o",)] + jobs
    head = [("s", 0, 0), ("s", 0, 1)]
    values = [("w", 0, kt) for kt in range(KT)]
    tail = [("s", 1, 0), ("s", 1, 1)] + (values[:M_AT] + [("m",)] + values[M_AT:] if ahead else values)
    if p == PU - 1:
        atoms = head + before[:2] + rows[:2] + before[2:] + rows[2:3] + tail[:1] + rows[3:] + tail[1:]
    else:
        atoms = rows[:2] + before + head[:1] + rows[2:] + head[1:] + tail
    out, done = [], 0
    for n, atom in enumerate(atoms):
        out.append(atom)
        due = (n + 1) * len(jobs) // len(atoms)
        while done < due:
            out.append(jobs[done])
            done += 1
    out += jobs[done:]
    if prepare:
        for n, event in enumerate(SPLITS[p]):
            out.insert(ROOT_AT if p == 0 and n == 0 else n * len(out) // len(SPLITS[p]), event)
    return out


MISC = ("k", "q", "v", "tk", "tq", "o", "m")
START = [("k", t) for t in range(KT)] + [("q", t) for t in range(QT)] + [("root",)] + [("v", t) for t in range(KT)] \
    + [("split", j) for j in range(6)] + [("tk", t) for t in range(KT)] + [("tq", t) for t in range(QT)] \
    + [("r", i, qt) for i in range(2) for qt in range(QT)] + [("neg",), ("m",)] + [("k", t) for t in range(KT)]


def number(events, bank, counts):
    counts, out = list(counts), []
    for event in events:
        out.append((event, (bank, counts[bank])))
        if event[0] in MISC:
            counts[bank] = counts[bank] + 1
            bank = 1 - bank
    return out, bank, counts


def steps_of(first, last):
    return [plan_step(s, first, last) for s in range(2 * PU)]


def totals(events, bank):
    return number(events, bank, (0, 0))[2]


def after_max(events, bank):
    numbered, _, counts = number(events, bank, (0, 0))
    at, n = next(use for event, use in numbered if event[0] == "m")
    return at, counts[at] - n


FIRST_BANK = 1


class Batch:

    def __init__(self, b, first=False, last=False):
        self.b, self.first, self.last = b, first, last
        self.bank = FIRST_BANK if first else 0
        start = totals(START, 0)
        if first:
            self.counts = start
        else:
            one = totals(sum(steps_of(True, False), []), FIRST_BANK)
            whole = totals(sum(steps_of(False, False), []), 0)
            self.counts = [start[i] + one[i] - whole[i] + whole[i] * b for i in range(2)]

    def steps(self):
        bank, counts = self.bank, self.counts
        if self.first:
            at, back = after_max(START, 0)
        else:
            before = steps_of(False, False)
            bank7 = number(sum(before[:-1], []), 0, (0, 0))[1]
            at, back = after_max(before[-1], bank7)
        for s, events in enumerate(steps_of(self.first, self.last)):
            maxima = at, counts[at] - back
            if events.count(("m",)):
                at, back = after_max(events, bank)
            start = counts
            events, bank, counts = number(events, bank, counts)
            yield s, events, start, maxima
        self.end = bank, counts[bank]


def attend_layer1(nc, io, keep):
    with ExitStack() as ctx:
        def sb(name, shape, dt):
            return ctx.enter_context(nc.sbuf_tensor("e_" + name, shape, dt))

        def psum(name, shape):
            return ctx.enter_context(nc.psum_tensor("e_" + name, shape, F32))

        def sem(name):
            return ctx.enter_context(nc.semaphore("e_" + name))

        xr, ident32, ident16 = keep["xr"], keep["ident32"], keep["ident16"]
        q_stack = [sb(f"q_stack{i}", [P, HU, S], F16) for i in range(2)]
        k_stack = [sb(f"k_stack{i}", [P, HU, NK1], F16) for i in range(2)]
        q_high = [sb(f"q_high{i}", [P, HU, S], F16) for i in range(2)]
        k_high = [sb(f"k_high{i}", [P, HU, NK1], F16) for i in range(2)]
        v_ones = [sb(f"v_ones{i}", [P, KT, HU, P], F32) for i in range(2)]
        raw = sb("raw", [P, 6, HU, D1], F32)
        squares = [sb(f"squares{i}", [P, HU, D1], F32) for i in range(2)]
        sum_sq = sb("sum_sq", [P, 6 * HU], F32)
        inv, mean_sq, newton = (sb(n, [P, 6 * HU], F32) for n in ("inv", "mean_sq", "newton"))
        halved = sb("halved", [P, 6 * HU], I32)
        natural = sb("natural", [P, 6, HU, P], F16)
        probs = [sb(f"probs{i}", [P, KT, S], F32) for i in range(2)]
        row_max = sb("row_max", [P, 2, QT], F32)
        neg_max = sb("neg_max", [P, 2 * QT, P], F16)
        mixed = [sb(f"mixed{i}", [P, S], F32) for i in range(2)]
        summed = [sb(f"summed{i}", [P, S], F32) for i in range(2)]
        inverse = sb("inverse", [P, S], F32)
        attended = sb("attended", [P, H1 // 2, S], F32)

        row_scores = [psum(f"row_scores{i}", [P, NK1]) for i in range(QT)]
        scores = [psum(f"scores{i}", [P, 2, S]) for i in range(3)]
        mix = psum("mix", [P, 512])
        misc = [psum(f"misc{i}", [P, 512]) for i in range(2)]

        cleared, fixed = sem("cleared"), sem("fixed")
        misc_ready, misc_taken = [sem(f"misc_ready{i}") for i in range(2)], [sem(f"misc_taken{i}") for i in range(2)]
        squared, summed_sq, inv_steps, inv_done, normed, gained, hi_done, lo_done = (sem(n) for n in (
            "squared", "summed_sq", "inv_steps", "inv_done", "normed", "gained", "hi_done", "lo_done"))
        mask_in = [sem(f"mask_in{i}") for i in range(2)]
        rows_ready, max_done, neg_done, high_done = (sem(n) for n in ("rows_ready", "max_done", "neg_done", "high_done"))
        scored, exp_done, weighed, mix_taken, inverted, att_done = (sem(n) for n in (
            "scored", "exp_done", "weighed", "mix_taken", "inverted", "att_done"))
        UB = 2

        block = ctx.enter_context(nc.Block())

        def flow(engine, program):
            program(Batch(0, first=True))
            with engine.Fori(1, B - 1) as b:
                program(Batch(b))
            program(Batch(B - 1, last=True))

        @block.sync
        def _(sp):
            sp.wait_ge(cleared, 7)
            for par in range(2):
                sp.dma_start(k_high[par][MROW1:MROW1 + 1, :, :],
                             io["ones"].rearrange("o (h a) s -> o h (a s)", a=2)).then_inc(fixed, 16)
                sp.dma_start(q_high[par][MASK1:MASK1 + 1, :, :], io["ones"][:, 0:HU, :]).then_inc(fixed, 16)

            def masks(b):
                for par in range(UB):
                    if not (isinstance(b, int) and b == 0):
                        sp.wait_ge(scored, 2 * HU * (UB * b + par - 1))
                    mask = io["mask_bias"][ds(b, 1), :].unsqueeze(1)
                    for half in range(2):
                        sp.dma_start(k_high[par][MASK1:MASK1 + 1, HU // 2 * half:HU // 2 * half + HU // 2, 0:S],
                                     mask.to_broadcast((1, HU // 2, S))).then_inc(mask_in[par], 16)

            masks(0)
            with sp.Fori(1, B) as b:
                masks(b)

        @block.gpsimd
        def _(pool):
            for par in range(2):
                nc.gpsimd.memset(q_high[par][:].bitcast(F32), 0.0).then_inc(cleared, 1)
                nc.gpsimd.memset(k_high[par][:].bitcast(F32), 0.0).then_inc(cleared, 1)
            nc.gpsimd.memset(neg_max[:].bitcast(F32), 0.0).then_inc(cleared, 1)

            def unit(u):
                def norm(j):
                    pool.wait_ge(inv_done, u + 1)
                    nc.gpsimd.tensor_tensor(raw[:, j], raw[:, j], bc(inv[:, HU * j:HU * j + HU], (P, HU, D1), 2),
                                            ALU.mult).then_inc(normed, 1)

                def low(j):
                    at = slice(D1, P) if j < KT else slice(0, D1)
                    hi = slice(0, D1) if j < KT else slice(D1, P)
                    pool.wait_ge(hi_done, 6 * u + j + 1)
                    nc.gpsimd.tensor_tensor(natural[:, j, :, at], raw[:, j], natural[:, j, :, hi],
                                            ALU.subtract).then_inc(lo_done, 1)

                norm(0)
                for j in range(1, 6):
                    norm(j)
                    low(j - 1)
                low(5)

            with pool.Fori(0, UB * B) as u:
                unit(u)

        @block.tensor
        def _(pe):
            def three(out, a_hi, a_lo, b_hi, b_lo):
                pe.matmul(out, a_hi, b_hi, start=True, stop=False)
                pe.matmul(out, a_lo, b_hi, start=False, stop=False)
                return pe.matmul(out, a_hi, b_lo, start=False, stop=True)

            def emptied(use):
                bank, n = use
                if not (isinstance(n, int) and n == 0):
                    pe.wait_ge(misc_taken[bank], n)
                return misc[bank], misc_ready[bank]

            def shared(event, use, b, hf):
                name, *rest = event
                bank, ready = emptied(use)
                if name in ("k", "v", "q"):
                    t = rest[0]
                    of_ctx = name != "q" and t < QT
                    hi, lo = (keep["ctx_hi"], keep["ctx_lo"]) if of_ctx else (keep["lat_hi"], keep["lat_lo"])
                    at = ds(S * b + P * (t % QT), P)
                    w = ("wq_hi", "wq_lo") if name == "q" else ("wkv_hi", "wkv_lo")
                    col = (H1 * D1 if name == "v" else 0) + HU * D1 * hf
                    cols = slice(col, col + HU * D1)
                    three(bank[:], hi[:, at], lo[:, at], keep[w[0]][:, cols], keep[w[1]][:, cols]).then_inc(ready, 1)

            def turn(j, use, u):
                bank, ready = emptied(use)
                pe.wait_ge(lo_done, 6 * u + j + 1)
                for h in range(HU):
                    mm = pe.transpose(bank[:].bitcast(F16)[:, P * h:P * h + P], natural[:, j, h, :], ident16[:])
                mm.then_inc(ready, 1)

            def turn_max(use, q):
                bank, ready = emptied(use)
                pe.wait_ge(neg_done, q + 1)
                for i in range(2 * QT):
                    mm = pe.matmul(bank[:, P * i:P * i + P], neg_max[:, i, :], ident16[:], start=True, stop=True)
                mm.then_inc(ready, 1)

            def rows(q, par, p, i, qt):
                if not (isinstance(q, int) and q == 0 and i == 0):
                    pe.wait_ge(max_done, 4 * q + 2 * i + qt - 1)
                h = 2 * p + i
                pe.matmul(row_scores[qt][:], q_high[par][0:MASK1 + 1, h, P * qt:P * qt + P], k_high[par][0:MASK1 + 1, h, :],
                          start=True, stop=True).then_inc(rows_ready, 1)

            pe.wait_ge(keep["wout_in"], 16)
            for n, (e, use) in enumerate(number(START, 0, (0, 0))[0]):
                if e[0] in ("k", "q", "v"):
                    shared(e, use, 0, int(n > START.index(("m",))))
                elif e[0] in ("tk", "tq"):
                    turn(e[1] + (KT if e[0] == "tq" else 0), use, 0)
                elif e[0] == "r":
                    if e[1:] == (0, 0):
                        pe.wait_ge(high_done, 6)
                        pe.wait_ge(mask_in[0], 32)
                        pe.wait_ge(fixed, 64)
                    rows(0, 0, 0, *e[1:])
                elif e[0] == "m":
                    turn_max(use, 0)

            def batch(bt):
                b = bt.b
                for s, events, _, maxima in bt.steps():
                    hf, p = s // PU, s % PU
                    q = 2 * PU * b + s
                    for event, use in events:
                        name, *rest = event
                        if name == "k":
                            shared(event, use, b + 1, hf)
                        elif name in ("q", "v"):
                            shared(event, use, b + hf, 1 - hf)
                        elif name in ("tk", "tq"):
                            turn(rest[0] + (KT if name == "tq" else 0), use, UB * b + hf + 1)
                        elif name == "m":
                            turn_max(use, q + 1)
                        elif name == "o":
                            project(b, use)
                        elif name == "r":
                            par = hf if p < PU - 1 else 1 - hf
                            if p == PU - 1 and tuple(rest) == (0, 0):
                                pe.wait_ge(high_done, 6 * (UB * b + hf + 2))
                                pe.wait_ge(mask_in[par], 32 * (b + 1 if par else b + 2))
                            rows(q + 1, par, (p + 1) % PU, *rest)
                        elif name == "s":
                            i, half = rest
                            h = 2 * p + i
                            if i == 0 and half == 0:
                                pe.wait_ge(misc_taken[maxima[0]], maxima[1] + 1)
                                if not (bt.first and s == 0):
                                    pe.wait_ge(exp_done, 4 * q)
                            if i == 1 and half == 1:
                                pe.wait_ge(exp_done, 4 * q + 1)
                            for kt in range(2):
                                out = scores[(2 * i + half) % 3][:, kt, :]
                                cols = slice(P * (2 * half + kt), P * (2 * half + kt) + P)
                                pe.matmul(out, k_stack[hf][:, h, cols], q_stack[hf][:, h, :], start=True, stop=False)
                                mm = pe.matmul(out, k_high[hf][:, h, cols], q_high[hf][:, h, :], start=False, stop=True)
                            mm.then_inc(scored, 1)
                        elif name == "w":
                            weigh(2 * q + rest[0], (hf if rest[0] == 0 or p else 1 - hf), (2 * p + rest[0]) % HU, rest[0] % 2, rest[1])

            def weigh(g, par, h, buf, kt):
                if kt % 2 == 0:
                    pe.wait_ge(exp_done, 2 * g + kt // 2 + 1)
                if kt == 0:
                    if not (isinstance(g, int) and g == 0):
                        pe.wait_ge(mix_taken, g)
                mm = pe.matmul(mix[:, 0:S], v_ones[par][:, kt, h, :], probs[buf][:, kt, :], start=(kt == 0), stop=(kt == KT - 1))
                if kt == KT - 1:
                    mm.then_inc(weighed, 1)

            def project(b, use):
                bank, ready = emptied(use)
                pe.wait_ge(att_done, H1 // 2 * b)
                for qt in range(QT):
                    for pair in range(H1 // 2):
                        mm = pe.matmul(bank[:, P * qt:P * qt + P], attended[:, pair, P * qt:P * qt + P], keep["wout"][:, pair, :],
                                       start=(pair == 0), stop=(pair == H1 // 2 - 1))
                mm.then_inc(ready, 1)

            flow(pe, batch)
            for kt in range(KT):
                weigh(H1 * B - 1, 1, HU - 1, 1, kt)
            project(B, FINAL_USE)

        @block.scalar
        def _(act):
            def filled(use):
                bank, n = use
                act.wait_ge(misc_ready[bank], n + 1)
                return misc[bank], misc_taken[bank]

            def shared(event, use, par, u):
                name, *rest = event
                bank, taken = filled(use)
                if name in ("k", "q"):
                    j = rest[0] + (KT if name == "q" else 0)
                    if not (isinstance(u, int) and u == 0):
                        act.wait_ge(lo_done, 6 * u)
                    act.copy(raw[:, j], bank[:].rearrange("p (h d) -> p h d", h=HU)).then_inc(taken, 1)
                    act.wait_ge(taken, use[1] + 1)
                    if not (isinstance(u, int) and u == 0 and j < 2):
                        act.wait_ge(summed_sq, 6 * u + j - 1)
                    act.activation(squares[j % 2][:], raw[:, j], ACT.Square).then_inc(squared, 1)
                elif name == "v":
                    act.copy(v_ones[par][:, rest[0], :, 0:D1], bank[:].rearrange("p (h d) -> p h d", h=HU)).then_inc(taken, 1)
                elif name in ("tk", "tq"):
                    stack = k_stack[par] if name == "tk" else q_stack[par]
                    act.copy(stack[:, :, P * rest[0]:P * rest[0] + P],
                             bank[:].bitcast(F16).rearrange("p (h t) -> p h t", h=HU)).then_inc(taken, 1)

            def place_max(use, par, p):
                bank, taken = filled(use)
                act.copy(q_high[par][MROW1:MROW1 + 1, 2 * p:2 * p + 2, :],
                         bank[MROW1:MROW1 + 1, :].rearrange("o (h t) -> o h t", h=2)).then_inc(taken, 1)

            for n, (e, use) in enumerate(number(START, 0, (0, 0))[0]):
                if e[0] == "m":
                    act.wait_ge(cleared, 7)
                    place_max(use, 0, 0)
                elif e[0] in MISC:
                    shared(e, use, 0, int(n > START.index(("m",))))

            def take_mix(q, buf, g, i):
                act.wait_ge(weighed, g + 1)
                if i == 0 and not (isinstance(q, int) and q < 2):
                    act.wait_ge(att_done, q - 1)
                at = slice(D1 * i, D1 * i + D1)
                act.copy(summed[buf][at, :], mix[D1:P, 0:S])
                act.copy(mixed[buf][at, :], mix[0:D1, 0:S]).then_inc(mix_taken, 1)

            def batch(bt):
                b = bt.b
                for s, events, _, _ in bt.steps():
                    hf, p = s // PU, s % PU
                    q = 2 * PU * b + s
                    for event, use in events:
                        name, *rest = event
                        if name == "m":
                            place_max(use, hf if p < PU - 1 else 1 - hf, (p + 1) % PU)
                        elif name == "o":
                            pass
                        elif name == "k":
                            shared(event, use, hf, UB * b + hf + 2)
                        elif name in MISC:
                            shared(event, use, 1 - hf, UB * b + hf + 1)
                        elif name == "s":
                            i, half = rest
                            act.wait_ge(scored, 4 * q + 2 * i + half + 1)
                            if half == 0 and not (bt.first and s == 0):
                                act.wait_ge(weighed, 2 * q + i - 1)
                            act.activation(probs[i][:, 2 * half:2 * half + 2, :], scores[(2 * i + half) % 3][:], ACT.Exp).then_inc(exp_done, 1)
                        elif name == "w" and rest[1] == KT - 1:
                            before = rest[0] < 0
                            if not (before and bt.first and s == 0):
                                take_mix(q - before, (s - before) % 2, 2 * q + rest[0], rest[0] % 2)

            flow(act, batch)
            take_mix(2 * PU * B - 1, 1, H1 * B - 1, 1)

        @block.vector
        def _(dve):
            for par in range(2):
                dve.memset(v_ones[par][:, :, :, D1:P], 1.0).then_inc(cleared, 1)
            dve.wait_ge(cleared, 7)
            chain = Chain(dve, inv_steps)

            def sum_squares(u, j):
                dve.wait_ge(squared, 6 * u + j + 1)
                if j == 0 and not (isinstance(u, int) and u == 0):
                    dve.wait_ge(inv_done, u)
                dve.tensor_reduce(sum_sq[:, HU * j:HU * j + HU], squares[j % 2][:], AX.X, ALU.add).then_inc(summed_sq, 1)

            def invert(u):
                dve.wait_ge(summed_sq, 6 * (u + 1))
                if not (isinstance(u, int) and u == 0):
                    dve.wait_ge(normed, 6 * u)
                chain.start(u * (3 * NEWTON + 2))
                chain.then(dve.tensor_scalar(mean_sq[:], sum_sq[:], 1.0 / D1, 1e-16, ALU.mult, ALU.max))
                chain.then(dve.tensor_scalar(halved[:], mean_sq[:].bitcast(I32), 1, None, ALU.logical_shift_right))
                chain.then(dve.tensor_scalar(inv[:].bitcast(I32), halved[:], -1.0, RSQRT_BITS, ALU.mult, ALU.add))
                for i in range(NEWTON):
                    chain.then(dve.tensor_tensor(newton[:], inv[:], inv[:], ALU.mult))
                    chain.then(dve.scalar_tensor_tensor(out=newton[:], in0=newton[:], scalar=-0.5, in1=mean_sq[:], op0=ALU.mult, op1=ALU.mult))
                    step = dve.scalar_tensor_tensor(out=inv[:], in0=newton[:], scalar=1.5, in1=inv[:], op0=ALU.add, op1=ALU.mult)
                    if i < NEWTON - 1:
                        chain.then(step)
                step.then_inc(inv_done, 1)

            def high(u, j):
                dve.wait_ge(normed, 6 * u + j + 1)
                at = slice(0, D1) if j < KT else slice(D1, P)
                if j >= KT:
                    dve.tensor_tensor(raw[:, j], raw[:, j], bc(keep["qk_gain"][:], (P, HU, D1), 1), ALU.mult).then_inc(gained, 1)
                    dve.wait_ge(gained, QT * u + j - KT + 1)
                dve.tensor_copy(natural[:, j, :, at], raw[:, j]).then_inc(hi_done, 1)

            def maximum(q, i, qt):
                dve.wait_ge(rows_ready, 4 * q + 2 * i + qt + 1)
                if i == 0 and qt == 0 and not (isinstance(q, int) and q == 0):
                    dve.wait_ge(neg_done, q)
                dve.tensor_reduce(row_max[:, i, qt:qt + 1], row_scores[qt][:], AX.X, ALU.max).then_inc(max_done, 1)

            def negate(q, use_before):
                dve.wait_ge(max_done, 4 * (q + 1))
                if use_before is not None:
                    dve.wait_ge(misc_ready[use_before[0]], use_before[1] + 1)
                dve.tensor_scalar(neg_max[:, :, MROW1], row_max[:].rearrange("p i t -> p (i t)"), -1.0, None, ALU.mult).then_inc(neg_done, 1)

            def copy_high(par, event, use):
                dve.wait_ge(misc_taken[use[0]], use[1] + 1)
                name, t = event
                cols = slice(P * t, P * t + P)
                if name == "tk":
                    ins = dve.tensor_copy(k_high[par][0:D1, :, cols], k_stack[par][0:D1, :, cols])
                else:
                    ins = dve.tensor_copy(q_high[par][0:D1, :, cols], q_stack[par][D1:P, :, cols])
                ins.then_inc(high_done, 1)

            for n, (e, use) in enumerate(number(START, 0, (0, 0))[0]):
                if e[0] in ("tk", "tq"):
                    copy_high(0, e, use)
                if e[0] in ("k", "q"):
                    sum_squares(int(n > START.index(("m",))), e[1] + (KT if e[0] == "q" else 0))
                elif e[0] == "root":
                    invert(0)
                elif e[0] == "split":
                    high(0, e[1])
                elif e[0] == "r":
                    maximum(0, *e[1:])
                elif e[0] == "neg":
                    negate(0, None)

            def scale(q, pair):
                buf = pair % 2
                dve.wait_ge(mix_taken, 2 * (q + 1))
                if not (isinstance(q, int) and q == 0):
                    dve.wait_ge(att_done, q)
                dve.reciprocal(inverse[:], summed[buf][:]).then_inc(inverted, 1)
                dve.wait_ge(inverted, q + 1)
                dve.tensor_tensor(attended[:, pair, :], mixed[buf][:], inverse[:], ALU.mult).then_inc(att_done, 1)

            def add(b, use):
                bank, n = use
                dve.wait_ge(misc_ready[bank], n + 1)
                rows = xr[:, ds(QT * (b - 1), QT), :]
                dve.tensor_tensor(rows, misc[bank][:, 0:S].rearrange("p (t d) -> p t d", t=QT), rows, ALU.add).then_inc(misc_taken[bank], 1)

            def batch(bt):
                b = bt.b
                for s, events, start, maxima in bt.steps():
                    hf, p = s // PU, s % PU
                    q = 2 * PU * b + s
                    u = UB * b + hf + 1
                    names = [e for e, _ in events]
                    due = {("w", -1, KT - 1), ("neg",), ("o",)} & set(names)
                    turned = []
                    for event, use in events:
                        name, *rest = event
                        if name in ("tk", "tq"):
                            for old in turned:
                                copy_high(1 - hf, *old)
                            turned = [(event, use)]
                        elif name == "o":
                            add(b, use)
                        elif name in ("k", "q"):
                            sum_squares(u + (name == "k"), rest[0] + (KT if name == "q" else 0))
                        elif name == "root":
                            invert(u)
                        elif name == "split":
                            if rest[0] == 0:
                                for bank in range(2):
                                    dve.wait_ge(misc_taken[bank], start[bank])
                            high(u, rest[0])
                        elif name == "r":
                            maximum(q + 1, *rest)
                        elif name == "neg":
                            negate(q + 1, maxima)
                        if event in due:
                            due.discard(event)
                            if not due and not (bt.first and s == 0):
                                scale(q - 1, (s - 1) % (2 * PU))
                    for old in turned:
                        copy_high(1 - hf, *old)

            flow(dve, batch)
            scale(2 * PU * B - 1, H1 // 2 - 1)
            add(B, FINAL_USE)


def final_use():
    batch = Batch(B - 1, last=True)
    list(batch.steps())
    return batch.end


FINAL_USE = final_use()


E1 = 8
F1 = 512
FB = F1 // P
CAP = -(-T * 5 // (4 * E1))
SLOTS = (E1 - 1) * CAP
ST = -(-SLOTS // P)
OUTSIDE = 65536.0
RC = 512
CARRY = 2 * D + 1
PLACED_AT = [(0, 12), (12, 16)]


def experts_layer1(nc, io, keep, out):
    with ExitStack() as ctx:
        def sb(name, shape, dt):
            return ctx.enter_context(nc.sbuf_tensor("f_" + name, shape, dt))

        def psum(name, shape, dt=F32):
            return ctx.enter_context(nc.psum_tensor("f_" + name, shape, dt))

        def sem(name):
            return ctx.enter_context(nc.semaphore("f_" + name))

        xr, ident32, ident_b = keep["xr"], keep["ident32"], keep["ident_b"]
        w1, w2, b1, b2 = keep["w1"], keep["w2"], keep["b1"], keep["b2"]
        w1_hi, w1_lo = sb("w1_hi", [P, E1, F1], F16), sb("w1_lo", [P, E1, F1], F16)
        carried = sb("carried", [P, NT, CARRY], F32)
        nrm = carried[:, :, 0:D]
        ids = sb("ids", [P, NT], F32)
        squares = sb("squares", [P, NT, D], F32)
        small = sb("small", [P, 4 * NT], F32)
        x_hi, x_lo = sb("x_hi", [P, ST * P], F16), sb("x_lo", [P, ST * P], F16)
        router = sb("router", [P, E1], F32)
        router_hi, router_lo = sb("router_hi", [P, E1], F16), sb("router_lo", [P, E1], F16)
        counting = sb("counting", [P, E0], F32)
        below = sb("below", [P, P], F32)
        logits = sb("logits", [P, NT, E1], F32)
        top = sb("top", [P, NT, 8], F32)
        top_at = sb("top_at", [P, NT, 8], U32)
        expert = sb("expert", [P, NT], F32)
        line = [sb(f"line{i}", [P, NT], F32) for i in range(6)]
        onehot = sb("onehot", [P, NT, E1], F32)
        key = sb("key", [P, NT, E1], F32)
        parts = sb("parts", [P, NT, 2, 32], BF16)
        keys_t = sb("keys_t", [P, T], BF16)
        onehot_t = sb("onehot_t", [P, T], BF16)
        compared = sb("compared", [P, 2, RC], BF16)
        tied = sb("tied", [P, P], BF16)
        counts = sb("counts", [P, NT, 8], F32)
        place = sb("place", [P, NT], U32)
        hidden = [sb(f"hidden{i}", [P, FB, 512], F32) for i in range(2)]
        placed = sb("placed", [P, ST, D], F32)
        y_rows = [sb(f"y_rows{i}", [P, 3, D], F32) for i in range(2)]
        slots = sb("slots", [P, E1 - 1, 3, D + 1], F32)
        back_to = sb("back_to", [P, E1 - 1, 3], U32)
        y0 = squares

        hid = [psum(f"hid{i}", [P, 512]) for i in range(FB)]
        yb = [psum(f"yb{i}", [P, 512]) for i in range(2)]
        rk = [psum(f"rk{i}", [P, RC]) for i in range(2)]

        small_in, empty_out = sem("small_in"), sem("empty_out")
        centred, squared, var_done, root_done = keep["norm_sems"]
        steps, norm_done, turned, hi_done, lo_done, w_hi_done, w_lo_done = (sem(n) for n in (
            "steps", "norm_done", "turned", "hi_done", "lo_done", "w_hi_done", "w_lo_done"))
        router_split, logits_ready, shifted, powers = (sem(n) for n in ("router_split", "logits_ready", "shifted", "powers"))
        parts_done, parts_turned, parts_taken, cleared = (sem(n) for n in ("parts_done", "parts_turned", "parts_taken", "cleared"))
        rank_ready, rank_taken, place_done, scattered, placed_in = (sem(n) for n in (
            "rank_ready", "rank_taken", "place_done", "scattered", "placed_in"))
        hid_ready, hid_taken, y_ready, y_taken, result, stored, slots_in, carried_done, back_done = (sem(n) for n in (
            "hid_ready", "hid_taken", "y_ready", "y_taken", "result", "stored", "slots_in", "carried_done", "back_done"))
        y_out = [sem(f"y_out{i}") for i in range(2)]

        NCHUNK = T // 512
        pieces = []
        for c in range(NCHUNK):
            pieces += [("h", c, fb) for fb in range(FB)]
            if c:
                pieces += [("y", c - 1, i) for i in range(4)]
        pieces += [("y", NCHUNK - 1, i) for i in range(4)]
        compares = [(t, c) for t in range(NT) for c in range(T // RC)]
        tiles = [(0, P), (P, P), (2 * P, CAP - 2 * P)]

        block = ctx.enter_context(nc.Block())

        @block.sync
        def _(sp):
            sp.dma_start(router[:], io["router"]).then_inc(small_in, 16)
            sp.dma_start(counting[:], io["counting"].partition_broadcast(P)).then_inc(small_in, 16)
            sp.dma_start(below[:], io["below"]).then_inc(small_in, 16)
            sp.dma_start(ids[:], io["ids"]).then_inc(small_in, 16)
            sp.dma_start(io["placed"], io["no_rows"]).then_inc(empty_out, 16)
            sp.wait_ge(scattered, 16 * NT)
            sp.dma_start(placed[:], io["placed"].rearrange("(t p) d -> p t d", p=P)[:, :, 0:D]).then_inc(placed_in, 16)
            by_expert = io["placed"][0:SLOTS].rearrange("(e c) d -> c e d", c=CAP)
            for i, (at, n) in enumerate(tiles):
                sp.dma_start(slots[0:n, :, i, :], by_expert[at:at + n, :, D:CARRY]).then_inc(slots_in, 16)
            sp.wait_ge(result, 1)
            sp.dma_start(out.rearrange("(t p) d -> p t d", p=P), xr[:]).then_inc(stored, 16)
            sp.wait_ge(stored, 16)

        @block.gpsimd
        def _(pool):
            pool.wait_ge(w_hi_done, 1)
            nc.gpsimd.tensor_tensor(w1_lo[:, 0], w1[:, 0], w1_hi[:, 0], ALU.subtract).then_inc(w_lo_done, 1)
            pool.wait_ge(w_hi_done, 2)
            nc.gpsimd.tensor_tensor(w1_lo[:, 1:E1], w1[:, 1:E1], w1_hi[:, 1:E1], ALU.subtract).then_inc(w_lo_done, 1)
            pool.wait_ge(empty_out, 16)
            pool.wait_ge(carried_done, 2)
            pool.wait_ge(norm_done, 1)
            for g, (first, end) in enumerate(PLACED_AT):
                pool.wait_ge(place_done, g + 1)
                for t in range(first, end):
                    nc.gpsimd.indirect_dma_start(
                        out=io["placed"], out_offset=bass.IndirectOffsetOnAxis(ap=place[:, t:t + 1], axis=0),
                        in_=carried[:, t, :], in_offset=None, bounds_check=SLOTS - 1, oob_is_err=False).then_inc(scattered, 16)
            pool.wait_ge(back_done, 2)
            pool.wait_ge(stored, 16)
            for e in range(1, E1):
                pool.wait_ge(y_taken, NCHUNK + e)
                for i, (_, n) in enumerate(tiles):
                    nc.gpsimd.indirect_dma_start(
                        out=out, out_offset=bass.IndirectOffsetOnAxis(ap=back_to[0:n, e - 1, i:i + 1], axis=0),
                        in_=y_rows[(e - 1) % 2][0:n, i, :], in_offset=None, bounds_check=T - 1, oob_is_err=False).then_inc(y_out[(e - 1) % 2], 16)
            pool.wait_ge(y_out[0], 16 * len(tiles) * (E1 // 2))
            pool.wait_ge(y_out[1], 16 * len(tiles) * (E1 // 2 - 1))

        @block.tensor
        def _(pe):
            def three(o, a_hi, a_lo, b_hi, b_lo):
                pe.matmul(o, a_hi, b_hi, start=True, stop=False)
                pe.matmul(o, a_lo, b_hi, start=False, stop=False)
                return pe.matmul(o, a_hi, b_lo, start=False, stop=True)

            pe.wait_ge(norm_done, 1)
            for g in range(4):
                for i in range(4):
                    mm = pe.transpose(hid[g][:, P * i:P * i + P], carried[:, 4 * g + i, 0:D], ident32[:])
                mm.then_inc(turned, 1)
            pe.wait_ge(router_split, 2)
            pe.wait_ge(lo_done, 4)
            for t in range(NT):
                cols = slice(P * t, P * t + P)
                mm = three(rk[0][:, E1 * t:E1 * t + E1], x_hi[:, cols], x_lo[:, cols], router_hi[:], router_lo[:])
            mm.then_inc(logits_ready, 1)

            def run(piece):
                kind, c, i = piece
                n = FB * c
                if kind == "h":
                    if n + i >= FB:
                        pe.wait_ge(hid_taken, n + i - FB + 1)
                    cols = slice(512 * c, 512 * c + 512)
                    w = slice(P * i, P * i + P)
                    three(hid[i][:], w1_hi[:, 0, w], w1_lo[:, 0, w], x_hi[:, cols], x_lo[:, cols]).then_inc(hid_ready, 1)
                else:
                    pe.wait_ge(hid_taken, n + FB)
                    if i == 0 and c >= 2:
                        pe.wait_ge(y_taken, c - 1)
                    for fb in range(FB):
                        mm = pe.matmul(yb[c % 2][:, P * i:P * i + P], hidden[c % 2][:, fb, P * i:P * i + P], w2[:, 0, fb, :],
                                       start=(fb == 0), stop=(fb == FB - 1))
                    if i == 3:
                        mm.then_inc(y_ready, 1)

            pe.wait_ge(w_lo_done, 1)
            pe.wait_ge(keep["w2_in"], 16)
            for piece in pieces[:FB]:
                run(piece)
            pe.wait_ge(parts_done, 1)
            for half in range(2):
                for g in range(2):
                    bank = rk[g][:].bitcast(BF16)
                    if half:
                        pe.wait_ge(parts_taken, g + 1)
                    for i in range(8):
                        mm = pe.transpose(bank[0:32, P * i:P * i + P], parts[:, 8 * g + i, half, :], ident_b[:])
                    mm.then_inc(parts_turned, 1)
            pe.wait_ge(parts_taken, 4)
            pe.wait_ge(cleared, 1)
            left = pieces[FB:]
            for n, (t, c) in enumerate(compares):
                if n >= 2:
                    pe.wait_ge(rank_taken, n - 1)
                pe.matmul(rk[n % 2][:], onehot_t[:, P * t:P * t + P], keys_t[:, RC * c:RC * c + RC], start=True, stop=True).then_inc(rank_ready, 1)
                if n % 2 and left:
                    run(left.pop(0))
            while left:
                run(left.pop(0))
            pe.wait_ge(placed_in, 16)
            for g in range(-(-ST // 4)):
                if g == 0:
                    pe.wait_ge(hid_taken, FB * NCHUNK)
                if g == 4:
                    pe.wait_ge(hi_done, 5)
                    pe.wait_ge(lo_done, 5)
                for i in range(min(4, ST - 4 * g)):
                    mm = pe.transpose(hid[g % 4][:, P * i:P * i + P], placed[:, 4 * g + i, :], ident32[:])
                mm.then_inc(turned, 1)
            pe.wait_ge(hi_done, 4 + -(-ST // 4))
            pe.wait_ge(lo_done, 4 + -(-ST // 4))
            pe.wait_ge(w_lo_done, 2)

            def hiddens(e):
                for fb in range(FB):
                    pe.wait_ge(hid_taken, FB * (NCHUNK + e - 1) + fb - FB + 1)
                    cols = ds((e - 1) * CAP, CAP)
                    w = slice(P * fb, P * fb + P)
                    at = ds(e, 1)
                    three(hid[fb][:, 0:CAP], w1_hi[:, at, w].rearrange("p e f -> p (e f)"), w1_lo[:, at, w].rearrange("p e f -> p (e f)"),
                          x_hi[:, cols], x_lo[:, cols]).then_inc(hid_ready, 1)

            def answers(e, buf):
                pe.wait_ge(hid_taken, FB * (NCHUNK + e))
                pe.wait_ge(y_taken, NCHUNK + e - 2)
                for i, (at, n) in enumerate(tiles):
                    for fb in range(FB):
                        mm = pe.matmul(yb[buf][0:n, P * i:P * i + P], hidden[buf][:, fb, at:at + n],
                                       w2[:, ds(e, 1), fb, :].rearrange("p e d -> p (e d)"),
                                       start=(fb == 0), stop=(fb == FB - 1))
                mm.then_inc(y_ready, 1)

            hiddens(1)
            with pe.Fori(0, (E1 - 1) // 2) as j:
                hiddens(2 * j + 2)
                answers(2 * j + 1, 0)
                hiddens(2 * j + 3)
                answers(2 * j + 2, 1)
            answers(E1 - 1, 0)

        @block.scalar
        def _(act):
            act.wait_ge(keep["w1_in"], 16)
            act.copy(w1_hi[:, 0], w1[:, 0]).then_inc(w_hi_done, 1)
            layer_norm_all_act(act, centred, squared, var_done, root_done, nrm, squares, small, 6)
            act.wait_ge(small_in, 64)
            act.copy(carried[:, :, D:2 * D], xr[:]).then_inc(carried_done, 1)
            act.copy(carried[:, :, 2 * D], ids[:]).then_inc(carried_done, 1)
            act.copy(w1_hi[:, 1:E1], w1[:, 1:E1]).then_inc(w_hi_done, 1)
            for g in range(4):
                act.wait_ge(turned, g + 1)
                act.copy(x_hi[:, 512 * g:512 * g + 512], hid[g][:]).then_inc(hi_done, 1)

            def relu(e, n, fb, buf, width):
                act.wait_ge(hid_ready, n + 1)
                act.activation(hidden[buf][:, fb, 0:width], hid[fb][:, 0:width], ACT.Relu,
                               bias=b1[:, ds(e * FB + fb, 1)]).then_inc(hid_taken, 1)

            act.wait_ge(keep["b1_in"], 16)
            relus = [p for p in pieces if p[0] == "h"]
            for n, (_, c, fb) in enumerate(relus):
                if n == FB:
                    act.wait_ge(shifted, 1)
                    act.activation(logits[:], logits[:], ACT.Exp).then_inc(powers, 1)
                if c >= 2:
                    act.wait_ge(y_ready, c - 1)
                relu(0, n, fb, c % 2, 512)
            for g in range(-(-ST // 4)):
                n = min(4, ST - 4 * g) * P
                act.wait_ge(turned, 5 + g)
                if g == 0:
                    act.wait_ge(hid_ready, FB * NCHUNK)
                act.copy(x_hi[:, 512 * g:512 * g + n], hid[g % 4][:, 0:n]).then_inc(hi_done, 1)

            def relus_of(e, buf):
                act.wait_ge(y_ready, NCHUNK + e - 2)
                for fb in range(FB):
                    relu(e, FB * (NCHUNK + e - 1) + fb, fb, buf, CAP)

            with act.Fori(0, (E1 - 1) // 2) as j:
                relus_of(2 * j + 1, 0)
                relus_of(2 * j + 2, 1)
            relus_of(E1 - 1, 0)

        @block.vector
        def _(dve):
            chain = Chain(dve, steps)
            inv = layer_norm_all(dve, chain, centred, squared, var_done, root_done, xr, nrm, squares, small, 6)
            dve.tensor_tensor(nrm[:], nrm[:], bc(inv, (P, NT, D), 2), ALU.mult).then_inc(norm_done, 1)
            dve.wait_ge(small_in, 64)
            dve.tensor_copy(router_hi[:], router[:]).then_inc(router_split, 1)
            dve.wait_ge(router_split, 1)
            dve.tensor_tensor(router_lo[:], router[:], router_hi[:], ALU.subtract).then_inc(router_split, 1)
            chain.then(dve.memset(keys_t[:].bitcast(F32), 0.0))
            chain.then(dve.memset(onehot_t[:].bitcast(F32), 0.0))
            chain.then(dve.memset(counts[:], 0.0))
            dve.memset(parts[:], 0.0).then_inc(cleared, 1)
            for g in range(4):
                cols = slice(512 * g, 512 * g + 512)
                dve.wait_ge(hi_done, g + 1)
                dve.tensor_tensor(x_lo[:, cols], hid[g][:], x_hi[:, cols], ALU.subtract).then_inc(lo_done, 1)
            total, prob, rank, kept, named, away = (x[:] for x in line)
            dve.wait_ge(logits_ready, 1)
            chain.then(dve.tensor_reduce(total, rk[0][:, 0:NT * E1].rearrange("p (t e) -> p t e", e=E1), AX.X, ALU.max))
            dve.tensor_tensor(logits[:], rk[0][:, 0:NT * E1].rearrange("p (t e) -> p t e", e=E1),
                              bc(total, (P, NT, E1), 2), ALU.subtract).then_inc(shifted, 1)
            dve.wait_ge(powers, 1)
            chain.then(dve.tensor_reduce(prob, logits[:], AX.X, ALU.add))
            chain.then(dve.reciprocal(prob, prob))
            for t in range(NT):
                ins = dve.max(top[:, t, :], logits[:, t, :])
            chain.then(ins)
            for t in range(NT):
                ins = dve.max_index(top_at[:, t, :], top[:, t, :], logits[:, t, :])
            chain.then(ins)
            chain.then(dve.tensor_copy(expert[:], top_at[:, :, 0]))
            chain.then(dve.tensor_tensor(onehot[:], bc(counting[:, 0:E1], (P, NT, E1), 1), bc(expert[:], (P, NT, E1), 2), ALU.is_equal))
            chain.then(dve.tensor_tensor(key[:], onehot[:], bc(prob, (P, NT, E1), 2), ALU.mult))
            dve.wait_ge(cleared, 1)
            for i in range(3):
                chain.then(dve.tensor_copy(parts[:, :, 0, E1 * i:E1 * i + E1], onehot[:]))
                step = dve.tensor_copy(parts[:, :, 1, E1 * i:E1 * i + E1], key[:])
                if i == 2:
                    step.then_inc(parts_done, 1)
                else:
                    chain.then(step)
                if i < 2:
                    chain.then(dve.tensor_tensor(key[:], key[:], parts[:, :, 1, E1 * i:E1 * i + E1], ALU.subtract))
            for half in range(2):
                dest = (onehot_t, keys_t)[half]
                for g in range(2):
                    dve.wait_ge(parts_turned, 2 * half + g + 1)
                    dve.tensor_copy(dest[0:32, 8 * P * g:8 * P * g + 8 * P], rk[g][:].bitcast(BF16)[0:32, :]).then_inc(parts_taken, 1)
            def rows_of_0(c):
                dve.wait_ge(y_ready, c + 1)
                dve.tensor_tensor(y0[:, 4 * c:4 * c + 4, :], yb[c % 2][:].rearrange("p (t d) -> p t d", t=4),
                                  bc(b2[:, 0, :], (P, 4, D), 1), ALU.add).then_inc(y_taken, 1)

            def places(first, end):
                at = slice(first, end)
                dve.wait_ge(rank_taken, T // RC * end)
                chain.then(dve.tensor_reduce(rank[:, at], counts[:, at], AX.X, ALU.add))
                chain.then(dve.tensor_tensor(rank[:, at], rank[:, at], away[:, at], ALU.add))
                chain.then(dve.tensor_scalar(kept[:, at], rank[:, at], float(CAP), None, ALU.is_lt))
                chain.then(dve.tensor_scalar(named[:, at], expert[:, at], 0.0, None, ALU.is_gt))
                chain.then(dve.tensor_tensor(kept[:, at], kept[:, at], named[:, at], ALU.mult))
                chain.then(dve.tensor_scalar(named[:, at], expert[:, at], float(CAP), float(OUTSIDE - CAP), ALU.mult, ALU.add))
                chain.then(dve.tensor_tensor(named[:, at], named[:, at], rank[:, at], ALU.add))
                chain.then(dve.tensor_scalar(away[:, at], kept[:, at], -OUTSIDE, None, ALU.mult))
                chain.then(dve.tensor_tensor(named[:, at], named[:, at], away[:, at], ALU.add))
                dve.tensor_copy(place[:, at], named[:, at]).then_inc(place_done, 1)

            dve.wait_ge(keep["b2_in"], 16)
            for n, (t, c) in enumerate(compares):
                dve.wait_ge(rank_ready, n + 1)
                bank = rk[n % 2]
                own = P * t - RC * c
                cut = min(max(own, 0), RC)
                mine = prob[:, t:t + 1]
                ops = []
                if cut > 0:
                    ops.append((slice(0, cut), ALU.is_ge, c))
                if cut < RC:
                    ops.append((slice(cut, RC), ALU.is_gt, 4 + c))
                if n >= 2:
                    dve.wait_ge(rank_taken, n - 1)
                for cells, op, at in ops:
                    ins = dve.tensor_scalar(compared[:, n % 2, cells], bank[:, cells], mine, None, op, ALU.add, accum_out=counts[:, t, at:at + 1])
                if 0 <= own < RC:
                    ins = dve.scalar_tensor_tensor(out=tied[:], in0=bank[:, own:own + P], scalar=mine, in1=below[:],
                                                   op0=ALU.is_equal, op1=ALU.mult, accum_out=line[5][:, t:t + 1])
                ins.then_inc(rank_taken, 1)
                if n in (18, 34, 50):
                    rows_of_0((n - 18) // 16)
                if c == T // RC - 1 and t + 1 in (end for _, end in PLACED_AT):
                    places(*next(p for p in PLACED_AT if p[1] == t + 1))
            rows_of_0(NCHUNK - 1)
            dve.wait_ge(y_taken, NCHUNK)
            dve.wait_ge(carried_done, 1)
            dve.tensor_tensor(xr[:], xr[:], y0[:], ALU.add).then_inc(result, 1)
            for g in range(-(-ST // 4)):
                n = min(4, ST - 4 * g) * P
                dve.wait_ge(hi_done, 5 + g)
                dve.tensor_tensor(x_lo[:, 512 * g:512 * g + n], hid[g % 4][:, 0:n], x_hi[:, 512 * g:512 * g + n], ALU.subtract).then_inc(lo_done, 1)

            def rows_of(e, buf, uses=None):
                dve.wait_ge(y_ready, NCHUNK + e)
                if uses is not None:
                    dve.wait_ge(y_out[buf], 16 * len(tiles) * uses)
                at = ds(e - 1, 1)
                dve.tensor_tensor(y_rows[buf][:, 0:2, :], yb[buf][:, 0:2 * P].rearrange("p (t d) -> p t d", t=2),
                                  slots[:, at, 0:2, 0:D].rearrange("p e t d -> p (e t) d"), ALU.add)
                n = tiles[2][1]
                dve.tensor_tensor(y_rows[buf][0:n, 2, :], yb[buf][0:n, 2 * P:3 * P],
                                  slots[0:n, at, 2, 0:D].rearrange("p e d -> p (e d)"), ALU.add).then_inc(y_taken, 1)

            dve.wait_ge(slots_in, 16 * len(tiles))
            last = tiles[2][1]
            dve.tensor_copy(back_to[:, :, 0:2], slots[:, :, 0:2, D]).then_inc(back_done, 1)
            dve.tensor_copy(back_to[0:last, :, 2], slots[0:last, :, 2, D]).then_inc(back_done, 1)
            for i, (_, n) in enumerate(tiles):
                chain.then(dve.tensor_tensor(slots[0:n, :, i, 0:D], slots[0:n, :, i, 0:D], b2[0:n, 1:E1, :], ALU.add))
            rows_of(1, 0)
            rows_of(2, 1)
            with dve.Fori(1, (E1 - 1) // 2) as j:
                rows_of(2 * j + 1, 0, j)
                rows_of(2 * j + 2, 1, j)
            rows_of(E1 - 1, 0, (E1 - 1) // 2)


def build(nc, io, out):
    with ExitStack() as ctx:
        def sb(name, shape, dt):
            return ctx.enter_context(nc.sbuf_tensor(name, shape, dt))

        keep = {
            "xr": sb("xr", [P, NT, D], F32),
            "nrm": sb("nrm", [P, NT, D], F32),
            "ident32": sb("ident32", [P, P], F32),
            "ident16": sb("ident16", [P, P], F16),
            "ident_b": sb("ident_b", [P, P], BF16),
            "nothing": sb("nothing", [P, 8], F32),
            "wo0": sb("wo0", [P, D], F32),
            "norm_sems": [ctx.enter_context(nc.semaphore(n)) for n in ("centred", "squared", "var", "root")],
            "wo0_in": ctx.enter_context(nc.semaphore("wo0_in")),
        }
        io["parts"] = nc.dram_tensor("parts_scratch", (4, P, T), F16, kind="Internal").ap()
        with ExitStack() as layer0:
            for name in ("q_stack", "k_stack"):
                keep[name] = [layer0.enter_context(nc.sbuf_tensor(f"{name}{i}", [P, H0, S], F16)) for i in range(RING)]
            keep["loaded"] = [ctx.enter_context(nc.semaphore(f"loaded{i}")) for i in range(RING)]
            keep["bias_q"] = layer0.enter_context(nc.sbuf_tensor("bias_q", [P, NT, S], F16))
            keep["bias_k"] = layer0.enter_context(nc.sbuf_tensor("bias_k", [P, NT, S], F16))
            keep["v_all"] = layer0.enter_context(nc.sbuf_tensor("v_all", [P, NT, D], F32))
            project_layer0(nc, io, keep)
            attend_layer0(nc, io, keep)
        experts_layer0(nc, io, keep)
        io["mask_bias"] = nc.dram_tensor("mask_scratch", (B, S), F16, kind="Internal").ap()
        with ExitStack() as layer1:
            def sb1(name, shape, dt):
                return layer1.enter_context(nc.sbuf_tensor(name, shape, dt))

            for name in ("ctx_hi", "ctx_lo", "lat_hi", "lat_lo"):
                keep[name] = sb1(name, [P, T], F16)
            for name in ("wq_hi", "wq_lo"):
                keep[name] = sb1(name, [P, H1 * D1], F16)
            for name in ("wkv_hi", "wkv_lo"):
                keep[name] = sb1(name, [P, 2 * H1 * D1], F16)
            keep["wout"] = sb1("wout", [P, H1 // 2, D], F32)
            keep["qk_gain"] = sb1("qk_gain", [P, D1], F32)
            keep["wout_in"] = layer1.enter_context(nc.semaphore("wout_in"))
            prepare_layer1(nc, io, keep)
            attend_layer1(nc, io, keep)
        io["placed"] = nc.dram_tensor("placed_scratch", (ST * P, CARRY), F32, kind="Internal").ap()
        keep["w1"] = sb("w1", [P, E1, F1], F32)
        keep["w2"] = sb("w2", [P, E1, FB, D], F32)
        keep["b1"] = sb("b1", [P, E1 * FB], F32)
        keep["b2"] = sb("b2", [P, E1, D], F32)
        for name in ("w1_in", "w2_in", "b1_in", "b2_in"):
            keep[name] = ctx.enter_context(nc.semaphore(name))
        with nc.Block() as block:
            @block.sync
            def _(sp):
                sp.dma_start(keep["w1"][:], io["w1"]).then_inc(keep["w1_in"], 16)
                sp.dma_start(keep["b1"][:], io["b1"]).then_inc(keep["b1_in"], 16)
                sp.dma_start(keep["w2"][:], io["w2"]).then_inc(keep["w2_in"], 16)
                sp.dma_start(keep["b2"][:], io["b2"].partition_broadcast(P)).then_inc(keep["b2_in"], 16)
        experts_layer1(nc, io, keep, out)


def layout(inputs):
    a = {k: np.asarray(v) for k, v in inputs.items()}
    mask = a["mask_BxSxS2_ik1"]

    def rows(x):
        return x.reshape(NT, P, D).transpose(1, 0, 2)

    gate_up = a["L0_ffn_experts_gate_up"].reshape(PAIRS, 2, 2, I0, D)
    w0 = np.concatenate([
        np.stack([a["L0_ffn_shared_gate_w"].T, a["L0_ffn_shared_up_w"].T, a["L0_ffn_shared_down_w"].T], 1)[None],
        np.stack([gate_up[:, :, 0].reshape(PAIRS, P, D).transpose(0, 2, 1),
                  gate_up[:, :, 1].reshape(PAIRS, P, D).transpose(0, 2, 1),
                  a["L0_ffn_experts_down"].transpose(0, 2, 1).reshape(PAIRS, P, D)], 2)])
    return {
        "w1": a["L1_ffn_W1"].transpose(1, 0, 2),
        "w2": a["L1_ffn_W2"].reshape(E1, FB, P, D).transpose(2, 0, 1, 3),
        "b1": a["L1_ffn_b1"].reshape(E1, FB, P).transpose(2, 0, 1).reshape(P, E1 * FB),
        "b2": a["L1_ffn_b2"],
        "router": a["L1_ffn_router_w"].T,
        "below": np.tril(np.ones((P, P), np.float32), -1),
        "no_rows": np.concatenate([np.zeros((ST * P, 2 * D), np.float32), np.full((ST * P, 1), OUTSIDE, np.float32)], 1),
        "ids": np.arange(T, dtype=np.float32).reshape(NT, P).T,
        "ctx_rows": rows(a["ctx_1024"]),
        "norm_w": np.stack([a["L1_xattn_ln_x_g"], a["L1_xattn_ln_x_b"], a["L1_xattn_ln_l_g"], a["L1_xattn_ln_l_b"]], 1),
        "q_gain": a["L1_xattn_qn_g"], "k_gain": a["L1_xattn_kn_g"], "bout": a["L1_xattn_bout"],
        "mask8": a["mask_BxS2_bf1"].view(np.uint8),
        "wq1": a["L1_xattn_Wq"], "wkv1": a["L1_xattn_Wkv"],
        "wout": a["L1_xattn_Wout"].reshape(H1 // 2, P, D).transpose(1, 0, 2),
        "ones": np.ones((1, H0, S), np.float16),
        "w0": w0,
        "gate0": a["L0_ffn_gate_weight"].T,
        "bias0": a["L0_ffn_e_score_correction_bias"],
        "counting": np.arange(E0, dtype=np.float32),
        "spread0": np.tile(np.kron(np.eye(E0), np.ones((1, I0))), (3, 1)).astype(np.float16),
        "x_rows": rows(a["x"]),
        "ctx_t": a["ctx_1024"].reshape(T, D).T,
        "wq0": a["L0_xattn_w_q"].T, "wk0": a["L0_xattn_w_k"].T, "wv0": a["L0_xattn_w_v"].T, "wo0": a["L0_xattn_w_o"].T,
        "mask_q": mask.reshape(NT, P, S).transpose(1, 0, 2),
        "mask_k": mask.transpose(0, 2, 1).reshape(NT, P, S).transpose(1, 0, 2),
        "zeros": np.zeros((1, H0, S), np.float16),
    }


def kernel(**inputs):
    import concourse.bacc as bacc
    from concourse.bass_utils import run_bass_kernel_spmd

    nc = bacc.Bacc("TRN2", target_bir_lowering=False, num_devices=1)
    arrays = {f"in_{k}": np.ascontiguousarray(v) for k, v in layout(inputs).items()}
    io = {k[3:]: nc.dram_tensor(k, v.shape, mybir.dt.from_np(v.dtype), kind="ExternalInput").ap() for k, v in arrays.items()}
    out = nc.dram_tensor("out", (T, D), F32, kind="ExternalOutput").ap()
    build(nc, io, out)
    got = run_bass_kernel_spmd(nc, [arrays], core_ids=[0])
    return got.results[0]["out"].reshape(B, S, D)
```
